# Optimizing a Trainium2 kernel written in Bass

```python
import numpy as np
import jax
import jax.numpy as jnp

def _softmax(x, axis=-1):
    return jax.nn.softmax(x, axis=axis)

def _gelu(x):
    return jax.nn.gelu(x, approximate=True)

def _silu(x):
    return jax.nn.silu(x)

def _sigmoid(x):
    return jax.nn.sigmoid(x)

def _layernorm(x, axis=-1, eps=1e-05):
    m = jnp.mean(x, axis=axis, keepdims=True)
    v = jnp.var(x, axis=axis, keepdims=True)
    return (x - m) / jnp.sqrt(v + eps)

def _scatter_add(tgt, idx, src, axis=0):
    return tgt.at[idx].add(src)

def _segment_sum(src, seg, n):
    return jax.ops.segment_sum(src, seg, n)
kernel_name = 'mk_lm_tower_d1_tok_ids1024_r4_e8c4a8'

def setup_inputs(seed: int=0):
    np.random.seed(seed)
    _w = jnp.asarray

    def _rec_inputs():
        import jax
        import jax.numpy as jnp
        _rk = jax.random.key(seed)
        x = jax.random.randint(jax.random.fold_in(_rk, 1), (1, 2048), 0, 31995, jnp.int32)
        return x
    x = _rec_inputs()

    def _L0_tok_setup():
        import jax, jax.numpy as jnp
        import numpy as np
        NUM_EMBEDDINGS = 32000
        EMBEDDING_DIM = 256
        EPS = 1e-05
        key = jax.random.key(seed)
        k_w, k_idx = jax.random.split(key)
        weight = jax.random.normal(k_w, (NUM_EMBEDDINGS, EMBEDDING_DIM), dtype=jnp.float32)
        input = jax.random.randint(k_idx, (4, 1024), 0, NUM_EMBEDDINGS, dtype=jnp.int64)
        return {'input': input, 'weight': weight}
    _L0_tok_all = _L0_tok_setup()
    _L0_tok_in = {k: v for k, v in _L0_tok_all.items() if k in ('weight',)}
    del _L0_tok_all

    def _L0_attn_setup():
        import jax, jax.numpy as jnp
        import numpy as np
        import math
        N_HEAD = 16
        V_HEAD = 32
        NOPE = 32
        ROPE_D = 64
        KEEP = 64
        EPS = 1e-06

        def _freqs(T, dim=ROPE_D, theta=10000.0):
            f = 1.0 / theta ** (jnp.arange(0, dim, 2, dtype=jnp.float32) / dim)
            t = jnp.arange(T, dtype=jnp.float32)
            a = jnp.outer(t, f)
            return (jnp.cos(a), jnp.sin(a))

        def _rope(x, cos, sin):
            S = x.shape[-2]
            c = cos[:S][None, None]
            s = sin[:S][None, None]
            x1, x2 = jnp.split(x, 2, axis=-1)
            return jnp.concatenate([x1 * c - x2 * s, x1 * s + x2 * c], axis=-1)

        def _rms(x, g, eps=EPS):
            return x * jax.lax.rsqrt(jnp.mean(x * x, axis=-1, keepdims=True) + eps) * g

        def _attn(q, k, v, causal):
            scale = 1.0 / math.sqrt(q.shape[-1])
            s = jnp.einsum('bhqd,bhkd->bhqk', q, k) * scale
            if causal:
                Tq, Tk = (s.shape[-2], s.shape[-1])
                mask = jnp.tril(jnp.ones((Tq, Tk), dtype=bool))
                s = jnp.where(mask, s, jnp.finfo(s.dtype).min)
            return jnp.einsum('bhqk,bhkd->bhqd', jax.nn.softmax(s, axis=-1), v)

        def _forward(x, w_cq, g_qnorm, w_dq_nope, w_dq_rope, w_ckv, g_kvnorm, w_dk_nope, w_dv, w_krope, w_imp, w_selk, w_selv, w_wink, w_winv, w_gate, w_proj):
            B, T, C = x.shape
            cos, sin = _freqs(T)
            nq = _rms(x @ w_cq, g_qnorm)
            q_nope = (nq @ w_dq_nope).reshape(B, T, N_HEAD, NOPE).transpose(0, 2, 1, 3)
            q_rope = (nq @ w_dq_rope).reshape(B, T, N_HEAD, ROPE_D).transpose(0, 2, 1, 3)
            q_rope = _rope(q_rope, cos, sin)
            q = jnp.concatenate([q_nope, q_rope], axis=-1)
            gate = jax.nn.softmax((x @ w_gate).mean(axis=1), axis=-1)
            ckv = _rms(x @ w_ckv, g_kvnorm)
            k_nope = (ckv @ w_dk_nope).reshape(B, T, N_HEAD, NOPE).transpose(0, 2, 1, 3)
            v1 = (ckv @ w_dv).reshape(B, T, N_HEAD, V_HEAD).transpose(0, 2, 1, 3)
            k_rope = (x @ w_krope).reshape(B, T, 1, ROPE_D).transpose(0, 2, 1, 3) / N_HEAD
            k_rope = _rope(k_rope, cos, sin)
            k1 = jnp.concatenate([k_nope, jnp.broadcast_to(k_rope, (B, N_HEAD, T, ROPE_D))], axis=-1)
            scores = (x @ w_imp)[..., 0]
            _, idx = jax.lax.top_k(scores, KEEP)
            idx = jnp.sort(idx, axis=1)
            sel = jnp.take_along_axis(x, idx[:, :, None], axis=1)
            ks = (sel @ w_selk).reshape(B, KEEP, N_HEAD, NOPE + ROPE_D).transpose(0, 2, 1, 3)
            vs = (sel @ w_selv).reshape(B, KEEP, N_HEAD, V_HEAD).transpose(0, 2, 1, 3)
            ks = jnp.concatenate([ks[..., :NOPE], _rope(ks[..., NOPE:], cos, sin)], axis=-1)
            kw = (x @ w_wink).reshape(B, T, N_HEAD, NOPE + ROPE_D).transpose(0, 2, 1, 3)
            vw = (x @ w_winv).reshape(B, T, N_HEAD, V_HEAD).transpose(0, 2, 1, 3)
            kw = jnp.concatenate([kw[..., :NOPE], _rope(kw[..., NOPE:], cos, sin)], axis=-1)
            a1 = _attn(q, k1, v1, causal=True)
            a2 = _attn(q, ks, vs, causal=False)
            a3 = _attn(q, kw, vw, causal=True)
            g = gate[:, :, None, None, None]
            out = g[:, 0] * a1 + g[:, 1] * a2 + g[:, 2] * a3
            out = out.transpose(0, 2, 1, 3).reshape(B, T, N_HEAD * V_HEAD)
            return out @ w_proj
        key = jax.random.key(seed)
        ks = jax.random.split(key, 20)
        B, T, C = (2, 256, 256)
        q_lora, kv_lora = (96, 32)
        std = 0.02

        def w(k, shape):
            return jax.random.normal(k, shape, dtype=jnp.float32) * std
        return {'x': jax.random.normal(ks[0], (B, T, C), dtype=jnp.float32), 'w_cq': w(ks[1], (C, q_lora)), 'g_qnorm': jnp.ones((q_lora,), jnp.float32), 'w_dq_nope': w(ks[2], (q_lora, N_HEAD * NOPE)), 'w_dq_rope': w(ks[3], (q_lora, N_HEAD * ROPE_D)), 'w_ckv': w(ks[4], (C, kv_lora)), 'g_kvnorm': jnp.ones((kv_lora,), jnp.float32), 'w_dk_nope': w(ks[5], (kv_lora, N_HEAD * NOPE)), 'w_dv': w(ks[6], (kv_lora, N_HEAD * V_HEAD)), 'w_krope': w(ks[7], (C, ROPE_D)), 'w_imp': w(ks[8], (C, 1)), 'w_selk': w(ks[9], (C, N_HEAD * (NOPE + ROPE_D))), 'w_selv': w(ks[10], (C, N_HEAD * V_HEAD)), 'w_wink': w(ks[11], (C, N_HEAD * (NOPE + ROPE_D))), 'w_winv': w(ks[12], (C, N_HEAD * V_HEAD)), 'w_gate': w(ks[13], (C, 3)), 'w_proj': w(ks[14], (N_HEAD * V_HEAD, C))}
    _L0_attn_all = _L0_attn_setup()
    _L0_attn_in = {k: v for k, v in _L0_attn_all.items() if k in ('w_cq', 'g_qnorm', 'w_dq_nope', 'w_dq_rope', 'w_ckv', 'g_kvnorm', 'w_dk_nope', 'w_dv', 'w_krope', 'w_imp', 'w_selk', 'w_selv', 'w_wink', 'w_winv', 'w_gate', 'w_proj')}
    del _L0_attn_all

    def _L0_ffn_setup():
        import jax, jax.numpy as jnp
        import numpy as np
        JITTER_EPS = 0.01
        NEG_INF = -jnp.inf

        def sparsemixer_eval(scores, jitter_eps):
            m1 = jnp.max(scores, axis=-1, keepdims=True)
            ind1 = jnp.argmax(scores, axis=-1)
            factor1 = jnp.maximum(jnp.abs(scores), m1)
            mask1 = jax.lax.stop_gradient((m1 - scores) / factor1 > 2.0 * jitter_eps)
            gates1 = jax.nn.softmax(jnp.where(mask1, NEG_INF, scores), axis=-1)
            mult1 = jnp.take_along_axis(gates1, ind1[:, None], axis=-1)[:, 0]
            E = scores.shape[-1]
            onehot1 = ind1[:, None] == jnp.arange(E)[None, :]
            masked_scores = jnp.where(onehot1, NEG_INF, scores)
            m2 = jnp.max(masked_scores, axis=-1, keepdims=True)
            ind2 = jnp.argmax(masked_scores, axis=-1)
            factor2 = jnp.maximum(jnp.abs(scores), m2)
            mask2 = jax.lax.stop_gradient((m2 - scores) / factor2 > 2.0 * jitter_eps)
            gates2 = jax.nn.softmax(jnp.where(mask2, NEG_INF, masked_scores), axis=-1)
            mult2 = jnp.take_along_axis(gates2, ind2[:, None], axis=-1)[:, 0]
            multiplier = jnp.stack([mult1, mult2], axis=-1)
            selected = jnp.stack([ind1, ind2], axis=-1)
            return (multiplier, selected)
        key = jax.random.key(seed)
        k0, k1, k2, k3, k4 = jax.random.split(key, 5)
        B, S, H, F, E = (2, 256, 256, 512, 8)
        scale = 0.02
        return {'hidden_states': jax.random.normal(k0, (B, S, H), dtype=jnp.float32), 'router_w': jax.random.normal(k1, (E, H), dtype=jnp.float32) * scale, 'w_gate': jax.random.normal(k2, (E, F, H), dtype=jnp.float32) * scale, 'w_up': jax.random.normal(k3, (E, F, H), dtype=jnp.float32) * scale, 'w_down': jax.random.normal(k4, (E, H, F), dtype=jnp.float32) * scale}
    _L0_ffn_all = _L0_ffn_setup()
    _L0_ffn_in = {k: v for k, v in _L0_ffn_all.items() if k in ('router_w', 'w_gate', 'w_up', 'w_down')}
    del _L0_ffn_all
    return {'x': x, 'L0_tok_weight': _L0_tok_in['weight'], 'L0_attn_w_cq': _L0_attn_in['w_cq'], 'L0_attn_g_qnorm': _L0_attn_in['g_qnorm'], 'L0_attn_w_dq_nope': _L0_attn_in['w_dq_nope'], 'L0_attn_w_dq_rope': _L0_attn_in['w_dq_rope'], 'L0_attn_w_ckv': _L0_attn_in['w_ckv'], 'L0_attn_g_kvnorm': _L0_attn_in['g_kvnorm'], 'L0_attn_w_dk_nope': _L0_attn_in['w_dk_nope'], 'L0_attn_w_dv': _L0_attn_in['w_dv'], 'L0_attn_w_krope': _L0_attn_in['w_krope'], 'L0_attn_w_imp': _L0_attn_in['w_imp'], 'L0_attn_w_selk': _L0_attn_in['w_selk'], 'L0_attn_w_selv': _L0_attn_in['w_selv'], 'L0_attn_w_wink': _L0_attn_in['w_wink'], 'L0_attn_w_winv': _L0_attn_in['w_winv'], 'L0_attn_w_gate': _L0_attn_in['w_gate'], 'L0_attn_w_proj': _L0_attn_in['w_proj'], 'L0_ffn_router_w': _L0_ffn_in['router_w'], 'L0_ffn_w_gate': _L0_ffn_in['w_gate'], 'L0_ffn_w_up': _L0_ffn_in['w_up'], 'L0_ffn_w_down': _L0_ffn_in['w_down']}

def reference(x, L0_tok_weight, L0_attn_w_cq, L0_attn_g_qnorm, L0_attn_w_dq_nope, L0_attn_w_dq_rope, L0_attn_w_ckv, L0_attn_g_kvnorm, L0_attn_w_dk_nope, L0_attn_w_dv, L0_attn_w_krope, L0_attn_w_imp, L0_attn_w_selk, L0_attn_w_selv, L0_attn_w_wink, L0_attn_w_winv, L0_attn_w_gate, L0_attn_w_proj, L0_ffn_router_w, L0_ffn_w_gate, L0_ffn_w_up, L0_ffn_w_down):
    import jax
    import jax.numpy as jnp

    def _L0_tok_ref(input, weight):
        import jax, jax.numpy as jnp
        import numpy as np
        NUM_EMBEDDINGS = 32000
        EMBEDDING_DIM = 256
        EPS = 1e-05
        scale = 1.0 / jnp.maximum(jnp.mean(jnp.abs(weight)), EPS)
        quantized_weight = jnp.clip(jnp.round(weight * scale), -1.0, 1.0) / scale
        return quantized_weight[input]

    def _L0_attn_ref(x, w_cq, g_qnorm, w_dq_nope, w_dq_rope, w_ckv, g_kvnorm, w_dk_nope, w_dv, w_krope, w_imp, w_selk, w_selv, w_wink, w_winv, w_gate, w_proj):
        import jax, jax.numpy as jnp
        import numpy as np
        import math
        N_HEAD = 16
        V_HEAD = 32
        NOPE = 32
        ROPE_D = 64
        KEEP = 64
        EPS = 1e-06

        def _freqs(T, dim=ROPE_D, theta=10000.0):
            f = 1.0 / theta ** (jnp.arange(0, dim, 2, dtype=jnp.float32) / dim)
            t = jnp.arange(T, dtype=jnp.float32)
            a = jnp.outer(t, f)
            return (jnp.cos(a), jnp.sin(a))

        def _rope(x, cos, sin):
            S = x.shape[-2]
            c = cos[:S][None, None]
            s = sin[:S][None, None]
            x1, x2 = jnp.split(x, 2, axis=-1)
            return jnp.concatenate([x1 * c - x2 * s, x1 * s + x2 * c], axis=-1)

        def _rms(x, g, eps=EPS):
            return x * jax.lax.rsqrt(jnp.mean(x * x, axis=-1, keepdims=True) + eps) * g

        def _attn(q, k, v, causal):
            scale = 1.0 / math.sqrt(q.shape[-1])
            s = jnp.einsum('bhqd,bhkd->bhqk', q, k) * scale
            if causal:
                Tq, Tk = (s.shape[-2], s.shape[-1])
                mask = jnp.tril(jnp.ones((Tq, Tk), dtype=bool))
                s = jnp.where(mask, s, jnp.finfo(s.dtype).min)
            return jnp.einsum('bhqk,bhkd->bhqd', jax.nn.softmax(s, axis=-1), v)

        def _forward(x, w_cq, g_qnorm, w_dq_nope, w_dq_rope, w_ckv, g_kvnorm, w_dk_nope, w_dv, w_krope, w_imp, w_selk, w_selv, w_wink, w_winv, w_gate, w_proj):
            B, T, C = x.shape
            cos, sin = _freqs(T)
            nq = _rms(x @ w_cq, g_qnorm)
            q_nope = (nq @ w_dq_nope).reshape(B, T, N_HEAD, NOPE).transpose(0, 2, 1, 3)
            q_rope = (nq @ w_dq_rope).reshape(B, T, N_HEAD, ROPE_D).transpose(0, 2, 1, 3)
            q_rope = _rope(q_rope, cos, sin)
            q = jnp.concatenate([q_nope, q_rope], axis=-1)
            gate = jax.nn.softmax((x @ w_gate).mean(axis=1), axis=-1)
            ckv = _rms(x @ w_ckv, g_kvnorm)
            k_nope = (ckv @ w_dk_nope).reshape(B, T, N_HEAD, NOPE).transpose(0, 2, 1, 3)
            v1 = (ckv @ w_dv).reshape(B, T, N_HEAD, V_HEAD).transpose(0, 2, 1, 3)
            k_rope = (x @ w_krope).reshape(B, T, 1, ROPE_D).transpose(0, 2, 1, 3) / N_HEAD
            k_rope = _rope(k_rope, cos, sin)
            k1 = jnp.concatenate([k_nope, jnp.broadcast_to(k_rope, (B, N_HEAD, T, ROPE_D))], axis=-1)
            scores = (x @ w_imp)[..., 0]
            _, idx = jax.lax.top_k(scores, KEEP)
            idx = jnp.sort(idx, axis=1)
            sel = jnp.take_along_axis(x, idx[:, :, None], axis=1)
            ks = (sel @ w_selk).reshape(B, KEEP, N_HEAD, NOPE + ROPE_D).transpose(0, 2, 1, 3)
            vs = (sel @ w_selv).reshape(B, KEEP, N_HEAD, V_HEAD).transpose(0, 2, 1, 3)
            ks = jnp.concatenate([ks[..., :NOPE], _rope(ks[..., NOPE:], cos, sin)], axis=-1)
            kw = (x @ w_wink).reshape(B, T, N_HEAD, NOPE + ROPE_D).transpose(0, 2, 1, 3)
            vw = (x @ w_winv).reshape(B, T, N_HEAD, V_HEAD).transpose(0, 2, 1, 3)
            kw = jnp.concatenate([kw[..., :NOPE], _rope(kw[..., NOPE:], cos, sin)], axis=-1)
            a1 = _attn(q, k1, v1, causal=True)
            a2 = _attn(q, ks, vs, causal=False)
            a3 = _attn(q, kw, vw, causal=True)
            g = gate[:, :, None, None, None]
            out = g[:, 0] * a1 + g[:, 1] * a2 + g[:, 2] * a3
            out = out.transpose(0, 2, 1, 3).reshape(B, T, N_HEAD * V_HEAD)
            return out @ w_proj
        return _forward(x, w_cq, g_qnorm, w_dq_nope, w_dq_rope, w_ckv, g_kvnorm, w_dk_nope, w_dv, w_krope, w_imp, w_selk, w_selv, w_wink, w_winv, w_gate, w_proj)

    def _L0_ffn_ref(hidden_states, router_w, w_gate, w_up, w_down):
        import jax, jax.numpy as jnp
        import numpy as np
        JITTER_EPS = 0.01
        NEG_INF = -jnp.inf

        def sparsemixer_eval(scores, jitter_eps):
            m1 = jnp.max(scores, axis=-1, keepdims=True)
            ind1 = jnp.argmax(scores, axis=-1)
            factor1 = jnp.maximum(jnp.abs(scores), m1)
            mask1 = jax.lax.stop_gradient((m1 - scores) / factor1 > 2.0 * jitter_eps)
            gates1 = jax.nn.softmax(jnp.where(mask1, NEG_INF, scores), axis=-1)
            mult1 = jnp.take_along_axis(gates1, ind1[:, None], axis=-1)[:, 0]
            E = scores.shape[-1]
            onehot1 = ind1[:, None] == jnp.arange(E)[None, :]
            masked_scores = jnp.where(onehot1, NEG_INF, scores)
            m2 = jnp.max(masked_scores, axis=-1, keepdims=True)
            ind2 = jnp.argmax(masked_scores, axis=-1)
            factor2 = jnp.maximum(jnp.abs(scores), m2)
            mask2 = jax.lax.stop_gradient((m2 - scores) / factor2 > 2.0 * jitter_eps)
            gates2 = jax.nn.softmax(jnp.where(mask2, NEG_INF, masked_scores), axis=-1)
            mult2 = jnp.take_along_axis(gates2, ind2[:, None], axis=-1)[:, 0]
            multiplier = jnp.stack([mult1, mult2], axis=-1)
            selected = jnp.stack([ind1, ind2], axis=-1)
            return (multiplier, selected)
        B, S, H = hidden_states.shape
        E = router_w.shape[0]
        x = hidden_states.reshape(-1, H)
        T = x.shape[0]
        logits = x @ router_w.T
        routing_weights, selected = sparsemixer_eval(logits, JITTER_EPS)
        tok = jnp.arange(T)
        dense_w = jnp.zeros((T, E), dtype=x.dtype)
        dense_w = dense_w.at[tok, selected[:, 0]].add(routing_weights[:, 0])
        dense_w = dense_w.at[tok, selected[:, 1]].add(routing_weights[:, 1])
        out = jnp.zeros_like(x)
        for e in range(E):
            h = jax.nn.silu(x @ w_gate[e].T) * (x @ w_up[e].T)
            out = out + dense_w[:, e:e + 1] * (h @ w_down[e].T)
        return out.reshape(B, S, H)
    h = _L0_tok_ref(x, L0_tok_weight)
    h = h + _L0_attn_ref(_layernorm(h, axis=-1), L0_attn_w_cq, L0_attn_g_qnorm, L0_attn_w_dq_nope, L0_attn_w_dq_rope, L0_attn_w_ckv, L0_attn_g_kvnorm, L0_attn_w_dk_nope, L0_attn_w_dv, L0_attn_w_krope, L0_attn_w_imp, L0_attn_w_selk, L0_attn_w_selv, L0_attn_w_wink, L0_attn_w_winv, L0_attn_w_gate, L0_attn_w_proj)
    h = h + _L0_ffn_ref(_layernorm(h, axis=-1), L0_ffn_router_w, L0_ffn_w_gate, L0_ffn_w_up, L0_ffn_w_down)
    return h

_drawn_inputs = setup_inputs


def setup_inputs(seed=0):
    import zlib

    import numpy as np

    out = dict(_drawn_inputs(seed))
    spreads = {'L0_attn_g_qnorm': (1.0, 0.6), 'L0_attn_g_kvnorm': (1.0, 0.6)}
    factors = {'L0_attn_w_cq': 8.0,
     'L0_attn_w_dq_nope': 8.0,
     'L0_attn_w_dq_rope': 8.0,
     'L0_attn_w_ckv': 8.0,
     'L0_attn_w_dk_nope': 8.0,
     'L0_attn_w_dv': 8.0,
     'L0_attn_w_krope': 33.747,
     'L0_attn_w_imp': 3.614,
     'L0_attn_w_selk': 8.0,
     'L0_attn_w_selv': 3.545,
     'L0_attn_w_wink': 8.0,
     'L0_attn_w_winv': 8.0,
     'L0_attn_w_gate': 8.0,
     'L0_attn_w_proj': 3.475}
    for name, (base, spread) in spreads.items():
        noise = np.random.default_rng([zlib.crc32(name.encode()), seed]).standard_normal(out[name].shape)
        drawn = base * np.exp(spread * noise) if base else spread * noise
        out[name] = jnp.asarray(drawn.astype(out[name].dtype))
    for name, factor in factors.items():
        out[name] = (out[name] * factor).astype(out[name].dtype)
    return out
```

```python
from contextlib import ExitStack

import concourse.bass as bass
from concourse import mybir

F32 = mybir.dt.float32
F32R = mybir.dt.float32r
BF16 = mybir.dt.bfloat16
I32 = mybir.dt.int32
ALU = mybir.AluOpType
ACT = mybir.ActivationFunctionType
AX = mybir.AxisListType

P = 128
T = 2048
C = 256
NT = T // P
KC = C // P
H = 16
NOPE, ROPE, HALF = 32, 64, 32
DQK = NOPE + ROPE
DV = 32
QL, KVL = 96, 32
KEEP = 64
VOCAB = 32000
SCALE = float(DQK) ** -0.5
MASKED = -1.0e30
CH = 512
NJ = T // CH
LATENT, WINDOW, SELECT = 0, 1, 2
NB = 3
GATE = {LATENT: 0, SELECT: 1, WINDOW: 2}
QA = DQK + NB
V1 = DV + 1
E, F = 8, 512
FB = F // P
JITTER = 0.01

CQ0, CKV0, KR0, IMP0, GATE0, NS = 0, QL, QL + KVL, QL + KVL + ROPE, QL + KVL + ROPE + 1, QL + KVL + ROPE + 4


class Count:

    def __init__(self, eng, sem, base=0, after=None):
        self.eng, self.sem, self.base, self.n, self.after = eng, sem, base, 0, after

    def add(self, ins):
        self.n += 1
        return ins.then_inc(self.sem, 1)

    def wait(self):
        self.eng.wait_ge(self.sem, self.base + self.n)
        if self.after is not None:
            self.eng.sem_inc(self.after, 1)


def embed(nc, g, x, weight):
    ROWS = VOCAB // P
    NCHUNK, BUF = 16, 4
    W = ROWS * C // NCHUNK
    SPLIT = 2200
    wv = weight.rearrange("(p r) c -> p (r c)", p=P)
    with ExitStack() as ctx:
        tile = lambda n, s, d=F32: ctx.enter_context(nc.sbuf_tensor(n, s, d))
        wbuf = tile("wbuf", [P, BUF, W])
        junk = tile("abs_junk", [P, SPLIT], BF16)
        part = tile("abs_part", [P, 2 * NCHUNK])
        tot = tile("abs_tot", [P, 1])
        scale = tile("scale", [P, 4])
        idx = tile("tok_idx", [P, NT], I32)
        rows = tile("tok_rows", [P, NT, C])
        below = tile("below", [P, NT, C])
        h0 = tile("h0_tile", [P, NT, C])
        tsum = tile("tsum", [P, NT])
        usq = tile("usq", [P, C])
        var = tile("var_u", [P, NT])
        inv2 = tile("inv2", [P, 1])
        std = tile("std_u", [P, NT])
        pt = ctx.enter_context(nc.psum_tensor("ps_total", [P, CH], F32))
        s = {k: ctx.enter_context(nc.semaphore("a_" + k)) for k in
             ("idx", "gather", "act", "dve", "pe", "scale", "tern", "sq", "h0", "h0st", "std", "v", "const", "rst")}
        ld = [ctx.enter_context(nc.semaphore(f"a_w{i}")) for i in range(BUF)]
        block = ctx.enter_context(nc.Block())

        @block.sync
        def _(sp):
            for n in range(NCHUNK):
                if n >= BUF:
                    sp.wait_ge(s["act"], n - BUF + 1)
                    sp.wait_ge(s["dve"], n - BUF + 1)
                sp.dma_start(wbuf[:, n % BUF, :], wv[:, n * W:(n + 1) * W]).then_inc(ld[n % BUF], 16)
            sp.wait_ge(s["h0"], 1)
            sp.dma_start(g.h0_dram, h0[:].rearrange("p t c -> p (t c)")).then_inc(s["h0st"], 16)
            sp.wait_ge(s["h0st"], 16)

        @block.gpsimd
        def _(pool):
            pool.dma_start(idx[:], x.rearrange("o (t p) -> p (o t)", p=P)).then_inc(s["idx"], 16)
            cst = Count(pool, s["const"])
            cst.add(nc.gpsimd.memset(g.ones[:], 1.0))
            cst.add(nc.gpsimd.memset(g.ident[:], 0.0))
            cst.wait()
            cst.add(nc.gpsimd.affine_select(out=g.ident[:], in_=g.ident[:], compare_op=ALU.not_equal, fill=1.0,
                                            base=0, pattern=[[-1, P]], channel_multiplier=1))
            cst.wait()
            cst.add(nc.gpsimd.tensor_copy(g.ident16[:], g.ident[:]))
            cst.add(nc.gpsimd.memset(g.mask_qk[:], 0.0))
            cst.add(nc.gpsimd.memset(g.mask_kq[:], 0.0))
            cst.wait()
            cst.add(nc.gpsimd.affine_select(out=g.mask_qk[:], in_=g.mask_qk[:], compare_op=ALU.is_ge, fill=MASKED,
                                            base=0, pattern=[[-1, P]], channel_multiplier=1))
            cst.add(nc.gpsimd.affine_select(out=g.mask_kq[:], in_=g.mask_kq[:], compare_op=ALU.is_ge, fill=MASKED,
                                            base=0, pattern=[[1, P]], channel_multiplier=-1))
            pool.wait_ge(s["idx"], 16)
            for t in range(NT):
                nc.gpsimd.indirect_dma_start(out=rows[:, t, :], out_offset=None, in_=weight,
                                             in_offset=bass.IndirectOffsetOnAxis(ap=idx[:, t:t + 1], axis=0)
                                             ).then_inc(s["gather"], 16)
            cst.wait()

        @block.scalar
        def _(act):
            for n in range(NCHUNK):
                act.wait_ge(ld[n % BUF], 16 * (n // BUF + 1))
                if n:
                    act.wait_ge(s["act"], n)
                nc.scalar.activation(junk[:], wbuf[:, n % BUF, 0:SPLIT], ACT.Abs,
                                     accum_out=part[:, n:n + 1]).then_inc(s["act"], 1)
            act.wait_ge(s["tern"], 1)
            nc.scalar.activation(h0[:].rearrange("p t c -> p (t c)"), rows[:].rearrange("p t c -> p (t c)"),
                                 ACT.Copy, scale=g.inv[:, 0:1]).then_inc(s["h0"], 1)
            act.wait_ge(s["tern"], 2)
            for t in range(NT):
                if t:
                    act.wait_ge(s["sq"], t)
                nc.scalar.activation(usq[:], g.U[:, t, :], ACT.Square, accum_out=var[:, t:t + 1]).then_inc(s["sq"], 1)
            act.wait_ge(s["std"], 1)
            nc.scalar.activation(std[:], var[:], ACT.Sqrt).then_inc(s["rst"], 1)

        @block.tensor
        def _(pe):
            pe.wait_ge(s["const"], 1)
            pe.wait_ge(s["scale"], 1)
            nc.tensor.matmul(pt[:, 0:1], g.ones[:], tot[:], start=True, stop=True).then_inc(s["pe"], 1)

        @block.vector
        def _(dve):
            for n in range(NCHUNK):
                dve.wait_ge(ld[n % BUF], 16 * (n // BUF + 1))
                nc.vector.tensor_reduce(part[:, NCHUNK + n:NCHUNK + n + 1], wbuf[:, n % BUF, SPLIT:W], axis=AX.X,
                                        op=ALU.add, apply_absolute_value=True).then_inc(s["dve"], 1)
            v = Count(dve, s["v"])
            dve.wait_ge(s["act"], NCHUNK)
            dve.wait_ge(s["dve"], NCHUNK)
            nc.vector.tensor_reduce(tot[:], part[:], axis=AX.X, op=ALU.add).then_inc(s["scale"], 1)
            dve.wait_ge(s["pe"], 1)
            v.add(nc.vector.tensor_scalar(scale[:, 0:1], pt[:, 0:1], 1.0 / (VOCAB * C), 1e-5, ALU.mult, ALU.max))
            v.wait()
            v.add(nc.vector.reciprocal(scale[:, 1:2], scale[:, 0:1]))
            v.wait()
            v.add(nc.vector.reciprocal(g.inv[:], scale[:, 1:2]))
            dve.wait_ge(s["gather"], 16 * NT)
            v.add(nc.vector.tensor_scalar(below[:], rows[:], scale[:, 1:2], -0.5, ALU.mult, ALU.is_lt))
            v.wait()
            v.add(nc.vector.tensor_scalar(rows[:], rows[:], scale[:, 1:2], 0.5, ALU.mult, ALU.is_gt))
            v.wait()
            nc.vector.tensor_tensor(rows[:], rows[:], below[:], ALU.subtract).then_inc(s["tern"], 1)
            dve.wait_ge(s["tern"], 1)
            v.add(nc.vector.tensor_reduce(tsum[:], rows[:], axis=AX.X, op=ALU.add))
            v.wait()
            v.add(nc.vector.tensor_scalar(tsum[:], tsum[:], -1.0 / C, None, ALU.mult))
            v.wait()
            nc.vector.tensor_tensor(g.U[:], rows[:], tsum[:].unsqueeze(2).to_broadcast([P, NT, C]),
                                    ALU.add).then_inc(s["tern"], 1)
            v.add(nc.vector.tensor_tensor(inv2[:], g.inv[:], g.inv[:], ALU.mult))
            dve.wait_ge(s["sq"], NT)
            v.wait()
            v.add(nc.vector.tensor_scalar(var[:], var[:], inv2[:, 0:1], 1.0 / C, ALU.mult, ALU.mult))
            v.wait()
            nc.vector.tensor_scalar(var[:], var[:], 1e-5, None, ALU.add).then_inc(s["std"], 1)
            dve.wait_ge(s["rst"], 1)
            v.add(nc.vector.reciprocal(std[:], std[:]))
            v.wait()
            v.add(nc.vector.tensor_scalar(g.rstd[:], std[:], g.inv[:, 0:1], None, ALU.mult))
            v.wait()


def project(nc, g, a):
    with ExitStack() as ctx:
        tile = lambda n, s, d=F32: ctx.enter_context(nc.sbuf_tensor(n, s, d))
        wsm = tile("wsm", [P, KC, NS])
        wsm_hi, wsm_lo = tile("wsm_hi", [P, KC, NS], F32R), tile("wsm_lo", [P, KC, NS], F32R)
        wv = tile("wv", [P, KC, CH])
        wv_hi, wv_lo = tile("wv_hi", [P, KC, CH], F32R), tile("wv_lo", [P, KC, CH], F32R)
        wd = tile("wd", [P, CH])
        wd_hi, wd_lo = tile("wd_hi", [P, CH], F32R), tile("wd_lo", [P, CH], F32R)
        gains = tile("gains", [P, QL + KVL])
        lat = tile("latents", [P, NT, P])
        ss = tile("lat_ss", [P, 2, NT])
        krot = tile("krot", [P, NT, DQK])
        vt = tile("vt", [P, H, NT, V1])
        t1 = tile("kr_t1", [DQK, CH])
        t2 = tile("kr_t2", [DQK, CH])
        full = tile("kr_full", [DQK, CH])
        bank = [ctx.enter_context(nc.psum_tensor(f"b_ps{i}", [P, CH], F32)) for i in range(8)]
        s = {k: ctx.enter_context(nc.semaphore("b_" + k)) for k in
             ("w", "wd", "tab", "gain", "whi", "wlo", "tr", "ut", "sm", "smev", "smev1", "v", "std", "rt", "lat", "lt", "lhi", "llo",
              "kt", "kt1", "full", "khi", "klo", "vps", "vev", "v1ps", "v1ev", "vst", "one", "arst", "arld", "ca", "gt", "rot", "sst", "p", "krow")}
        block = ctx.enter_context(nc.Block())

        @block.sync
        def _(sp):
            for lo, w in ((CQ0, a["w_cq"]), (CKV0, a["w_ckv"]), (KR0, a["w_krope"]), (IMP0, a["w_imp"]), (GATE0, a["w_gate"])):
                sp.dma_start(wsm[:, :, lo:lo + w.shape[1]], w.rearrange("(k p) n -> p k n", p=P)).then_inc(s["w"], 16)
            sp.dma_start(wv[:], a["w_winv"].rearrange("(k p) n -> p k n", p=P)).then_inc(s["wd"], 16)
            sp.dma_start(wd[QL:P, :], a["w_dv"]).then_inc(s["wd"], 16)
            sp.dma_start(g.row_dram[0:1, :].rearrange("o (t p) -> p (o t)", p=P), g.rstd[:]).then_inc(s["arst"], 16)
            sp.wait_ge(s["arst"], 16)
            sp.dma_start(g.cos_a[:], g.row_dram[0:1, :].to_broadcast([DQK, T])).then_inc(s["arld"], 16)
            for b, (ev, n) in enumerate((("vev", 16), ("v1ev", 16))):
                sp.wait_ge(s[ev], n)
                if b == 0:
                    sp.wait_ge(s["one"], 1)
                sp.dma_start(g.v_dram[(WINDOW, LATENT)[b]].rearrange("h p n -> p h n"),
                             vt[:].rearrange("p h t n -> p h (t n)")).then_inc(s["vst"], 16)
                sp.wait_ge(s["vst"], 16 * (b + 1))
            sp.wait_ge(s["smev"], NT)
            sp.wait_ge(s["smev1"], 1)
            sp.dma_start(g.row_dram[1:2, :].rearrange("o (t p) -> p (o t)", p=P), g.imp[:]).then_inc(s["sst"], 16)
            sp.wait_ge(s["sst"], 16)

        @block.gpsimd
        def _(pool):
            for r in (NOPE, NOPE + HALF):
                pool.dma_start(g.cos[r:r + HALF, :], a["cos"]).then_inc(s["tab"], 16)
                pool.dma_start(g.sin[r:r + HALF, :], a["sin"]).then_inc(s["tab"], 16)
            pool.dma_start(gains[:, 0:QL], a["g_qnorm"].rearrange("(o n) -> o n", o=1).to_broadcast([P, QL])).then_inc(s["gain"], 16)
            pool.dma_start(gains[:, QL:P], a["g_kvnorm"].rearrange("(o n) -> o n", o=1).to_broadcast([P, KVL])).then_inc(s["gain"], 16)
            nc.gpsimd.memset(vt[:, :, :, DV:V1], 1.0).then_inc(s["one"], 1)
            p = Count(pool, s["p"])
            p.add(nc.gpsimd.memset(g.cos[0:NOPE, :], 1.0))
            p.add(nc.gpsimd.memset(g.sin[0:NOPE, :], 0.0))
            p.add(nc.gpsimd.memset(krot[:, :, 0:NOPE], 0.0))
            pool.wait_ge(s["tab"], 64)
            pool.wait_ge(s["arld"], 16)
            p.wait()
            nc.gpsimd.tensor_tensor(g.sin_a[:], g.sin[:], g.cos_a[:], ALU.mult).then_inc(s["ca"], 1)
            pool.wait_ge(s["ca"], 1)
            nc.gpsimd.tensor_tensor(g.cos_a[:], g.cos[:], g.cos_a[:], ALU.mult).then_inc(s["ca"], 1)
            for j in range(NJ):
                pool.wait_ge(s["khi"], 2 * (j + 1))
                nc.gpsimd.tensor_tensor(g.k1_lo[1][0:DQK, j * CH:(j + 1) * CH], full[:],
                                        g.k1_hi[1][0:DQK, j * CH:(j + 1) * CH].bitcast(F32), ALU.subtract).then_inc(s["klo"], 1)
            pool.wait_ge(s["klo"], NJ)
            pool.wait_ge(s["ca"], 2)

        def kr_transposes(pe):
            for j in range(NJ):
                for n, src in ((0, g.sm[:, :, CKV0:CKV0 + DQK]), (1, krot[:])):
                    m = 2 * j + n
                    if m >= 2:
                        pe.wait_ge(s["kt1"], m - 1)
                    for q in range(4):
                        last = nc.tensor.transpose(bank[4 + m % 2][0:DQK, q * P:(q + 1) * P], src[:, 4 * j + q, :], g.ident[:])
                    last.then_inc(s["kt"], 1)

        @block.tensor
        def _(pe):
            for n in range(8):
                kc, j = divmod(n, NJ)
                if n >= 4:
                    pe.wait_ge(s["ut"], n - 3)
                for q in range(4):
                    last = nc.tensor.transpose(bank[n % 4][:, q * P:(q + 1) * P],
                                               g.U[:, 4 * j + q, kc * P:(kc + 1) * P], g.ident[:])
                last.then_inc(s["tr"], 1)
            pe.wait_ge(s["ut"], 8)
            pe.wait_ge(s["whi"], 1)
            pe.wait_ge(s["wlo"], 1)
            for t in range(NT):
                if t >= 2:
                    pe.wait_ge(s["smev"], t - 1)
                for kc in range(KC):
                    for w in (wsm_hi, wsm_lo):
                        last = nc.tensor.matmul(bank[4 + t % 2][:, 0:NS], g.uT[:, kc, t * P:(t + 1) * P], w[:, kc, :],
                                                start=(kc == 0 and w is wsm_hi), stop=(kc == KC - 1 and w is wsm_lo))
                last.then_inc(s["sm"], 1)
            pe.wait_ge(s["whi"], 2)
            pe.wait_ge(s["wlo"], 2)
            for t in range(NT):
                if t >= 4:
                    pe.wait_ge(s["vev"], t - 3)
                for kc in range(KC):
                    for w in (wv_hi, wv_lo):
                        last = nc.tensor.matmul(bank[t % 4][:], g.uT[:, kc, t * P:(t + 1) * P], w[:, kc, :],
                                                start=(kc == 0 and w is wv_hi), stop=(kc == KC - 1 and w is wv_lo))
                last.then_inc(s["vps"], 1)
            pe.wait_ge(s["smev"], NT)
            for t in range(NT):
                last = nc.tensor.matmul(bank[7][:, 0:3], g.ones[:], g.sm[:, t, GATE0:GATE0 + 3], start=(t == 0), stop=(t == NT - 1))
            last.then_inc(s["gt"], 1)
            pe.wait_ge(s["rot"], 2)
            pe.wait_ge(s["p"], 3)
            kr_transposes(pe)
            pe.wait_ge(s["lat"], 1)
            for j in range(NJ):
                if j == 0:
                    pe.wait_ge(s["vev"], NT)
                if j >= 2:
                    pe.wait_ge(s["llo"], j - 1)
                for q in range(4):
                    last = nc.tensor.transpose(bank[j % 2][:, q * P:(q + 1) * P], lat[:, 4 * j + q, :], g.ident[:])
                last.then_inc(s["lt"], 1)
            pe.wait_ge(s["llo"], NJ)
            pe.wait_ge(s["whi"], 3)
            pe.wait_ge(s["wlo"], 3)
            for t in range(NT):
                if t >= 4:
                    pe.wait_ge(s["v1ev"], t - 3)
                for n, (l, w) in enumerate(((g.lat_hi, wd_hi), (g.lat_hi, wd_lo), (g.lat_lo, wd_hi))):
                    last = nc.tensor.matmul(bank[t % 4][:], l[QL:P, t * P:(t + 1) * P], w[QL:P, :], start=(n == 0), stop=(n == 2))
                last.then_inc(s["v1ps"], 1)

        @block.scalar
        def _(act):
            act.wait_ge(s["w"], 80)
            nc.scalar.copy(wsm_hi[:], wsm[:]).then_inc(s["whi"], 1)
            for n in range(0, 8, 2):
                kc, j = divmod(n, NJ)
                act.wait_ge(s["tr"], n + 1)
                if n:
                    act.wait_ge(s["ut"], n)
                nc.scalar.copy(g.uT[:, kc, j * CH:(j + 1) * CH], bank[n % 4][:]).then_inc(s["ut"], 1)
            for t in range(NT):
                act.wait_ge(s["sm"], t + 1)
                nc.scalar.activation(g.sm[:, t, :], bank[4 + t % 2][:, 0:NS], ACT.Copy, scale=g.rstd[:, t:t + 1]).then_inc(s["smev"], 1)
            act.wait_ge(s["wd"], 32)
            nc.scalar.copy(wv_hi[:], wv[:]).then_inc(s["whi"], 1)
            nc.scalar.copy(wd_hi[QL:P, :], wd[QL:P, :]).then_inc(s["whi"], 1)
            for t in range(NT):
                act.wait_ge(s["vps"], t + 1)
                nc.scalar.activation(vt[:, :, t, 0:DV], bank[t % 4][:].rearrange("p (h d) -> p h d", h=H), ACT.Copy,
                                     scale=g.rstd[:, t:t + 1]).then_inc(s["vev"], 1)
            act.wait_ge(s["std"], 1)
            nc.scalar.activation(ss[:], ss[:], ACT.Sqrt).then_inc(s["rt"], 1)
            for j in range(NJ):
                act.wait_ge(s["full"], j + 1)
                for par in range(2):
                    nc.scalar.copy(g.k1_hi[par][0:DQK, j * CH:(j + 1) * CH], full[:]).then_inc(s["khi"], 1)
            for j in range(NJ):
                act.wait_ge(s["lt"], j + 1)
                nc.scalar.copy(g.lat_hi[:, j * CH:(j + 1) * CH], bank[j % 2][:]).then_inc(s["lhi"], 1)
            act.wait_ge(s["vst"], 16)
            for t in range(NT):
                act.wait_ge(s["v1ps"], t + 1)
                nc.scalar.copy(vt[:, :, t, 0:DV], bank[t % 4][:].rearrange("p (h d) -> p h d", h=H)).then_inc(s["v1ev"], 1)

        @block.vector
        def _(dve):
            v = Count(dve, s["v"])
            for n in range(1, 8, 2):
                kc, j = divmod(n, NJ)
                dve.wait_ge(s["tr"], n + 1)
                dve.wait_ge(s["ut"], n)
                nc.vector.tensor_copy(g.uT[:, kc, j * CH:(j + 1) * CH], bank[n % 4][:]).then_inc(s["ut"], 1)
            dve.wait_ge(s["whi"], 1)
            nc.vector.tensor_tensor(wsm_lo[:], wsm[:], wsm_hi[:].bitcast(F32), ALU.subtract).then_inc(s["wlo"], 1)
            dve.wait_ge(s["whi"], 3)
            nc.vector.tensor_tensor(wv_lo[:], wv[:], wv_hi[:].bitcast(F32), ALU.subtract).then_inc(s["wlo"], 1)
            nc.vector.tensor_tensor(wd_lo[QL:P, :], wd[QL:P, :], wd_hi[QL:P, :].bitcast(F32), ALU.subtract).then_inc(s["wlo"], 1)
            dve.wait_ge(s["smev"], NT)
            nc.vector.tensor_copy(g.imp[:], g.sm[:, :, IMP0]).then_inc(s["smev1"], 1)
            v.add(nc.vector.tensor_scalar(g.sm[:, :, KR0:KR0 + ROPE], g.sm[:, :, KR0:KR0 + ROPE], 1.0 / H, None, ALU.mult))
            v.wait()
            nc.vector.tensor_scalar(krot[:, :, NOPE:NOPE + HALF], g.sm[:, :, KR0 + HALF:KR0 + ROPE], -1.0, None, ALU.mult).then_inc(s["rot"], 1)
            nc.vector.tensor_copy(krot[:, :, NOPE + HALF:DQK], g.sm[:, :, KR0:KR0 + HALF]).then_inc(s["rot"], 1)
            v.add(nc.vector.tensor_tensor(lat[:], g.sm[:, :, 0:P], g.sm[:, :, 0:P], ALU.mult))
            v.wait()
            v.add(nc.vector.tensor_reduce(ss[:, 0, :], lat[:, :, 0:QL], axis=AX.X, op=ALU.add))
            v.add(nc.vector.tensor_reduce(ss[:, 1, :], lat[:, :, QL:P], axis=AX.X, op=ALU.add))
            v.wait()
            v.add(nc.vector.tensor_scalar(ss[:, 0, :], ss[:, 0, :], 1.0 / QL, 1e-6, ALU.mult, ALU.add))
            nc.vector.tensor_scalar(ss[:, 1, :], ss[:, 1, :], 1.0 / KVL, 1e-6, ALU.mult, ALU.add).then_inc(s["std"], 1)
            dve.wait_ge(s["rt"], 1)
            v.add(nc.vector.reciprocal(ss[:], ss[:]))
            v.wait()
            v.add(nc.vector.tensor_tensor(lat[:, :, 0:QL], g.sm[:, :, 0:QL], ss[:, 0, :].unsqueeze(2).to_broadcast([P, NT, QL]), ALU.mult))
            v.add(nc.vector.tensor_tensor(lat[:, :, QL:P], g.sm[:, :, QL:P], ss[:, 1, :].unsqueeze(2).to_broadcast([P, NT, KVL]), ALU.mult))
            dve.wait_ge(s["gain"], 32)
            v.wait()
            nc.vector.tensor_tensor(lat[:], lat[:], gains[:].unsqueeze(1).to_broadcast([P, NT, P]), ALU.mult).then_inc(s["lat"], 1)
            dve.wait_ge(s["gt"], 1)
            v.add(nc.vector.tensor_scalar(g.gates[:], bank[7][:, 0:3], 1.0 / T, None, ALU.mult))
            dve.wait_ge(s["tab"], 64)
            dve.wait_ge(s["p"], 3)
            for j in range(NJ):
                c = slice(j * CH, (j + 1) * CH)
                dve.wait_ge(s["kt"], 2 * j + 1)
                nc.vector.tensor_tensor(t1[:], bank[4][0:DQK, :], g.cos[:, c], ALU.mult).then_inc(s["kt1"], 1)
                dve.wait_ge(s["kt"], 2 * j + 2)
                nc.vector.tensor_tensor(t2[:], bank[5][0:DQK, :], g.sin[:, c], ALU.mult).then_inc(s["kt1"], 1)
                dve.wait_ge(s["kt1"], 2 * j + 2)
                if j:
                    dve.wait_ge(s["klo"], j)
                nc.vector.tensor_tensor(full[:], t1[:], t2[:], ALU.add).then_inc(s["full"], 1)
                dve.wait_ge(s["khi"], 2 * j + 2)
                dve.wait_ge(s["full"], j + 1)
                v.add(nc.vector.tensor_tensor(g.k1_lo[0][0:DQK, c], full[:], g.k1_hi[0][0:DQK, c].bitcast(F32), ALU.subtract))
            for j in range(NJ):
                dve.wait_ge(s["lhi"], j + 1)
                nc.vector.tensor_tensor(g.lat_lo[:, j * CH:(j + 1) * CH], bank[j % 2][:], g.lat_hi[:, j * CH:(j + 1) * CH].bitcast(F32),
                                        ALU.subtract).then_inc(s["llo"], 1)
            v.wait()


def select(nc, g, a):
    with ExitStack() as ctx:
        tile = lambda n, s, d=F32: ctx.enter_context(nc.sbuf_tensor(n, s, d))
        srow = tile("score_row", [P, T])
        junk = tile("rank_junk", [P, T], BF16)
        before = tile("before", [P, T], BF16)
        strict = tile("strict", [P, P])
        ranks = tile("ranks", [P, 2, NT])
        flag = tile("flag", [P, NT])
        run = tile("flag_run", [P, NT])
        zero = tile("zero16", [P, NT])
        pos = tile("pos", [P, NT])
        slots = tile("slots", [P, KEEP])
        hot = tile("hot", [P, NT, KEEP])
        frs = tile("flag_rstd", [P, NT])
        selT = tile("selT", [P, KC, KEEP])
        wk = tile("wselk", [P, KC, H * DQK])
        wv = tile("wselv", [P, KC, H * DV])
        ktm = tile("ks_tok", [KEEP, H, DQK])
        krt = tile("ks_rot", [KEEP, H, DQK])
        kt1, kt2 = tile("ks_t1", [KEEP, H, HALF]), tile("ks_t2", [KEEP, H, HALF])
        kt3, kt4 = tile("ks_t3", [KEEP, H, HALF]), tile("ks_t4", [KEEP, H, HALF])
        ck, sk = tile("ck", [KEEP, HALF]), tile("sk", [KEEP, HALF])
        khi = tile("ks_hi_all", [QA, H, P], F32R)
        klo = tile("ks_lo_all", [DQK, H, P], F32R)
        gm = tile("gate_tmp", [P, 8])
        bank = [ctx.enter_context(nc.psum_tensor(f"s_ps{i}", [P, CH], F32)) for i in range(8)]
        s = {k: ctx.enter_context(nc.semaphore("s_" + k)) for k in
             ("row", "w", "t", "p", "v", "flag", "run", "pos", "hot", "sel", "selc", "ks", "rope", "kt", "khi", "klo", "vs", "vsc", "st", "ge", "gx", "c1", "kcp")}
        block = ctx.enter_context(nc.Block())

        @block.sync
        def _(sp):
            sp.dma_start(srow[:], g.row_dram[1:2, :].to_broadcast([P, T])).then_inc(s["row"], 16)
            sp.dma_start(wk[:], a["w_selk"].rearrange("(k p) n -> p k n", p=P)).then_inc(s["w"], 16)
            sp.dma_start(wv[:], a["w_selv"].rearrange("(k p) n -> p k n", p=P)).then_inc(s["w"], 16)
            sp.dma_start(ck[:], a["cos_tok"]).then_inc(s["t"], 16)
            sp.dma_start(sk[:], a["sin_tok"]).then_inc(s["t"], 16)
            sp.wait_ge(s["khi"], 2)
            sp.wait_ge(s["c1"], 7)
            sp.dma_start(g.ks_dram[:, 0:QA, :].rearrange("h r k -> r h k"), khi[:].bitcast(F32)).then_inc(s["st"], 16)
            sp.wait_ge(s["klo"], 2)
            sp.dma_start(g.ks_dram[:, QA:QA + DQK, :].rearrange("h r k -> r h k"), klo[:].bitcast(F32)).then_inc(s["st"], 16)
            sp.wait_ge(s["st"], 32)

        @block.gpsimd
        def _(pool):
            p = Count(pool, s["p"])
            p.add(nc.gpsimd.memset(before[:], 1.0))
            p.add(nc.gpsimd.memset(strict[:], 1.0))
            p.add(nc.gpsimd.memset(zero[:], 0.0))
            p.add(nc.gpsimd.iota(slots[:], pattern=[[1, KEEP]], base=0, channel_multiplier=0, allow_small_or_imprecise_dtypes=True))
            p.wait()
            p.add(nc.gpsimd.affine_select(out=before[:], in_=before[:], compare_op=ALU.is_gt, fill=0.0,
                                          base=T - P, pattern=[[-1, T]], channel_multiplier=1))
            p.add(nc.gpsimd.affine_select(out=strict[:], in_=strict[:], compare_op=ALU.is_gt, fill=0.0,
                                          base=0, pattern=[[1, P]], channel_multiplier=-1))
            c1 = Count(pool, s["c1"])
            c1.add(nc.gpsimd.memset(khi[:].bitcast(F32), 0.0))
            c1.add(nc.gpsimd.memset(klo[:].bitcast(F32), 0.0))
            c1.wait()
            c1.add(nc.gpsimd.memset(g.onehot[DQK:QA, :], 0.0))
            c1.wait()
            c1.add(nc.gpsimd.affine_select(out=g.onehot[DQK:QA, :], in_=g.onehot[DQK:QA, :], compare_op=ALU.not_equal, fill=1.0,
                                           base=0, pattern=[[-1, NB]], channel_multiplier=1))
            c1.wait()
            for k in g.k1_hi:
                c1.add(nc.gpsimd.tensor_copy(k[DQK:QA, :], g.onehot[DQK:QA, LATENT:LATENT + 1].to_broadcast([NB, T])))
            c1.add(nc.gpsimd.tensor_copy(khi[DQK:QA, :, :].rearrange("r h k -> r (h k)"),
                                         g.onehot[DQK:QA, SELECT:SELECT + 1].to_broadcast([NB, H * P])))
            c1.wait()
            p.wait()

        @block.tensor
        def _(pe):
            pe.wait_ge(s["p"], 6)
            pe.wait_ge(s["flag"], 1)
            nc.tensor.matmul(bank[0][:, 0:NT], strict[:], flag[:], start=True, stop=False)
            pe.wait_ge(s["run"], 1)
            nc.tensor.matmul(bank[0][:, 0:NT], g.ones[:], run[:], start=False, stop=True).then_inc(s["pos"], 1)
            pe.wait_ge(s["hot"], 1)
            for kc in range(KC):
                for t in range(NT):
                    last = nc.tensor.matmul(bank[1 + kc][:, 0:KEEP], g.U[:, t, kc * P:(kc + 1) * P], hot[:, t, :], start=(t == 0), stop=(t == NT - 1))
            last.then_inc(s["sel"], 1)
            pe.wait_ge(s["selc"], 1)
            pe.wait_ge(s["w"], 32)
            for n in range(4):
                for kc in range(KC):
                    w = wk[:, kc, n * CH:(n + 1) * CH] if n < 3 else wv[:, kc, :]
                    last = nc.tensor.matmul(bank[3 + n][0:KEEP, :], selT[:, kc, :], w, start=(kc == 0), stop=(kc == KC - 1))
                last.then_inc(s["ks"], 1)
            pe.wait_ge(s["rope"], 1)
            for h in range(H):
                last = nc.tensor.transpose(bank[h // 8][0:DQK, (h % 8) * KEEP:(h % 8 + 1) * KEEP], krt[:, h, :], g.ident[0:KEEP, 0:KEEP])
            last.then_inc(s["kt"], 1)

        @block.scalar
        def _(act):
            act.wait_ge(s["ge"], 1)
            nc.scalar.activation(gm[:, 2:5], g.gates[:], ACT.Exp, bias=gm[:, 0:1], accum_out=gm[:, 1:2]).then_inc(s["gx"], 1)
            act.wait_ge(s["ks"], 4)
            nc.scalar.copy(g.vs[:, :, 0:DV], bank[6][0:KEEP, :].rearrange("p (h d) -> p h d", h=H)).then_inc(s["vsc"], 1)
            act.wait_ge(s["kt"], 1)
            act.wait_ge(s["c1"], 2)
            for n in range(2):
                nc.scalar.copy(khi[0:DQK, 8 * n:8 * n + 8, 0:KEEP], bank[n][0:DQK, :].rearrange("p (h k) -> p h k", h=8)).then_inc(s["khi"], 1)
            act.wait_ge(s["vsc"], 1)

        @block.vector
        def _(dve):
            v = Count(dve, s["v"])
            v.add(nc.vector.tensor_reduce(gm[:, 0:1], g.gates[:], axis=AX.X, op=ALU.max))
            v.wait()
            nc.vector.tensor_scalar(gm[:, 0:1], gm[:, 0:1], -1.0, None, ALU.mult).then_inc(s["ge"], 1)
            v.add(nc.vector.memset(g.vs[:, :, DV:V1], 1.0))
            dve.wait_ge(s["row"], 16)
            dve.wait_ge(s["p"], 6)
            for t in range(NT):
                sc = g.imp[:, t:t + 1]
                v.wait()
                v.add(nc.vector.tensor_scalar(junk[:], srow[:], sc, None, ALU.is_gt, ALU.add, accum_out=ranks[:, 0, t:t + 1]))
                n = (t + 1) * P
                v.wait()
                v.add(nc.vector.scalar_tensor_tensor(junk[:, 0:n], srow[:, 0:n], sc, before[:, T - n:T], ALU.is_equal, ALU.mult,
                                                     accum_out=ranks[:, 1, t:t + 1]))
            v.wait()
            v.add(nc.vector.tensor_tensor(flag[:], ranks[:, 0, :], ranks[:, 1, :], ALU.add))
            v.wait()
            nc.vector.tensor_scalar(flag[:], flag[:], float(KEEP), None, ALU.is_lt).then_inc(s["flag"], 1)
            dve.wait_ge(s["flag"], 1)
            v.add(nc.vector.tensor_tensor_scan(run[:], flag[:], zero[:], 0.0, ALU.add, ALU.add))
            v.wait()
            nc.vector.tensor_tensor(run[:], run[:], flag[:], ALU.subtract).then_inc(s["run"], 1)
            dve.wait_ge(s["gx"], 1)
            v.add(nc.vector.reciprocal(gm[:, 5:6], gm[:, 1:2]))
            v.wait()
            v.add(nc.vector.tensor_scalar(g.gates[:], gm[:, 2:5], gm[:, 5:6], None, ALU.mult))
            dve.wait_ge(s["pos"], 1)
            v.add(nc.vector.tensor_copy(pos[:], bank[0][:, 0:NT]))
            v.add(nc.vector.tensor_tensor(frs[:], flag[:], g.rstd[:], ALU.mult))
            v.wait()
            for t in range(NT):
                ins = nc.vector.tensor_scalar(hot[:, t, :], slots[:], pos[:, t:t + 1], frs[:, t:t + 1], ALU.is_equal, ALU.mult)
            ins.then_inc(s["hot"], 1)
            dve.wait_ge(s["sel"], 1)
            v.add(nc.vector.tensor_copy(selT[:, 0, :], bank[1][:, 0:KEEP]))
            nc.vector.tensor_copy(selT[:, 1, :], bank[2][:, 0:KEEP]).then_inc(s["selc"], 1)
            dve.wait_ge(s["ks"], 3)
            for n in range(3):
                v.add(nc.vector.tensor_copy(ktm[:].rearrange("p h d -> p (h d)")[:, n * CH:(n + 1) * CH], bank[3 + n][0:KEEP, :]))
            v.wait()
            dve.wait_ge(s["t"], 32)
            x1, x2 = ktm[:, :, NOPE:NOPE + HALF], ktm[:, :, NOPE + HALF:DQK]
            cb = ck[:].unsqueeze(1).to_broadcast([KEEP, H, HALF])
            sbc = sk[:].unsqueeze(1).to_broadcast([KEEP, H, HALF])
            v.add(nc.vector.tensor_tensor(kt1[:], x1, cb, ALU.mult))
            v.add(nc.vector.tensor_tensor(kt2[:], x2, sbc, ALU.mult))
            v.add(nc.vector.tensor_tensor(kt3[:], x1, sbc, ALU.mult))
            v.add(nc.vector.tensor_tensor(kt4[:], x2, cb, ALU.mult))
            v.add(nc.vector.tensor_copy(krt[:, :, 0:NOPE], ktm[:, :, 0:NOPE]))
            v.wait()
            v.add(nc.vector.tensor_tensor(krt[:, :, NOPE:NOPE + HALF], kt1[:], kt2[:], ALU.subtract))
            nc.vector.tensor_tensor(krt[:, :, NOPE + HALF:DQK], kt3[:], kt4[:], ALU.add).then_inc(s["rope"], 1)
            for n in range(2):
                dve.wait_ge(s["khi"], n + 1)
                nc.vector.tensor_tensor(klo[:, 8 * n:8 * n + 8, 0:KEEP], bank[n][0:DQK, :].rearrange("p (h k) -> p h k", h=8),
                                        khi[0:DQK, 8 * n:8 * n + 8, 0:KEEP].bitcast(F32), ALU.subtract).then_inc(s["klo"], 1)
            v.wait()


def units():
    out = []
    for b in (WINDOW, LATENT):
        out += [(b, j, k) for j in range(NJ) for k in range(4 * j + 4)]
    return out + [(SELECT, j, 0) for j in range(NJ)]


UNITS = units()
NU = len(UNITS)
NPJ = 21
NMX = 82


def side_tasks():
    proj = lambda what: [(what, j, rot) for j in range(NJ) for rot in (0, 1)]
    mx = lambda b: [("max", b, q, c) for q in range(NT) for c in range(q // 4 + 1)]
    late = 6
    first = proj("q") + [("k1", j) for j in range(NJ)] + [("max", SELECT, n, 0) for n in range(2)]
    lat, win = mx(LATENT), mx(WINDOW)
    first += lat[:-late]
    second = proj("kw") + lat[-late:] + win + [("neg",)]
    at = {}
    for tasks, lo, hi in ((first, 3, 39), (second, 41, NU - 5)):
        for n, t in enumerate(tasks):
            at.setdefault(lo + n * (hi - lo) // len(tasks), []).append(t)
    return at


SIDE = side_tasks()


def attend(nc, g, a):
    with ExitStack() as ctx:
        tile = lambda n, s, d=F32: ctx.enter_context(nc.sbuf_tensor(n, s, d))
        q_hi = [tile(f"q_hi{i}", [QA, T], F32R) for i in range(2)]
        q_lo = [tile(f"q_lo{i}", [DQK, T], F32R) for i in range(2)]
        kw_hi, kw_lo = tile("kw_hi", [QA, T], F32R), tile("kw_lo", [DQK, T], F32R)
        ks_hi = [tile(f"ks_hi{i}", [QA, P], F32R) for i in range(2)]
        ks_lo = [tile(f"ks_lo{i}", [DQK, P], F32R) for i in range(2)]
        v_lat = [tile(f"v_lat{i}", [P, NT, V1]) for i in range(2)]
        v_win = [tile(f"v_win{i}", [P, NT, V1]) for i in range(2)]
        prob = g.early[:, 0:4 * CH].rearrange("p (n c) -> p n c", c=CH)
        oh = [g.early[:, (4 + i) * CH:(5 + i) * CH].rearrange("p (t d) -> p t d", d=DV) for i in range(2)]
        otmp = tile("o_tmp", [P, 4, DV])
        rec = tile("rec", [P, 2, 4])
        t1, t2, full = (g.early[0:DQK, n * CH:(n + 2) * CH].rearrange("p (n c) -> p n c", c=CH) for n in (6, 8, 10))
        mpart = tile("max_part", [P, 2, NT, NJ])
        nm = tile("neg_max", [P, NB * NT])
        nm_t = tile("neg_max_t", [NB * NT, P], F32R)
        raw_q = tile("raw_q", [DQK, DQK])
        raw_k1 = tile("raw_k1", [P, NOPE])
        raw_kw = tile("raw_kw", [P, KC, DQK])
        wq = [tile(f"wq_{n}", [QL, 2, DQK], F32R) for n in ("hi", "lo")]
        wk1 = [tile(f"wk1_{n}", [P, DQK], F32R) for n in ("hi", "lo")]
        wkw = [tile(f"wkw_{n}", [P, KC, 2, DQK], F32R) for n in ("hi", "lo")]
        ps_s = [ctx.enter_context(nc.psum_tensor(f"ps_s{i}", [P, CH], F32)) for i in range(3)]
        ps_o = [ctx.enter_context(nc.psum_tensor(f"ps_o{i}", [P, CH], F32)) for i in range(2)]
        ps_m = [ctx.enter_context(nc.psum_tensor(f"ps_m{i}", [P, CH], F32)) for i in range(2)]
        ps_p = ctx.enter_context(nc.psum_tensor("ps_p", [P, CH], F32))
        s = {k: ctx.enter_context(nc.semaphore("h_" + k)) for k in
             ("scores", "exp", "pv", "acc", "fin", "mx", "mxfree", "pj", "pjfree", "rotd", "full", "hi", "lo", "k1", "k1c", "nm", "nmt", "rows",
              "raw", "built", "wb", "wz", "v", "ks", "store", "ohd", "mz", "kwz", "passed", "pe_passed")}
        block = ctx.enter_context(nc.Block())
        k_hi = {LATENT: g.k1_hi, WINDOW: [kw_hi, kw_hi], SELECT: ks_hi}
        k_lo = {LATENT: g.k1_lo, WINDOW: [kw_lo, kw_lo], SELECT: ks_lo}
        NFIN = 3 * 4 + 4 * 8

        def load_raw(sp, h):
            sp.dma_start(raw_q[:, 0:NOPE], a["w_dq_nope"][:, bass.ds(h * NOPE, NOPE)]).then_inc(s["raw"], 16)
            sp.dma_start(raw_q[:, NOPE:DQK], a["w_dq_rope"][:, bass.ds(h * ROPE, ROPE)]).then_inc(s["raw"], 16)
            sp.dma_start(raw_k1[QL:P, :], a["w_dk_nope"][:, bass.ds(h * NOPE, NOPE)]).then_inc(s["raw"], 16)
            sp.dma_start(raw_kw[:], a["w_wink"].rearrange("(k p) n -> p k n", p=P)[:, :, bass.ds(h * DQK, DQK)]).then_inc(s["raw"], 16)

        def load_kv(sp, h, par):
            for vt, b in ((v_lat, LATENT), (v_win, WINDOW)):
                sp.dma_start(vt[par][:].rearrange("p t n -> p (t n)"),
                             g.v_dram[b, bass.ds(h, 1)].rearrange("o p n -> (o p) n")).then_inc(s["v"], 16)
            sp.dma_start(ks_hi[par][:].bitcast(F32), g.ks_dram[bass.ds(h, 1), 0:QA, :].rearrange("o r k -> (o r) k")).then_inc(s["ks"], 16)
            sp.dma_start(ks_lo[par][:].bitcast(F32), g.ks_dram[bass.ds(h, 1), QA:QA + DQK, :].rearrange("o r k -> (o r) k")).then_inc(s["ks"], 16)

        def store_rows(sp, p, par):
            sp.wait_ge(s["nmt"], p + 1)
            for b in range(NB):
                sp.dma_start(q_hi[par][DQK + b:DQK + b + 1, :].bitcast(F32).rearrange("o (t q) -> o t q", q=P),
                             nm_t[b * NT:(b + 1) * NT, :].bitcast(F32)).then_inc(s["rows"], 16)

        def sp_head(sp, h, par, prep, prep2):
            if prep:
                sp.wait_ge(s["pv"], NU * h + 4)
                load_kv(sp, h + 1, 1 - par)
            if prep2:
                sp.wait_ge(s["built"], h + 2)
                load_raw(sp, h + 2)
            if prep:
                store_rows(sp, h + 1, 1 - par)
            sp.wait_ge(s["ohd"], h + 1)
            sp.dma_start(g.o_dram[:, :, bass.ds(h * DV, DV)], oh[par]).then_inc(s["store"], 16)

        @block.sync
        def _(sp):
            load_kv(sp, 0, 0)
            load_raw(sp, 0)
            sp.wait_ge(s["built"], 1)
            load_raw(sp, 1)
            store_rows(sp, 0, 0)
            with sp.Fori(0, H // 2 - 1) as pair:
                sp_head(sp, 2 * pair, 0, True, True)
                sp_head(sp, 2 * pair + 1, 1, True, True)
            sp_head(sp, H - 2, 0, True, False)
            sp_head(sp, H - 1, 1, False, False)
            sp.wait_ge(s["store"], 32 + 16 * H)

        NWB = 14

        def build_weights(pool, p):
            w = Count(pool, s["wb"], NWB * p, after=s["passed"])
            pool.wait_ge(s["raw"], 64 * (p + 1))
            if not isinstance(p, int) or p > 0:
                pool.wait_ge(s["pj"], NPJ * p)
            pool.sem_inc(s["passed"], 1)
            w.add(nc.gpsimd.tensor_copy(wq[0][:, 0, :], raw_q[:]))
            w.add(nc.gpsimd.tensor_copy(wkw[0][:, :, 0, :], raw_kw[:]))
            w.wait()
            w.add(nc.gpsimd.tensor_copy(wk1[0][QL:P, 0:NOPE], raw_k1[QL:P, :]))
            w.wait()
            w.add(nc.gpsimd.tensor_tensor(wq[1][:, 0, :], raw_q[:], wq[0][:, 0, :].bitcast(F32), ALU.subtract))
            w.add(nc.gpsimd.tensor_tensor(wkw[1][:, :, 0, :], raw_kw[:], wkw[0][:, :, 0, :].bitcast(F32), ALU.subtract))
            w.wait()
            w.add(nc.gpsimd.tensor_tensor(wk1[1][QL:P, 0:NOPE], raw_k1[QL:P, :], wk1[0][QL:P, 0:NOPE].bitcast(F32), ALU.subtract))
            w.wait()
            x1, x2 = slice(NOPE, NOPE + HALF), slice(NOPE + HALF, DQK)
            for t in wq:
                w.add(nc.gpsimd.tensor_scalar(t[:, 1, x1], t[:, 0, x2].bitcast(F32), -1.0, None, ALU.mult))
                w.add(nc.gpsimd.tensor_copy(t[:, 1, x2], t[:, 0, x1].bitcast(F32)))
            for t in wkw:
                w.add(nc.gpsimd.tensor_scalar(t[:, :, 1, x1], t[:, :, 0, x2].bitcast(F32), -1.0, None, ALU.mult))
                w.add(nc.gpsimd.tensor_copy(t[:, :, 1, x2], t[:, :, 0, x1].bitcast(F32)))
            w.wait()
            assert w.n == NWB, w.n
            pool.sem_inc(s["built"], 1)

        def dst(what, par):
            return (q_hi[par], q_lo[par]) if what == "q" else (kw_hi, kw_lo)

        ROPED = [(w, j) for w in ("q", "kw") for j in range(NJ)]

        def pool_prep(pool, p, par):
            for half in range(2):
                for n in range(4 * half, 4 * half + 4):
                    pool.wait_ge(s["rotd"], 8 * p + n + 1)
                    if n >= 2 or not isinstance(p, int) or p:
                        pool.wait_ge(s["lo"], 8 * p + n - 1)
                    nc.gpsimd.tensor_tensor(full[:, n % 2, :], t1[:, n % 2, :], t2[:, n % 2, :], ALU.add).then_inc(s["full"], 1)
                    if n > 4 * half:
                        rest_of(pool, p, par, n - 1)
                rest_of(pool, p, par, 4 * half + 3)

        def rest_of(pool, p, par, n):
            what, j = ROPED[n]
            hi, lo = dst(what, par)
            pool.wait_ge(s["hi"], 8 * p + n + 1)
            nc.gpsimd.tensor_tensor(lo[0:DQK, j * CH:(j + 1) * CH], full[:, n % 2, :],
                                    hi[0:DQK, j * CH:(j + 1) * CH].bitcast(F32), ALU.subtract).then_inc(s["lo"], 1)

        @block.gpsimd
        def _(pool):
            for t in wq + wkw:
                nc.gpsimd.memset(t[:].bitcast(F32), 0.0).then_inc(s["wz"], 1)
            nc.gpsimd.memset(mpart[:], -3.0e38).then_inc(s["mz"], 1)
            pool.wait_ge(s["wz"], 4)
            pool.wait_ge(s["mz"], 1)
            for t in wk1:
                nc.gpsimd.memset(t[QL:P, :].bitcast(F32), 0.0).then_inc(s["wz"], 1)
            nc.gpsimd.tensor_copy(kw_hi[DQK:QA, :], g.onehot[DQK:QA, WINDOW:WINDOW + 1].to_broadcast([NB, T])).then_inc(s["kwz"], 1)
            pool.wait_ge(s["wz"], 6)
            pool.wait_ge(s["kwz"], 1)
            build_weights(pool, 0)
            pool_prep(pool, 0, 0)

            def head(h, par):
                build_weights(pool, h + 1)
                pool_prep(pool, h + 1, 1 - par)
            with pool.Fori(0, H // 2 - 1) as pair:
                head(2 * pair, 0)
                head(2 * pair + 1, 1)
            head(H - 2, 0)

        def act_task(act, task, p, par):
            if task[0] in ("q", "kw") and task[2] == 1:
                n = ROPED.index((task[0], task[1]))
                act.wait_ge(s["full"], 2 + 8 * p + n + 1)
                nc.scalar.copy(dst(task[0], par)[0][0:DQK, task[1] * CH:(task[1] + 1) * CH], full[:, n % 2, :]).then_inc(s["hi"], 1)

        def act_unit(act, h, i):
            b, j, k = UNITS[i]
            c = max(0, k - 4 * j) * P if b != SELECT else 0
            rows = KEEP if b == SELECT else P
            act.wait_ge(s["scores"], NU * h + i + 1)
            act.wait_ge(s["pv"], NU * h + i + 1)
            nc.scalar.activation(prob[0:rows, i % 4, c:CH], ps_s[i % 3][0:rows, c:CH], ACT.Exp, scale=SCALE).then_inc(s["exp"], 1)

        ACT_LAG = 2

        @block.scalar
        def _(act):
            act.sem_inc(s["exp"], 3)
            for i in sorted(SIDE):
                for task in SIDE[i]:
                    act_task(act, task, 0, 0)

            def head(h, par, prep):
                for i in range(NU):
                    act_unit(act, h, i)
                    if prep:
                        for task in SIDE.get(i - ACT_LAG, ()):
                            act_task(act, task, h + 1, 1 - par)
            with act.Fori(0, H // 2 - 1) as pair:
                head(2 * pair, 0, True)
                head(2 * pair + 1, 1, True)
            head(H - 2, 0, True)
            head(H - 1, 1, False)

        PJ, MX, FIRST_MX = {}, {}, {}
        for i in sorted(SIDE):
            for task in SIDE[i]:
                if task[0] == "max":
                    MX[task] = len(MX)
                    FIRST_MX.setdefault(task[1], task)
                else:
                    PJ[task] = len(PJ)
        assert len(PJ) == NPJ and len(MX) == NMX

        def three(out, khi, klo, qhi, qlo, mid=None, rows=DQK, start=True, stop=True):
            nc.tensor.matmul(out, khi, qhi, start=start, stop=False)
            if mid:
                mid()
            nc.tensor.matmul(out, khi[0:rows] if rows else khi, qlo, start=False, stop=False)
            return nc.tensor.matmul(out, klo, qhi[0:rows] if rows else qhi, start=False, stop=stop)

        def pe_task(pe, task, p, par):
            if task[0] == "max":
                _, b, q, c = task
                n = MX[task]
                if task == FIRST_MX[b]:
                    pe.wait_ge(s["hi"], 8 * p + (8 if b == WINDOW else 4))
                    if b == LATENT:
                        pe.wait_ge(s["k1"], 4 * p + 4)
                    if b == SELECT:
                        pe.wait_ge(s["ks"], 32 * (p + 1))
                pe.wait_ge(s["mxfree"], NMX * p + n + 1)
                bank = ps_m[n % 2]
                if b == SELECT:
                    for r in range(8):
                        last = nc.tensor.matmul(bank[:, r * KEEP:(r + 1) * KEEP], q_hi[par][0:DQK, (8 * q + r) * P:(8 * q + r + 1) * P],
                                                ks_hi[par][0:DQK, 0:KEEP], start=True, stop=True)
                else:
                    w = min(CH, (q + 1) * P - c * CH)
                    diag = c == q // 4
                    last = nc.tensor.matmul(bank[:, 0:w], q_hi[par][0:DQK, q * P:(q + 1) * P], k_hi[b][par][0:DQK, c * CH:c * CH + w],
                                            start=True, stop=not diag)
                    if diag:
                        last = nc.tensor.matmul(bank[:, w - P:w], g.ident16[:], g.mask_qk[:], start=False, stop=True)
                last.then_inc(s["mx"], 1)
                return
            n = PJ[task]
            if n == 0:
                pe.wait_ge(s["built"], p + 1)
            pe.wait_ge(s["pjfree"], NPJ * p + n + 1)
            if task[0] == "q":
                _, j, rot = task
                c = slice(j * CH, (j + 1) * CH)
                last = three(ps_p[0:DQK, :], wq[0][:, rot, :], wq[1][:, rot, :], g.lat_hi[0:QL, c], g.lat_lo[0:QL, c], rows=None)
            elif task[0] == "k1":
                c = slice(task[1] * CH, (task[1] + 1) * CH)
                last = three(ps_p[0:DQK, :], wk1[0][QL:P, :], wk1[1][QL:P, :], g.lat_hi[QL:P, c], g.lat_lo[QL:P, c], rows=None)
            elif task[0] == "kw":
                _, j, rot = task
                for kc in range(KC):
                    for w in range(2):
                        last = nc.tensor.matmul(ps_p[0:DQK, :], wkw[w][:, kc, rot, :], g.uT[:, kc, j * CH:(j + 1) * CH],
                                                start=(kc == 0 and w == 0), stop=(kc == KC - 1 and w == 1))
            else:
                pe.wait_ge(s["nm"], p + 1)
                pe.sem_inc(s["pe_passed"], 1)
                last = nc.tensor.transpose(ps_p[0:NB * NT, 0:P], nm[:], g.ident[:])
            last.then_inc(s["pj"], 1)

        def pe_scores(pe, h, par, i):
            b, j, k = UNITS[i]
            if i == 0:
                pe.wait_ge(s["lo"], 8 * h + 8)
                pe.wait_ge(s["rows"], 48 * (h + 1))
            if b == LATENT and j == 0 and k == 0:
                pe.wait_ge(s["k1"], 4 * h + 4)
            d = max(0, k - 4 * j) if b != SELECT else 0
            diag = b != SELECT and k >= 4 * j
            pe.wait_ge(s["exp"], NU * h + i + 1)
            qs, ks = slice(j * CH + d * P, (j + 1) * CH), slice(k * P, (k + 1) * P)
            bank = ps_s[i % 3]
            mid = (lambda: nc.tensor.matmul(bank[:, d * P:(d + 1) * P], g.ident16[:], g.mask_kq[:], start=False, stop=False)) if diag else None
            three(bank[:, d * P:CH], k_hi[b][par][:, ks], k_lo[b][par][:, ks], q_hi[par][:, qs], q_lo[par][:, qs], mid).then_inc(s["scores"], 1)

        def pe_values(pe, h, par, i):
            b, j, k = UNITS[i]
            n = 4 * (WINDOW, LATENT, SELECT).index(b) + j
            if i == 0:
                pe.wait_ge(s["v"], 32 * (h + 1))
            pe.wait_ge(s["exp"], NU * h + i + 4)
            if k == 0:
                pe.wait_ge(s["acc"], 12 * h + n + 1)
            if b == SELECT:
                pe.sem_inc(s["pe_passed"], 1)
            d = max(0, k - 4 * j) if b != SELECT else 0
            for q in range(d, 4):
                first, lastk = k == 0 and q == 0, (b == SELECT or k == 4 * j + 3) and q == 3
                if b == SELECT:
                    lhs, rhs = prob[0:KEEP, i % 4, q * P:(q + 1) * P], g.vs[:, bass.ds(h, 1), :].rearrange("p o n -> p (o n)")
                else:
                    lhs, rhs = prob[:, i % 4, q * P:(q + 1) * P], (v_lat if b == LATENT else v_win)[par][:, k, :]
                last = nc.tensor.matmul(ps_o[n % 2][:, q * V1:(q + 1) * V1], lhs, rhs, start=first, stop=lastk, skip_group_check=True)
            last.then_inc(s["pv"], 1)

        PV_LAG = 2

        @block.tensor
        def _(pe):
            pe.sem_inc(s["pv"], 4)
            pe.wait_ge(s["kwz"], 1)
            for i in sorted(SIDE):
                for task in SIDE[i]:
                    pe_task(pe, task, 0, 0)

            def head(h, par, prep):
                for i in range(NU):
                    pe_scores(pe, h, par, i)
                    if prep:
                        for task in SIDE.get(i, ()):
                            pe_task(pe, task, h + 1, 1 - par)
                    if i >= PV_LAG:
                        pe_values(pe, h, par, i - PV_LAG)
                for i in range(NU - PV_LAG, NU):
                    pe_values(pe, h, par, i)
            with pe.Fori(0, H // 2 - 1) as pair:
                head(2 * pair, 0, True)
                head(2 * pair + 1, 1, True)
            head(H - 2, 0, True)
            head(H - 1, 1, False)

        def dve_task(dve, task, p, par):
            if task[0] == "max":
                _, b, q, c = task
                n = MX[task]
                dve.wait_ge(s["mx"], NMX * p + n + 1)
                bank = ps_m[n % 2]
                if b == SELECT:
                    ins = nc.vector.tensor_reduce(nm[:, SELECT * NT + 8 * q:SELECT * NT + 8 * q + 8],
                                                  bank[:].rearrange("p (q k) -> p q k", k=KEEP), axis=AX.X, op=ALU.max, negate=True)
                else:
                    w = min(CH, (q + 1) * P - c * CH)
                    ins = nc.vector.tensor_reduce(mpart[:, b, q, c:c + 1], bank[:, 0:w], axis=AX.X, op=ALU.max)
                ins.then_inc(s["mxfree"], 1)
                return
            n = PJ[task]
            if task[0] in ("q", "kw"):
                what, j, rot = task
                r = ROPED.index((what, j))
                c = slice(j * CH, (j + 1) * CH)
                tab = (g.cos, g.sin) if what == "q" else (g.cos_a, g.sin_a)
                if rot == 0:
                    dve.wait_ge(s["full"], 8 * p + r + 1)
                dve.wait_ge(s["pj"], NPJ * p + n + 1)
                nc.vector.tensor_tensor((t1, t2)[rot][:, r % 2, :], ps_p[0:DQK, :], tab[rot][:, c], ALU.mult).then_inc(s["pjfree"], 1)
                if rot:
                    dve.wait_ge(s["pjfree"], 1 + NPJ * p + n + 1)
                    dve.sem_inc(s["rotd"], 1)
            elif task[0] == "k1":
                c = slice(task[1] * CH, (task[1] + 1) * CH)
                dve.wait_ge(s["pj"], NPJ * p + n + 1)
                nc.vector.tensor_copy(g.k1_hi[par][0:NOPE, c], ps_p[0:NOPE, :]).then_inc(s["k1c"], 1)
                dve.wait_ge(s["k1c"], 4 * p + task[1] + 1)
                nc.vector.tensor_tensor(g.k1_lo[par][0:NOPE, c], ps_p[0:NOPE, :], g.k1_hi[par][0:NOPE, c].bitcast(F32), ALU.subtract).then_inc(s["pjfree"], 1)
                dve.wait_ge(s["pjfree"], 1 + NPJ * p + n + 1)
                dve.sem_inc(s["k1"], 1)
            else:
                dve.wait_ge(s["mxfree"], 2 + NMX * (p + 1))
                if not isinstance(p, int) or p:
                    dve.wait_ge(s["pj"], NPJ * p)
                nc.vector.tensor_reduce(nm[:, 0:2 * NT], mpart[:].rearrange("p b q c -> p (b q) c"), axis=AX.X, op=ALU.max, negate=True).then_inc(s["nm"], 1)
                dve.wait_ge(s["pj"], NPJ * p + n + 1)
                if not isinstance(p, int) or p:
                    dve.wait_ge(s["rows"], 48 * p)
                nc.vector.tensor_copy(nm_t[:], ps_p[0:NB * NT, 0:P]).then_inc(s["pjfree"], 1)
                dve.wait_ge(s["pjfree"], 1 + NPJ * p + n + 1)
                dve.sem_inc(s["nmt"], 1)

        def dve_output(dve, h, par, i):
            b, j, k = UNITS[i]
            if b != SELECT and k != 4 * j + 3:
                return
            nb = (WINDOW, LATENT, SELECT).index(b)
            n = 4 * nb + j
            f = Count(dve, s["fin"], NFIN * h + (3 * j if nb == 0 else 12 + 4 * (n - 4)))
            bank = ps_o[n % 2][:, 0:4 * V1].rearrange("p (q n) -> p q n", n=V1)
            if n == 0:
                dve.wait_ge(s["store"], 16 * h + 16)
            dve.wait_ge(s["pv"], 4 + NU * h + i + 1)
            f.add(nc.vector.reciprocal(rec[:, 0, :], bank[:, :, DV]))
            f.wait()
            f.add(nc.vector.tensor_scalar(rec[:, 1, :], rec[:, 0, :], g.gates[:, GATE[b]:GATE[b] + 1], None, ALU.mult))
            f.wait()
            fac = rec[:, 1, :].unsqueeze(2).to_broadcast([P, 4, DV])
            out = oh[par][:, 4 * j:4 * j + 4, :]
            if nb == 0:
                f.add(nc.vector.tensor_tensor(out, bank[:, :, 0:DV], fac, ALU.mult))
                f.wait()
            else:
                f.add(nc.vector.tensor_tensor(otmp[:], bank[:, :, 0:DV], fac, ALU.mult))
                f.wait()
                f.add(nc.vector.tensor_tensor(out, out, otmp[:], ALU.add))
                f.wait()
            dve.sem_inc(s["acc"], 1)
            if n == 11:
                dve.sem_inc(s["ohd"], 1)

        @block.vector
        def _(dve):
            dve.sem_inc(s["mxfree"], 2)
            dve.sem_inc(s["pjfree"], 1)
            dve.sem_inc(s["acc"], 2)
            dve.sem_inc(s["full"], 2)
            dve.sem_inc(s["store"], 32)
            dve.wait_ge(s["mz"], 1)
            for i in sorted(SIDE):
                for task in SIDE[i]:
                    dve_task(dve, task, 0, 0)

            def head(h, par, prep):
                for i in range(NU):
                    if prep:
                        for task in SIDE.get(i, ()):
                            dve_task(dve, task, h + 1, 1 - par)
                    if i >= PV_LAG:
                        dve_output(dve, h, par, i - PV_LAG)
                for i in range(NU - PV_LAG, NU):
                    dve_output(dve, h, par, i)
            with dve.Fori(0, H // 2 - 1) as pair:
                head(2 * pair, 0, True)
                head(2 * pair + 1, 1, True)
            head(H - 2, 0, True)
            head(H - 1, 1, False)


def mix(nc, g, a):
    with ExitStack() as ctx:
        tile = lambda n, s, d=F32: ctx.enter_context(nc.sbuf_tensor(n, s, d))
        KB = H * DV // P
        o = tile("o_all", [P, NT, H * DV])
        h0 = tile("h0_again", [P, NT, C])
        wp = tile("wp", [P, KB, C])
        wp_hi, wp_lo = tile("wp_hi", [P, KB, C], F32R), tile("wp_lo", [P, KB, C], F32R)
        rw = tile("rw", [P, KC, E])
        rw_hi, rw_lo = tile("rw_hi", [P, KC, E], F32R), tile("rw_lo", [P, KC, E], F32R)
        ot_hi, ot_lo = tile("ot_hi", [P, 2, CH], F32R), tile("ot_lo", [P, 2, CH], F32R)
        stats = tile("bn", [P, NT, 6])
        mv = tile("bn_mv", [P, NT, 2])
        rstd = tile("rstd2", [P, NT])
        x2 = tile("x2", [P, NT, C])
        logit = tile("logit", [P, NT, E])
        sc = {n: tile("sm_" + n, [P, NT, E]) for n in ("hot1", "hot2", "rest", "dist", "fac", "keep", "ex", "tie", "order")}
        top = {n: tile("st_" + n, [P, NT]) for n in ("m1", "m2", "t", "sum", "w1", "w2")}
        bank = [ctx.enter_context(nc.psum_tensor(f"m_ps{i}", [P, CH], F32)) for i in range(8)]
        s = {k: ctx.enter_context(nc.semaphore("m_" + k)) for k in
             ("o", "w", "rw", "h0", "whi", "wlo", "tr", "ohi", "olo", "y", "h1", "v", "var", "rt", "x2", "xt", "xhi", "xlo", "lg", "ord", "ex", "exd", "lgc")}
        block = ctx.enter_context(nc.Block())

        @block.sync
        def _(sp):
            sp.dma_start(o[:], g.o_dram).then_inc(s["o"], 16)
            sp.dma_start(wp[:], a["w_proj"].rearrange("(k p) n -> p k n", p=P)).then_inc(s["w"], 16)
            sp.dma_start(h0[:].rearrange("p t c -> p (t c)"), g.h0_dram).then_inc(s["h0"], 16)

        @block.gpsimd
        def _(pool):
            for k in range(KC):
                pool.dma_start(rw[:, k, :], a["router_w"][:, k * P:(k + 1) * P].rearrange("e p -> p e")).then_inc(s["rw"], 16)
            nc.gpsimd.iota(sc["order"][:], pattern=[[0, NT], [-1, E]], base=E, channel_multiplier=0,
                           allow_small_or_imprecise_dtypes=True).then_inc(s["ord"], 1)
            pool.wait_ge(s["ord"], 1)

        @block.tensor
        def _(pe):
            def out_transposes(t):
                if t >= 2:
                    pe.wait_ge(s["olo"], t - 1)
                for k in range(KB):
                    last = nc.tensor.transpose(bank[t % 2][:, k * P:(k + 1) * P], o[:, t, k * P:(k + 1) * P], g.ident[:])
                last.then_inc(s["tr"], 1)

            def out_product(t):
                pe.wait_ge(s["olo"], t + 1)
                if t >= 2:
                    pe.wait_ge(s["h1"], t - 1)
                for k in range(KB):
                    for n, (l, w) in enumerate(((ot_hi, wp_hi), (ot_hi, wp_lo), (ot_lo, wp_hi))):
                        last = nc.tensor.matmul(bank[2 + t % 2][:, 0:C], l[:, t % 2, k * P:(k + 1) * P], w[:, k, :],
                                                start=(k == 0 and n == 0), stop=(k == KB - 1 and n == 2))
                last.then_inc(s["y"], 1)
            pe.wait_ge(s["o"], 16)
            out_transposes(0)
            pe.wait_ge(s["whi"], 2)
            pe.wait_ge(s["wlo"], 2)
            for t in range(NT):
                if t + 1 < NT:
                    out_transposes(t + 1)
                out_product(t)
            for n in range(8):
                kc, j = divmod(n, NJ)
                pe.wait_ge(s["x2"], 4 * j + 4)
                if n >= 4:
                    pe.wait_ge(s["xlo"], n - 3)
                for q in range(4):
                    last = nc.tensor.transpose(bank[4 + n % 4][:, q * P:(q + 1) * P], x2[:, 4 * j + q, kc * P:(kc + 1) * P], g.ident[:])
                last.then_inc(s["xt"], 1)
            pe.wait_ge(s["xlo"], 8)
            for t in range(NT):
                for kc in range(KC):
                    for n, (l, w) in enumerate(((g.x_hi, rw_hi), (g.x_hi, rw_lo), (g.x_lo, rw_hi))):
                        last = nc.tensor.matmul(bank[0][:, t * E:(t + 1) * E], l[:, kc, t * P:(t + 1) * P], w[:, kc, :],
                                                start=(kc == 0 and n == 0), stop=(kc == KC - 1 and n == 2))
            last.then_inc(s["lg"], 1)

        @block.scalar
        def _(act):
            act.wait_ge(s["w"], 16)
            act.wait_ge(s["rw"], 32)
            nc.scalar.copy(wp_hi[:], wp[:]).then_inc(s["whi"], 1)
            nc.scalar.copy(rw_hi[:], rw[:]).then_inc(s["whi"], 1)
            for t in range(NT):
                act.wait_ge(s["tr"], t + 1)
                if t >= 2:
                    act.wait_ge(s["y"], t - 1)
                nc.scalar.copy(ot_hi[:, t % 2, :], bank[t % 2][:]).then_inc(s["ohi"], 1)
            act.wait_ge(s["var"], 1)
            nc.scalar.activation(rstd[:], rstd[:], ACT.Sqrt).then_inc(s["rt"], 1)
            for n in range(8):
                kc, j = divmod(n, NJ)
                act.wait_ge(s["xt"], n + 1)
                nc.scalar.copy(g.x_hi[:, kc, j * CH:(j + 1) * CH], bank[4 + n % 4][:]).then_inc(s["xhi"], 1)
            for n in range(2):
                act.wait_ge(s["ex"], n + 1)
                nc.scalar.activation(sc["ex"][:], sc["dist"][:], ACT.Exp, scale=-1.0).then_inc(s["exd"], 1)

        @block.vector
        def _(dve):
            v = Count(dve, s["v"])
            dve.wait_ge(s["whi"], 2)
            nc.vector.tensor_tensor(wp_lo[:], wp[:], wp_hi[:].bitcast(F32), ALU.subtract).then_inc(s["wlo"], 1)
            nc.vector.tensor_tensor(rw_lo[:], rw[:], rw_hi[:].bitcast(F32), ALU.subtract).then_inc(s["wlo"], 1)
            dve.wait_ge(s["h0"], 16)

            def residual(t):
                dve.wait_ge(s["y"], t + 1)
                nc.vector.tensor_tensor(g.h1[:, t, :], bank[2 + t % 2][:, 0:C], h0[:, t, :], ALU.add).then_inc(s["h1"], 1)
            for t in range(NT):
                dve.wait_ge(s["ohi"], t + 1)
                nc.vector.tensor_tensor(ot_lo[:, t % 2, :], bank[t % 2][:], ot_hi[:, t % 2, :].bitcast(F32), ALU.subtract).then_inc(s["olo"], 1)
                if t:
                    residual(t - 1)
            residual(NT - 1)
            for t in range(NT):
                dve.wait_ge(s["h1"], t + 1)
                v.add(nc.vector.bn_stats(stats[:, t, :], g.h1[:, t, :]))
            v.wait()
            for t in range(NT):
                v.add(nc.vector.bn_aggr(mv[:, t, :], stats[:, t, :]))
            v.wait()
            nc.vector.tensor_scalar(rstd[:], mv[:, :, 1], 1e-5, None, ALU.add).then_inc(s["var"], 1)
            dve.wait_ge(s["rt"], 1)
            v.add(nc.vector.reciprocal(rstd[:], rstd[:]))
            v.wait()
            for t in range(NT):
                nc.vector.tensor_scalar(x2[:, t, :], g.h1[:, t, :], mv[:, t, 0:1], rstd[:, t:t + 1], ALU.subtract, ALU.mult).then_inc(s["x2"], 1)
            for n in range(8):
                kc, j = divmod(n, NJ)
                c = slice(j * CH, (j + 1) * CH)
                dve.wait_ge(s["xhi"], n + 1)
                nc.vector.tensor_tensor(g.x_lo[:, kc, c], bank[4 + n % 4][:], g.x_hi[:, kc, c].bitcast(F32), ALU.subtract).then_inc(s["xlo"], 1)
            dve.wait_ge(s["lg"], 1)
            dve.wait_ge(s["ord"], 1)
            v.add(nc.vector.tensor_copy(logit[:].rearrange("p t e -> p (t e)"), bank[0][:, 0:NT * E]))
            v.wait()

            def step(ins):
                v.add(ins)
                v.wait()

            wide = lambda t: t[:].unsqueeze(2).to_broadcast([P, NT, E])

            def gate(scores, m, hot, weight, n, banned):
                step(nc.vector.tensor_reduce(m[:], scores[:], axis=AX.X, op=ALU.max))
                step(nc.vector.tensor_tensor(sc["tie"][:], scores[:], wide(m), ALU.is_equal))
                step(nc.vector.tensor_tensor(sc["tie"][:], sc["tie"][:], sc["order"][:], ALU.mult))
                step(nc.vector.tensor_reduce(top["t"][:], sc["tie"][:], axis=AX.X, op=ALU.max))
                step(nc.vector.tensor_tensor(hot[:], sc["tie"][:], wide(top["t"]), ALU.is_equal))
                step(nc.vector.tensor_scalar(sc["fac"][:], logit[:], -1.0, None, ALU.mult))
                step(nc.vector.tensor_tensor(sc["fac"][:], sc["fac"][:], logit[:], ALU.max))
                step(nc.vector.tensor_tensor(sc["fac"][:], sc["fac"][:], wide(m), ALU.max))
                v.add(nc.vector.tensor_tensor(sc["dist"][:], wide(m), logit[:], ALU.subtract))
                v.wait()
                step(nc.vector.tensor_scalar(sc["fac"][:], sc["fac"][:], 2.0 * JITTER, None, ALU.mult))
                step(nc.vector.tensor_tensor(sc["keep"][:], sc["dist"][:], sc["fac"][:], ALU.is_le))
                if banned is not None:
                    step(nc.vector.tensor_tensor(sc["tie"][:], sc["keep"][:], banned[:], ALU.mult))
                    step(nc.vector.tensor_tensor(sc["keep"][:], sc["keep"][:], sc["tie"][:], ALU.subtract))
                    step(nc.vector.tensor_scalar(sc["dist"][:], sc["dist"][:], 0.0, None, ALU.max))
                dve.sem_inc(s["ex"], 1)
                dve.wait_ge(s["exd"], n + 1)
                step(nc.vector.tensor_tensor(sc["keep"][:], sc["keep"][:], sc["ex"][:], ALU.mult))
                step(nc.vector.tensor_reduce(top["sum"][:], sc["keep"][:], axis=AX.X, op=ALU.add))
                step(nc.vector.reciprocal(weight[:], top["sum"][:]))

            gate(logit, top["m1"], sc["hot1"], top["w1"], 0, None)
            step(nc.vector.tensor_scalar(sc["rest"][:], sc["hot1"][:], -3.0e38, None, ALU.mult))
            step(nc.vector.tensor_tensor(sc["rest"][:], sc["rest"][:], logit[:], ALU.add))
            gate(sc["rest"], top["m2"], sc["hot2"], top["w2"], 1, sc["hot1"])
            step(nc.vector.tensor_tensor(sc["hot1"][:], sc["hot1"][:], wide(top["w1"]), ALU.mult))
            step(nc.vector.tensor_tensor(sc["hot2"][:], sc["hot2"][:], wide(top["w2"]), ALU.mult))
            step(nc.vector.tensor_tensor(g.dense[:], sc["hot1"][:], sc["hot2"][:], ALU.add))


def experts(nc, g, a, out):
    with ExitStack() as ctx:
        tile = lambda n, s, d=F32: ctx.enter_context(nc.sbuf_tensor(n, s, d))
        NG = NJ * FB
        raw = {"g": tile("raw_g", [P, FB, C]), "u": tile("raw_u", [P, FB, C]), "d": tile("raw_d", [P, KC, F])}
        wt = [[tile(f"wt{i}_{n}", [P, 6, CH], F32R) for n in ("hi", "lo")] for i in range(2)]
        sg = tile("silu", [P, 2, CH])
        hm = tile("hm", [P, 2, CH])
        h_hi, h_lo = tile("h_hi", [P, 2, FB, CH], F32R), tile("h_lo", [P, 2, FB, CH], F32R)
        ps_g = [ctx.enter_context(nc.psum_tensor(f"e_g{i}", [P, CH], F32)) for i in range(2)]
        ps_u = [ctx.enter_context(nc.psum_tensor(f"e_u{i}", [P, CH], F32)) for i in range(2)]
        ps_y = [ctx.enter_context(nc.psum_tensor(f"e_y{i}", [P, CH], F32)) for i in range(2)]
        ps_t = [ctx.enter_context(nc.psum_tensor(f"e_t{i}", [P, CH], F32)) for i in range(2)]
        s = {k: ctx.enter_context(nc.semaphore("e_" + k)) for k in
             ("raw", "tr", "whi", "wlo", "g", "u", "silu", "hm", "hi", "lo", "y", "acc", "out")}
        block = ctx.enter_context(nc.Block())
        LOOP = E - 2

        def load(sp, e):
            pick = lambda w: w[bass.ds(e, 1)].rearrange("o r c -> (o r) c")
            sp.dma_start(raw["g"][:], pick(a["w_gate_e"]).rearrange("(b p) c -> p b c", p=P)).then_inc(s["raw"], 16)
            sp.dma_start(raw["u"][:], pick(a["w_up"]).rearrange("(b p) c -> p b c", p=P)).then_inc(s["raw"], 16)
            sp.dma_start(raw["d"][:], pick(a["w_down"]).rearrange("(b p) c -> p b c", p=P)).then_inc(s["raw"], 16)

        @block.sync
        def _(sp):
            load(sp, 0)
            sp.wait_ge(s["tr"], 6)
            load(sp, 1)
            with sp.Fori(0, LOOP) as e:
                sp.wait_ge(s["tr"], 6 * e + 12)
                load(sp, e + 2)
            for n in range(NT):
                sp.wait_ge(s["acc"], 2 + NT * (E - 1) + n + 1)
                sp.dma_start(out[0, n * P:(n + 1) * P, :], g.h1[:, n, :]).then_inc(s["out"], 16)
            sp.wait_ge(s["out"], 16 * NT)

        def transposes(pe, e, par):
            pe.wait_ge(s["raw"], 48 * (e + 1))
            for b in range(6):
                pe.wait_ge(s["wlo"], 6 * e + b + 1)
                for q in range(4):
                    if b < 4:
                        src = raw["gu"[b // 2]][:, q, (b % 2) * P:(b % 2 + 1) * P]
                    else:
                        f = 2 * (b - 4) + q // 2
                        src = raw["d"][:, q % 2, f * P:(f + 1) * P]
                    last = nc.tensor.transpose(ps_t[b % 2][:, q * P:(q + 1) * P], src, g.ident[:])
                last.then_inc(s["tr"], 1)

        def gate_up(pe, e, par, n):
            hi, lo = wt[par]
            c = slice(n * CH, (n + 1) * CH)
            if n == 0:
                pe.wait_ge(s["wlo"], 2 + 6 * (e + 1))
            for f in range(FB):
                i = n * FB + f
                cols = slice(f * P, (f + 1) * P)
                for ps, m, sem, free in ((ps_g, 0, "g", "silu"), (ps_u, 2, "u", "hm")):
                    pe.wait_ge(s[free], NG * e + i + 1)
                    for kc in range(KC):
                        for k, (w, x) in enumerate(((hi, g.x_hi), (hi, g.x_lo), (lo, g.x_hi))):
                            last = nc.tensor.matmul(ps[i % 2][:], w[:, m + kc, cols], x[:, kc, c],
                                                    start=(kc == 0 and k == 0), stop=(kc == KC - 1 and k == 2))
                    last.then_inc(s[sem], 1)

        def down(pe, e, par, n):
            hi, lo = wt[par]
            pe.wait_ge(s["lo"], 2 + NG * e + FB * (n + 1))
            for q in range(4):
                i = 4 * n + q
                pe.wait_ge(s["acc"], NT * e + i + 1)
                for f in range(FB):
                    wcols = slice((f % 2) * C, (f % 2 + 1) * C)
                    for k, (h, w) in enumerate(((h_hi, hi), (h_hi, lo), (h_lo, hi))):
                        last = nc.tensor.matmul(ps_y[i % 2][:, 0:C], h[:, n % 2, f, q * P:(q + 1) * P], w[:, 4 + f // 2, wcols],
                                                start=(f == 0 and k == 0), stop=(f == FB - 1 and k == 2))
                last.then_inc(s["y"], 1)

        @block.tensor
        def _(pe):
            def expert(e, par, prep):
                for n in range(NJ):
                    gate_up(pe, e, par, n)
                    if n:
                        down(pe, e, par, n - 1)
                if prep:
                    transposes(pe, e + 1, 1 - par)
                down(pe, e, par, NJ - 1)
            transposes(pe, 0, 0)
            with pe.Fori(0, LOOP // 2) as pair:
                expert(2 * pair, 0, True)
                expert(2 * pair + 1, 1, True)
            expert(E - 2, 0, True)
            expert(E - 1, 1, False)

        @block.scalar
        def _(act):
            act.sem_inc(s["silu"], 2)

            def upper_weights(e, par):
                for b in range(6):
                    act.wait_ge(s["tr"], 6 * e + b + 1)
                    nc.scalar.copy(wt[par][0][:, b, :], ps_t[b % 2][:]).then_inc(s["whi"], 1)

            def upper(e, i):
                n, f = divmod(i, FB)
                act.wait_ge(s["hm"], 2 + NG * e + i + 1)
                act.wait_ge(s["y"], NT * e + 4 * n + 4)
                nc.scalar.copy(h_hi[:, n % 2, f, :], hm[:, i % 2, :]).then_inc(s["hi"], 1)

            def expert(e, par, prep):
                for i in range(NG):
                    act.wait_ge(s["g"], NG * e + i + 1)
                    act.wait_ge(s["hm"], NG * e + i + 1)
                    nc.scalar.activation(sg[:, i % 2, :], ps_g[i % 2][:], ACT.Silu).then_inc(s["silu"], 1)
                    if i:
                        upper(e, i - 1)
                upper(e, NG - 1)
                if prep:
                    upper_weights(e + 1, 1 - par)
            upper_weights(0, 0)
            with act.Fori(0, LOOP // 2) as pair:
                expert(2 * pair, 0, True)
                expert(2 * pair + 1, 1, True)
            expert(E - 2, 0, True)
            expert(E - 1, 1, False)

        @block.gpsimd
        def _(pool):
            pool.sem_inc(s["lo"], 2)

            def expert(e):
                for i in range(NG):
                    n, f = divmod(i, FB)
                    pool.wait_ge(s["hi"], NG * e + i + 1)
                    nc.gpsimd.tensor_tensor(h_lo[:, n % 2, f, :], hm[:, i % 2, :], h_hi[:, n % 2, f, :].bitcast(F32), ALU.subtract).then_inc(s["lo"], 1)
            with pool.Fori(0, E) as e:
                expert(e)

        @block.vector
        def _(dve):
            dve.sem_inc(s["wlo"], 2)
            dve.sem_inc(s["hm"], 2)
            dve.sem_inc(s["acc"], 2)
            dve.sem_inc(s["y"], 8)

            def lower_weights(e, par):
                for b in range(6):
                    dve.wait_ge(s["whi"], 6 * e + b + 1)
                    nc.vector.tensor_tensor(wt[par][1][:, b, :], ps_t[b % 2][:], wt[par][0][:, b, :].bitcast(F32), ALU.subtract).then_inc(s["wlo"], 1)

            def accumulate(e, n):
                for q in range(4):
                    i = 4 * n + q
                    dve.wait_ge(s["y"], 8 + NT * e + i + 1)
                    nc.vector.scalar_tensor_tensor(g.h1[:, i, :], ps_y[i % 2][:, 0:C], g.dense[:, i, bass.ds(e, 1)], g.h1[:, i, :],
                                                   ALU.mult, ALU.add).then_inc(s["acc"], 1)

            def expert(e, par, prep):
                for n in range(NJ):
                    for f in range(FB):
                        i = n * FB + f
                        dve.wait_ge(s["silu"], 2 + NG * e + i + 1)
                        dve.wait_ge(s["u"], NG * e + i + 1)
                        dve.wait_ge(s["lo"], NG * e + i + 1)
                        nc.vector.tensor_tensor(hm[:, i % 2, :], sg[:, i % 2, :], ps_u[i % 2][:], ALU.mult).then_inc(s["hm"], 1)
                    if n:
                        accumulate(e, n - 1)
                if prep:
                    lower_weights(e + 1, 1 - par)
                accumulate(e, NJ - 1)
            lower_weights(0, 0)
            with dve.Fori(0, LOOP // 2) as pair:
                expert(2 * pair, 0, True)
                expert(2 * pair + 1, 1, True)
            expert(E - 2, 0, True)
            expert(E - 1, 1, False)


class Tiles:
    pass


def layer(nc, a, out):
    g = Tiles()
    g.h0_dram = nc.dram_tensor("h0_scratch", [P, NT * C], F32).ap()
    g.row_dram = nc.dram_tensor("row_scratch", [2, T], F32).ap()
    g.v_dram = nc.dram_tensor("v_scratch", [2, H, P, NT * V1], F32).ap()
    g.ks_dram = nc.dram_tensor("ks_scratch", [H, QA + DQK, P], F32).ap()
    g.o_dram = nc.dram_tensor("o_scratch", [P, NT, H * DV], F32).ap()
    with ExitStack() as ctx:
        tile = lambda n, s, d=F32: ctx.enter_context(nc.sbuf_tensor(n, s, d))
        g.ident, g.ones = tile("ident", [P, P]), tile("ones", [P, P])
        g.ident16, g.mask_qk, g.mask_kq = tile("ident16", [P, P], BF16), tile("mask_qk", [P, P], BF16), tile("mask_kq", [P, P], BF16)
        g.inv, g.rstd, g.imp, g.gates = tile("inv", [P, 1]), tile("rstd", [P, NT]), tile("imp", [P, NT]), tile("gates", [P, 3])
        g.onehot = tile("onehot", [QA, NB])
        g.vs = tile("v_sel", [KEEP, H, V1])
        early = tile("early", [P, NT * (C + NS)])
        g.early = early
        g.U = early[:, 0:NT * C].rearrange("p (t c) -> p t c", c=C)
        g.sm = early[:, NT * C:NT * (C + NS)].rearrange("p (t n) -> p t n", n=NS)
        embed(nc, g, a["x"], a["tok_weight"])
        with ExitStack() as mid:
            tile = lambda n, s, d=F32: mid.enter_context(nc.sbuf_tensor(n, s, d))
            g.uT = tile("uT", [P, KC, T], F32R)
            g.lat_hi, g.lat_lo = tile("lat_hi", [P, T], F32R), tile("lat_lo", [P, T], F32R)
            g.cos, g.sin, g.cos_a, g.sin_a = (tile(n, [DQK, T]) for n in ("cos", "sin", "cos_a", "sin_a"))
            g.k1_hi = [tile(f"k1_hi{i}", [QA, T], F32R) for i in range(2)]
            g.k1_lo = [tile(f"k1_lo{i}", [DQK, T], F32R) for i in range(2)]
            project(nc, g, a)
            select(nc, g, a)
            attend(nc, g, a)
        g.h1 = ctx.enter_context(nc.sbuf_tensor("h1", [P, NT, C], F32))
        g.x_hi = ctx.enter_context(nc.sbuf_tensor("x2T_hi", [P, KC, T], F32R))
        g.x_lo = ctx.enter_context(nc.sbuf_tensor("x2T_lo", [P, KC, T], F32R))
        g.dense = ctx.enter_context(nc.sbuf_tensor("dense_w", [P, NT, E], F32))
        mix(nc, g, a)
        experts(nc, g, a, out)


_NAMES = {
    "x": "x", "L0_tok_weight": "tok_weight", "L0_attn_w_cq": "w_cq", "L0_attn_g_qnorm": "g_qnorm", "L0_attn_w_dq_nope": "w_dq_nope",
    "L0_attn_w_dq_rope": "w_dq_rope", "L0_attn_w_ckv": "w_ckv", "L0_attn_g_kvnorm": "g_kvnorm", "L0_attn_w_dk_nope": "w_dk_nope",
    "L0_attn_w_dv": "w_dv", "L0_attn_w_krope": "w_krope", "L0_attn_w_imp": "w_imp", "L0_attn_w_selk": "w_selk", "L0_attn_w_selv": "w_selv",
    "L0_attn_w_wink": "w_wink", "L0_attn_w_winv": "w_winv", "L0_attn_w_gate": "w_gate", "L0_attn_w_proj": "w_proj",
    "L0_ffn_router_w": "router_w", "L0_ffn_w_gate": "w_gate_e", "L0_ffn_w_up": "w_up", "L0_ffn_w_down": "w_down",
}
_OUTS = [((1, T, C), "float32")]


def rope_tables():
    import numpy as np
    f = (np.float32(1.0) / np.power(np.float32(10000.0), np.arange(0, ROPE, 2, dtype=np.float32) / np.float32(ROPE))).astype(np.float32)
    angle = np.outer(np.arange(T, dtype=np.float32), f).astype(np.float32)
    c, s = np.cos(angle), np.sin(angle)
    return {"cos": np.ascontiguousarray(c.T), "sin": np.ascontiguousarray(s.T), "cos_tok": c[:KEEP].copy(), "sin_tok": s[:KEEP].copy()}


def kernel(**inputs):
    import numpy as _np
    import concourse.bacc as _bacc
    from concourse import mybir as _mybir
    from concourse.bass_utils import run_bass_kernel_spmd as _run

    nc = _bacc.Bacc("TRN2", target_bir_lowering=False, num_devices=1)
    arrays, args = {}, {}
    given = {_NAMES[n]: inputs[n] for n in _NAMES}
    for name, value in {**given, **rope_tables()}.items():
        v = _np.ascontiguousarray(value)
        arrays[f"in_{name}_dram"] = v
        args[name] = nc.dram_tensor(f"in_{name}_dram", v.shape, _mybir.dt.from_np(v.dtype), kind="ExternalInput").ap()
    outs = [nc.dram_tensor(f"out_{i}_dram", shape, _mybir.dt.from_np(_np.dtype(dtype)), kind="ExternalOutput").ap()
            for i, (shape, dtype) in enumerate(_OUTS)]
    with nc.allow_non_contiguous_dma(reason="small index, router and row loads"):
        layer(nc, args, outs[0])
    r = _run(nc, [arrays], core_ids=[0])
    return r.results[0]["out_0_dram"]
```

```python
from contextlib import ExitStack

import concourse.bass as bass
from concourse import mybir

F32 = mybir.dt.float32
F32R = mybir.dt.float32r
BF16 = mybir.dt.bfloat16
I32 = mybir.dt.int32
ALU = mybir.AluOpType
ACT = mybir.ActivationFunctionType
AX = mybir.AxisListType

P = 128
T = 2048
C = 256
NT = T // P
KC = C // P
H = 16
NOPE, ROPE, HALF = 32, 64, 32
DQK = NOPE + ROPE
DV = 32
QL, KVL = 96, 32
KEEP = 64
VOCAB = 32000
SCALE = float(DQK) ** -0.5
MASKED = -1.0e30
CH = 512
NJ = T // CH
WINDOW, SELECT, LATENT = 0, 1, 2
NB = 3
GATE = {LATENT: 0, SELECT: 1, WINDOW: 2}
QA = DQK + NB
E, F = 8, 512
FB = F // P
JITTER = 0.01

CQ0, CKV0, KR0, IMP0, GATE0, NS = 0, QL, QL + KVL, QL + KVL + ROPE, QL + KVL + ROPE + 1, QL + KVL + ROPE + 4


class Count:

    def __init__(self, eng, sem, base=0, after=None):
        self.eng, self.sem, self.base, self.n, self.after = eng, sem, base, 0, after

    def add(self, ins):
        self.n += 1
        return ins.then_inc(self.sem, 1)

    def wait(self):
        self.eng.wait_ge(self.sem, self.base + self.n)
        if self.after is not None:
            self.eng.sem_inc(self.after, 1)


class Signal:

    def __init__(self, sem, per, t0=0, k0=0, prime=None):
        self.sem, self.per, self.t0, self.k0 = sem, per, t0, k0
        self.prime_by = per if prime is None else prime

    def prime(self, eng):
        eng.sem_inc(self.sem, self.prime_by)

    def wait(self, eng, t, k):
        eng.wait_ge(self.sem, self.per * t + (self.prime_by - self.per * self.t0 + k - self.k0 + 1))

    def after(self, ins):
        return ins.then_inc(self.sem, 1)


def embed(nc, g, x, weight):
    ROWS = VOCAB // P
    NCHUNK, BUF = 16, 4
    W = ROWS * C // NCHUNK
    SPLIT = 2200
    wv = weight.rearrange("(p r) c -> p (r c)", p=P)
    with ExitStack() as ctx:
        tile = lambda n, s, d=F32: ctx.enter_context(nc.sbuf_tensor(n, s, d))
        wbuf = tile("wbuf", [P, BUF, W])
        junk = tile("abs_junk", [P, SPLIT], BF16)
        part = tile("abs_part", [P, 2 * NCHUNK])
        tot = tile("abs_tot", [P, 1])
        scale = tile("scale", [P, 4])
        idx = tile("tok_idx", [P, NT], I32)
        rows = tile("tok_rows", [P, NT, C])
        below = tile("below", [P, NT, C])
        h0 = tile("h0_tile", [P, NT, C])
        tsum = tile("tsum", [P, NT])
        usq = tile("usq", [P, C])
        var = tile("var_u", [P, NT])
        inv2 = tile("inv2", [P, 1])
        std = tile("std_u", [P, NT])
        pt = ctx.enter_context(nc.psum_tensor("ps_total", [P, CH], F32))
        s = {k: ctx.enter_context(nc.semaphore("a_" + k)) for k in
             ("idx", "gather", "act", "dve", "pe", "scale", "tern", "sq", "h0", "h0st", "std", "v", "const", "rst")}
        ld = [ctx.enter_context(nc.semaphore(f"a_w{i}")) for i in range(BUF)]
        block = ctx.enter_context(nc.Block())

        @block.sync
        def _(sp):
            for n in range(NCHUNK):
                if n >= BUF:
                    sp.wait_ge(s["act"], n - BUF + 1)
                    sp.wait_ge(s["dve"], n - BUF + 1)
                sp.dma_start(wbuf[:, n % BUF, :], wv[:, n * W:(n + 1) * W]).then_inc(ld[n % BUF], 16)
            sp.wait_ge(s["h0"], 1)
            sp.dma_start(g.h0_dram, h0[:].rearrange("p t c -> p (t c)")).then_inc(s["h0st"], 16)
            sp.wait_ge(s["h0st"], 16)

        @block.gpsimd
        def _(pool):
            pool.dma_start(idx[:], x.rearrange("o (t p) -> p (o t)", p=P)).then_inc(s["idx"], 16)
            cst = Count(pool, s["const"])
            cst.add(nc.gpsimd.memset(g.ones[:], 1.0))
            cst.add(nc.gpsimd.memset(g.ident[:], 0.0))
            cst.wait()
            cst.add(nc.gpsimd.affine_select(out=g.ident[:], in_=g.ident[:], compare_op=ALU.not_equal, fill=1.0,
                                            base=0, pattern=[[-1, P]], channel_multiplier=1))
            cst.wait()
            cst.add(nc.gpsimd.tensor_copy(g.ident16[:], g.ident[:]))
            cst.add(nc.gpsimd.memset(g.mask_qk[:], 0.0))
            cst.add(nc.gpsimd.memset(g.mask_kq[:], 0.0))
            cst.wait()
            cst.add(nc.gpsimd.affine_select(out=g.mask_qk[:], in_=g.mask_qk[:], compare_op=ALU.is_ge, fill=MASKED,
                                            base=0, pattern=[[-1, P]], channel_multiplier=1))
            cst.add(nc.gpsimd.affine_select(out=g.mask_kq[:], in_=g.mask_kq[:], compare_op=ALU.is_ge, fill=MASKED,
                                            base=0, pattern=[[1, P]], channel_multiplier=-1))
            pool.wait_ge(s["idx"], 16)
            for t in range(NT):
                nc.gpsimd.indirect_dma_start(out=rows[:, t, :], out_offset=None, in_=weight,
                                             in_offset=bass.IndirectOffsetOnAxis(ap=idx[:, t:t + 1], axis=0)
                                             ).then_inc(s["gather"], 16)
            cst.wait()

        @block.scalar
        def _(act):
            for n in range(NCHUNK):
                act.wait_ge(ld[n % BUF], 16 * (n // BUF + 1))
                if n:
                    act.wait_ge(s["act"], n)
                nc.scalar.activation(junk[:], wbuf[:, n % BUF, 0:SPLIT], ACT.Abs,
                                     accum_out=part[:, n:n + 1]).then_inc(s["act"], 1)
            act.wait_ge(s["tern"], 1)
            nc.scalar.activation(h0[:].rearrange("p t c -> p (t c)"), rows[:].rearrange("p t c -> p (t c)"),
                                 ACT.Copy, scale=g.inv[:, 0:1]).then_inc(s["h0"], 1)
            act.wait_ge(s["tern"], 2)
            for t in range(NT):
                if t:
                    act.wait_ge(s["sq"], t)
                nc.scalar.activation(usq[:], g.U[:, t, :], ACT.Square, accum_out=var[:, t:t + 1]).then_inc(s["sq"], 1)
            act.wait_ge(s["std"], 1)
            nc.scalar.activation(std[:], var[:], ACT.Sqrt).then_inc(s["rst"], 1)

        @block.tensor
        def _(pe):
            pe.wait_ge(s["const"], 1)
            pe.wait_ge(s["scale"], 1)
            nc.tensor.matmul(pt[:, 0:1], g.ones[:], tot[:], start=True, stop=True).then_inc(s["pe"], 1)

        @block.vector
        def _(dve):
            for n in range(NCHUNK):
                dve.wait_ge(ld[n % BUF], 16 * (n // BUF + 1))
                nc.vector.tensor_reduce(part[:, NCHUNK + n:NCHUNK + n + 1], wbuf[:, n % BUF, SPLIT:W], axis=AX.X,
                                        op=ALU.add, apply_absolute_value=True).then_inc(s["dve"], 1)
            v = Count(dve, s["v"])
            dve.wait_ge(s["act"], NCHUNK)
            dve.wait_ge(s["dve"], NCHUNK)
            nc.vector.tensor_reduce(tot[:], part[:], axis=AX.X, op=ALU.add).then_inc(s["scale"], 1)
            dve.wait_ge(s["pe"], 1)
            v.add(nc.vector.tensor_scalar(scale[:, 0:1], pt[:, 0:1], 1.0 / (VOCAB * C), 1e-5, ALU.mult, ALU.max))
            v.wait()
            v.add(nc.vector.reciprocal(scale[:, 1:2], scale[:, 0:1]))
            v.wait()
            v.add(nc.vector.reciprocal(g.inv[:], scale[:, 1:2]))
            dve.wait_ge(s["gather"], 16 * NT)
            v.add(nc.vector.tensor_scalar(below[:], rows[:], scale[:, 1:2], -0.5, ALU.mult, ALU.is_lt))
            v.wait()
            v.add(nc.vector.tensor_scalar(rows[:], rows[:], scale[:, 1:2], 0.5, ALU.mult, ALU.is_gt))
            v.wait()
            nc.vector.tensor_tensor(rows[:], rows[:], below[:], ALU.subtract).then_inc(s["tern"], 1)
            dve.wait_ge(s["tern"], 1)
            v.add(nc.vector.tensor_reduce(tsum[:], rows[:], axis=AX.X, op=ALU.add))
            v.wait()
            v.add(nc.vector.tensor_scalar(tsum[:], tsum[:], -1.0 / C, None, ALU.mult))
            v.wait()
            nc.vector.tensor_tensor(g.U[:], rows[:], tsum[:].unsqueeze(2).to_broadcast([P, NT, C]),
                                    ALU.add).then_inc(s["tern"], 1)
            v.add(nc.vector.tensor_tensor(inv2[:], g.inv[:], g.inv[:], ALU.mult))
            dve.wait_ge(s["sq"], NT)
            v.wait()
            v.add(nc.vector.tensor_scalar(var[:], var[:], inv2[:, 0:1], 1.0 / C, ALU.mult, ALU.mult))
            v.wait()
            nc.vector.tensor_scalar(var[:], var[:], 1e-5, None, ALU.add).then_inc(s["std"], 1)
            dve.wait_ge(s["rst"], 1)
            v.add(nc.vector.reciprocal(std[:], std[:]))
            v.wait()
            v.add(nc.vector.tensor_scalar(g.rstd[:], std[:], g.inv[:, 0:1], None, ALU.mult))
            v.wait()


def project(nc, g, a):
    with ExitStack() as ctx:
        tile = lambda n, s, d=F32: ctx.enter_context(nc.sbuf_tensor(n, s, d))
        wsm = tile("wsm", [P, KC, NS])
        wsm_hi, wsm_lo = tile("wsm_hi", [P, KC, NS], F32R), tile("wsm_lo", [P, KC, NS], F32R)
        wv = tile("wv", [P, KC, CH])
        wv_hi, wv_lo = tile("wv_hi", [P, KC, CH], F32R), tile("wv_lo", [P, KC, CH], F32R)
        wd = tile("wd", [P, CH])
        wd_hi, wd_lo = tile("wd_hi", [P, CH], F32R), tile("wd_lo", [P, CH], F32R)
        gains = tile("gains", [P, QL + KVL])
        lat = tile("latents", [P, NT, P])
        ss = tile("lat_ss", [P, 2, NT])
        krot = tile("krot", [P, NT, DQK])
        vt = tile("vt", [P, H, NT, DV])
        t1 = tile("kr_t1", [DQK, CH])
        t2 = tile("kr_t2", [DQK, CH])
        full = tile("kr_full", [DQK, CH])
        bank = [ctx.enter_context(nc.psum_tensor(f"b_ps{i}", [P, CH], F32)) for i in range(8)]
        s = {k: ctx.enter_context(nc.semaphore("b_" + k)) for k in
             ("w", "wd", "tab", "gain", "whi", "wlo", "tr", "ut", "sm", "smev", "smev1", "v", "std", "rt", "lat", "lt", "lhi", "llo",
              "kt", "kt1", "full", "khi", "klo", "vps", "vev", "v1ps", "v1ev", "vst", "arst", "arld", "ca", "gt", "rot", "sst", "p")}
        block = ctx.enter_context(nc.Block())

        @block.sync
        def _(sp):
            for lo, w in ((CQ0, a["w_cq"]), (CKV0, a["w_ckv"]), (KR0, a["w_krope"]), (IMP0, a["w_imp"]), (GATE0, a["w_gate"])):
                sp.dma_start(wsm[:, :, lo:lo + w.shape[1]], w.rearrange("(k p) n -> p k n", p=P)).then_inc(s["w"], 16)
            sp.dma_start(wv[:], a["w_winv"].rearrange("(k p) n -> p k n", p=P)).then_inc(s["wd"], 16)
            sp.dma_start(wd[QL:P, :], a["w_dv"]).then_inc(s["wd"], 16)
            sp.dma_start(g.row_dram[0:1, :].rearrange("o (t p) -> p (o t)", p=P), g.rstd[:]).then_inc(s["arst"], 16)
            sp.wait_ge(s["arst"], 16)
            sp.dma_start(g.cos_a[:], g.row_dram[0:1, :].to_broadcast([DQK, T])).then_inc(s["arld"], 16)
            for b, (ev, n) in enumerate((("vev", 16), ("v1ev", 16))):
                sp.wait_ge(s[ev], n)
                sp.dma_start(g.v_dram[(1, 0)[b]].rearrange("h p n -> p h n"),
                             vt[:].rearrange("p h t n -> p h (t n)")).then_inc(s["vst"], 16)
                sp.wait_ge(s["vst"], 16 * (b + 1))
            sp.wait_ge(s["smev"], NT)
            sp.wait_ge(s["smev1"], 1)
            sp.dma_start(g.row_dram[1:2, :].rearrange("o (t p) -> p (o t)", p=P), g.imp[:]).then_inc(s["sst"], 16)
            sp.wait_ge(s["sst"], 16)

        @block.gpsimd
        def _(pool):
            for r in (NOPE, NOPE + HALF):
                pool.dma_start(g.cos[r:r + HALF, :], a["cos"]).then_inc(s["tab"], 16)
                pool.dma_start(g.sin[r:r + HALF, :], a["sin"]).then_inc(s["tab"], 16)
            pool.dma_start(gains[:, 0:QL], a["g_qnorm"].rearrange("(o n) -> o n", o=1).to_broadcast([P, QL])).then_inc(s["gain"], 16)
            pool.dma_start(gains[:, QL:P], a["g_kvnorm"].rearrange("(o n) -> o n", o=1).to_broadcast([P, KVL])).then_inc(s["gain"], 16)
            p = Count(pool, s["p"])
            p.add(nc.gpsimd.memset(g.cos[0:NOPE, :], 1.0))
            p.add(nc.gpsimd.memset(g.sin[0:NOPE, :], 0.0))
            p.add(nc.gpsimd.memset(krot[:, :, 0:NOPE], 0.0))
            pool.wait_ge(s["tab"], 64)
            pool.wait_ge(s["arld"], 16)
            p.wait()
            nc.gpsimd.tensor_tensor(g.sin_a[:], g.sin[:], g.cos_a[:], ALU.mult).then_inc(s["ca"], 1)
            pool.wait_ge(s["ca"], 1)
            nc.gpsimd.tensor_tensor(g.cos_a[:], g.cos[:], g.cos_a[:], ALU.mult).then_inc(s["ca"], 1)
            pool.wait_ge(s["ca"], 2)

        def kr_transposes(pe):
            for j in range(NJ):
                for n, src in ((0, g.sm[:, :, CKV0:CKV0 + DQK]), (1, krot[:])):
                    m = 2 * j + n
                    if m >= 2:
                        pe.wait_ge(s["kt1"], m - 1)
                    for q in range(4):
                        last = nc.tensor.transpose(bank[4 + m % 2][0:DQK, q * P:(q + 1) * P], src[:, 4 * j + q, :], g.ident[:])
                    last.then_inc(s["kt"], 1)

        @block.tensor
        def _(pe):
            for n in range(8):
                kc, j = divmod(n, NJ)
                if n >= 4:
                    pe.wait_ge(s["ut"], n - 3)
                for q in range(4):
                    last = nc.tensor.transpose(bank[n % 4][:, q * P:(q + 1) * P],
                                               g.U[:, 4 * j + q, kc * P:(kc + 1) * P], g.ident[:])
                last.then_inc(s["tr"], 1)
            pe.wait_ge(s["ut"], 8)
            pe.wait_ge(s["whi"], 1)
            pe.wait_ge(s["wlo"], 1)
            for t in range(NT):
                if t >= 2:
                    pe.wait_ge(s["smev"], t - 1)
                for kc in range(KC):
                    for w in (wsm_hi, wsm_lo):
                        last = nc.tensor.matmul(bank[4 + t % 2][:, 0:NS], g.uT[:, kc, t * P:(t + 1) * P], w[:, kc, :],
                                                start=(kc == 0 and w is wsm_hi), stop=(kc == KC - 1 and w is wsm_lo))
                last.then_inc(s["sm"], 1)
            pe.wait_ge(s["whi"], 2)
            pe.wait_ge(s["wlo"], 2)
            for t in range(NT):
                if t >= 4:
                    pe.wait_ge(s["vev"], t - 3)
                for kc in range(KC):
                    for w in (wv_hi, wv_lo):
                        last = nc.tensor.matmul(bank[t % 4][:], g.uT[:, kc, t * P:(t + 1) * P], w[:, kc, :],
                                                start=(kc == 0 and w is wv_hi), stop=(kc == KC - 1 and w is wv_lo))
                last.then_inc(s["vps"], 1)
            pe.wait_ge(s["smev"], NT)
            for t in range(NT):
                last = nc.tensor.matmul(bank[7][:, 0:3], g.ones[:], g.sm[:, t, GATE0:GATE0 + 3], start=(t == 0), stop=(t == NT - 1))
            last.then_inc(s["gt"], 1)
            pe.wait_ge(s["rot"], 2)
            pe.wait_ge(s["p"], 3)
            kr_transposes(pe)
            pe.wait_ge(s["lat"], 1)
            for j in range(NJ):
                if j == 0:
                    pe.wait_ge(s["vev"], NT)
                if j >= 2:
                    pe.wait_ge(s["llo"], j - 1)
                for q in range(4):
                    last = nc.tensor.transpose(bank[j % 2][:, q * P:(q + 1) * P], lat[:, 4 * j + q, :], g.ident[:])
                last.then_inc(s["lt"], 1)
            pe.wait_ge(s["llo"], NJ)
            pe.wait_ge(s["whi"], 3)
            pe.wait_ge(s["wlo"], 3)
            for t in range(NT):
                if t >= 4:
                    pe.wait_ge(s["v1ev"], t - 3)
                for n, (l, w) in enumerate(((g.lat_hi, wd_hi), (g.lat_hi, wd_lo), (g.lat_lo, wd_hi))):
                    last = nc.tensor.matmul(bank[t % 4][:], l[QL:P, t * P:(t + 1) * P], w[QL:P, :], start=(n == 0), stop=(n == 2))
                last.then_inc(s["v1ps"], 1)

        @block.scalar
        def _(act):
            act.wait_ge(s["w"], 80)
            nc.scalar.copy(wsm_hi[:], wsm[:]).then_inc(s["whi"], 1)
            for n in range(0, 8, 2):
                kc, j = divmod(n, NJ)
                act.wait_ge(s["tr"], n + 1)
                if n:
                    act.wait_ge(s["ut"], n)
                nc.scalar.copy(g.uT[:, kc, j * CH:(j + 1) * CH], bank[n % 4][:]).then_inc(s["ut"], 1)
            for t in range(NT):
                act.wait_ge(s["sm"], t + 1)
                nc.scalar.activation(g.sm[:, t, :], bank[4 + t % 2][:, 0:NS], ACT.Copy, scale=g.rstd[:, t:t + 1]).then_inc(s["smev"], 1)
            act.wait_ge(s["wd"], 32)
            nc.scalar.copy(wv_hi[:], wv[:]).then_inc(s["whi"], 1)
            nc.scalar.copy(wd_hi[QL:P, :], wd[QL:P, :]).then_inc(s["whi"], 1)
            for t in range(NT):
                act.wait_ge(s["vps"], t + 1)
                nc.scalar.activation(vt[:, :, t, :], bank[t % 4][:].rearrange("p (h d) -> p h d", h=H), ACT.Copy,
                                     scale=g.rstd[:, t:t + 1]).then_inc(s["vev"], 1)
            act.wait_ge(s["std"], 1)
            nc.scalar.activation(ss[:], ss[:], ACT.Sqrt).then_inc(s["rt"], 1)
            for j in range(NJ):
                act.wait_ge(s["full"], j + 1)
                nc.scalar.copy(g.k1_hi[0:DQK, j * CH:(j + 1) * CH], full[:]).then_inc(s["khi"], 1)
            for j in range(NJ):
                act.wait_ge(s["lt"], j + 1)
                nc.scalar.copy(g.lat_hi[:, j * CH:(j + 1) * CH], bank[j % 2][:]).then_inc(s["lhi"], 1)
            act.wait_ge(s["vst"], 16)
            for t in range(NT):
                act.wait_ge(s["v1ps"], t + 1)
                nc.scalar.copy(vt[:, :, t, :], bank[t % 4][:].rearrange("p (h d) -> p h d", h=H)).then_inc(s["v1ev"], 1)

        @block.vector
        def _(dve):
            v = Count(dve, s["v"])
            for n in range(1, 8, 2):
                kc, j = divmod(n, NJ)
                dve.wait_ge(s["tr"], n + 1)
                dve.wait_ge(s["ut"], n)
                nc.vector.tensor_copy(g.uT[:, kc, j * CH:(j + 1) * CH], bank[n % 4][:]).then_inc(s["ut"], 1)
            dve.wait_ge(s["whi"], 1)
            nc.vector.tensor_tensor(wsm_lo[:], wsm[:], wsm_hi[:].bitcast(F32), ALU.subtract).then_inc(s["wlo"], 1)
            dve.wait_ge(s["whi"], 3)
            nc.vector.tensor_tensor(wv_lo[:], wv[:], wv_hi[:].bitcast(F32), ALU.subtract).then_inc(s["wlo"], 1)
            nc.vector.tensor_tensor(wd_lo[QL:P, :], wd[QL:P, :], wd_hi[QL:P, :].bitcast(F32), ALU.subtract).then_inc(s["wlo"], 1)
            dve.wait_ge(s["smev"], NT)
            nc.vector.tensor_copy(g.imp[:], g.sm[:, :, IMP0]).then_inc(s["smev1"], 1)
            v.add(nc.vector.tensor_scalar(g.sm[:, :, KR0:KR0 + ROPE], g.sm[:, :, KR0:KR0 + ROPE], 1.0 / H, None, ALU.mult))
            v.wait()
            nc.vector.tensor_scalar(krot[:, :, NOPE:NOPE + HALF], g.sm[:, :, KR0 + HALF:KR0 + ROPE], -1.0, None, ALU.mult).then_inc(s["rot"], 1)
            nc.vector.tensor_copy(krot[:, :, NOPE + HALF:DQK], g.sm[:, :, KR0:KR0 + HALF]).then_inc(s["rot"], 1)
            v.add(nc.vector.tensor_tensor(lat[:], g.sm[:, :, 0:P], g.sm[:, :, 0:P], ALU.mult))
            v.wait()
            v.add(nc.vector.tensor_reduce(ss[:, 0, :], lat[:, :, 0:QL], axis=AX.X, op=ALU.add))
            v.add(nc.vector.tensor_reduce(ss[:, 1, :], lat[:, :, QL:P], axis=AX.X, op=ALU.add))
            v.wait()
            v.add(nc.vector.tensor_scalar(ss[:, 0, :], ss[:, 0, :], 1.0 / QL, 1e-6, ALU.mult, ALU.add))
            nc.vector.tensor_scalar(ss[:, 1, :], ss[:, 1, :], 1.0 / KVL, 1e-6, ALU.mult, ALU.add).then_inc(s["std"], 1)
            dve.wait_ge(s["rt"], 1)
            v.add(nc.vector.reciprocal(ss[:], ss[:]))
            v.wait()
            v.add(nc.vector.tensor_tensor(lat[:, :, 0:QL], g.sm[:, :, 0:QL], ss[:, 0, :].unsqueeze(2).to_broadcast([P, NT, QL]), ALU.mult))
            v.add(nc.vector.tensor_tensor(lat[:, :, QL:P], g.sm[:, :, QL:P], ss[:, 1, :].unsqueeze(2).to_broadcast([P, NT, KVL]), ALU.mult))
            dve.wait_ge(s["gain"], 32)
            v.wait()
            nc.vector.tensor_tensor(lat[:], lat[:], gains[:].unsqueeze(1).to_broadcast([P, NT, P]), ALU.mult).then_inc(s["lat"], 1)
            dve.wait_ge(s["gt"], 1)
            v.add(nc.vector.tensor_scalar(g.gates[:], bank[7][:, 0:3], 1.0 / T, None, ALU.mult))
            dve.wait_ge(s["tab"], 64)
            dve.wait_ge(s["p"], 3)
            for j in range(NJ):
                c = slice(j * CH, (j + 1) * CH)
                dve.wait_ge(s["kt"], 2 * j + 1)
                nc.vector.tensor_tensor(t1[:], bank[4][0:DQK, :], g.cos[:, c], ALU.mult).then_inc(s["kt1"], 1)
                dve.wait_ge(s["kt"], 2 * j + 2)
                nc.vector.tensor_tensor(t2[:], bank[5][0:DQK, :], g.sin[:, c], ALU.mult).then_inc(s["kt1"], 1)
                dve.wait_ge(s["kt1"], 2 * j + 2)
                if j:
                    dve.wait_ge(s["klo"], j)
                nc.vector.tensor_tensor(full[:], t1[:], t2[:], ALU.add).then_inc(s["full"], 1)
                dve.wait_ge(s["khi"], j + 1)
                dve.wait_ge(s["full"], j + 1)
                nc.vector.tensor_tensor(g.k1_lo[:, c], full[:], g.k1_hi[0:DQK, c].bitcast(F32), ALU.subtract).then_inc(s["klo"], 1)
            for j in range(NJ):
                dve.wait_ge(s["lhi"], j + 1)
                nc.vector.tensor_tensor(g.lat_lo[:, j * CH:(j + 1) * CH], bank[j % 2][:], g.lat_hi[:, j * CH:(j + 1) * CH].bitcast(F32),
                                        ALU.subtract).then_inc(s["llo"], 1)
            v.wait()


def select(nc, g, a):
    with ExitStack() as ctx:
        tile = lambda n, s, d=F32: ctx.enter_context(nc.sbuf_tensor(n, s, d))
        srow = tile("score_row", [P, T])
        junk = tile("rank_junk", [P, T], BF16)
        before = tile("before", [P, T], BF16)
        strict = tile("strict", [P, P])
        ranks = tile("ranks", [P, 2, NT])
        flag = tile("flag", [P, NT])
        run = tile("flag_run", [P, NT])
        zero = tile("zero16", [P, NT])
        pos = tile("pos", [P, NT])
        slots = tile("slots", [P, KEEP])
        hot = tile("hot", [P, NT, KEEP])
        frs = tile("flag_rstd", [P, NT])
        selT = tile("selT", [P, KC, KEEP])
        wk = tile("wselk", [P, KC, H * DQK])
        wv = tile("wselv", [P, KC, H * DV])
        ktm = tile("ks_tok", [KEEP, H, DQK])
        krt = tile("ks_rot", [KEEP, H, DQK])
        kt1, kt2 = tile("ks_t1", [KEEP, H, HALF]), tile("ks_t2", [KEEP, H, HALF])
        kt3, kt4 = tile("ks_t3", [KEEP, H, HALF]), tile("ks_t4", [KEEP, H, HALF])
        ck, sk = tile("ck", [KEEP, HALF]), tile("sk", [KEEP, HALF])
        khi = tile("ks_hi_all", [QA, H, P], F32R)
        klo = tile("ks_lo_all", [DQK, H, P], F32R)
        gm = tile("gate_tmp", [P, 8])
        bank = [ctx.enter_context(nc.psum_tensor(f"s_ps{i}", [P, CH], F32)) for i in range(8)]
        s = {k: ctx.enter_context(nc.semaphore("s_" + k)) for k in
             ("row", "w", "t", "p", "v", "flag", "run", "pos", "hot", "sel", "selc", "ks", "rope", "kt", "khi", "klo", "vsc", "st", "ge", "gx", "c1")}
        block = ctx.enter_context(nc.Block())

        @block.sync
        def _(sp):
            sp.dma_start(srow[:], g.row_dram[1:2, :].to_broadcast([P, T])).then_inc(s["row"], 16)
            sp.dma_start(wk[:], a["w_selk"].rearrange("(k p) n -> p k n", p=P)).then_inc(s["w"], 16)
            sp.dma_start(wv[:], a["w_selv"].rearrange("(k p) n -> p k n", p=P)).then_inc(s["w"], 16)
            sp.dma_start(ck[:], a["cos_tok"]).then_inc(s["t"], 16)
            sp.dma_start(sk[:], a["sin_tok"]).then_inc(s["t"], 16)
            sp.wait_ge(s["khi"], 2)
            sp.wait_ge(s["c1"], 6)
            sp.dma_start(g.ks_dram[:, 0:QA, :].rearrange("h r k -> r h k"), khi[:].bitcast(F32)).then_inc(s["st"], 16)
            sp.wait_ge(s["klo"], 2)
            sp.dma_start(g.ks_dram[:, QA:QA + DQK, :].rearrange("h r k -> r h k"), klo[:].bitcast(F32)).then_inc(s["st"], 16)
            sp.wait_ge(s["st"], 32)

        @block.gpsimd
        def _(pool):
            p = Count(pool, s["p"])
            p.add(nc.gpsimd.memset(before[:], 1.0))
            p.add(nc.gpsimd.memset(strict[:], 1.0))
            p.add(nc.gpsimd.memset(zero[:], 0.0))
            p.add(nc.gpsimd.iota(slots[:], pattern=[[1, KEEP]], base=0, channel_multiplier=0, allow_small_or_imprecise_dtypes=True))
            p.wait()
            p.add(nc.gpsimd.affine_select(out=before[:], in_=before[:], compare_op=ALU.is_gt, fill=0.0,
                                          base=T - P, pattern=[[-1, T]], channel_multiplier=1))
            p.add(nc.gpsimd.affine_select(out=strict[:], in_=strict[:], compare_op=ALU.is_gt, fill=0.0,
                                          base=0, pattern=[[1, P]], channel_multiplier=-1))
            c1 = Count(pool, s["c1"])
            c1.add(nc.gpsimd.memset(khi[:].bitcast(F32), 0.0))
            c1.add(nc.gpsimd.memset(klo[:].bitcast(F32), 0.0))
            c1.wait()
            c1.add(nc.gpsimd.memset(g.onehot[DQK:QA, :], 0.0))
            c1.wait()
            c1.add(nc.gpsimd.affine_select(out=g.onehot[DQK:QA, :], in_=g.onehot[DQK:QA, :], compare_op=ALU.not_equal, fill=1.0,
                                           base=0, pattern=[[-1, NB]], channel_multiplier=1))
            c1.wait()
            c1.add(nc.gpsimd.tensor_copy(g.k1_hi[DQK:QA, :], g.onehot[DQK:QA, LATENT:LATENT + 1].to_broadcast([NB, T])))
            c1.add(nc.gpsimd.tensor_copy(khi[DQK:QA, :, :].rearrange("r h k -> r (h k)"),
                                         g.onehot[DQK:QA, SELECT:SELECT + 1].to_broadcast([NB, H * P])))
            c1.wait()
            p.wait()

        @block.tensor
        def _(pe):
            pe.wait_ge(s["p"], 6)
            pe.wait_ge(s["flag"], 1)
            nc.tensor.matmul(bank[0][:, 0:NT], strict[:], flag[:], start=True, stop=False)
            pe.wait_ge(s["run"], 1)
            nc.tensor.matmul(bank[0][:, 0:NT], g.ones[:], run[:], start=False, stop=True).then_inc(s["pos"], 1)
            pe.wait_ge(s["hot"], 1)
            for kc in range(KC):
                for t in range(NT):
                    last = nc.tensor.matmul(bank[1 + kc][:, 0:KEEP], g.U[:, t, kc * P:(kc + 1) * P], hot[:, t, :], start=(t == 0), stop=(t == NT - 1))
            last.then_inc(s["sel"], 1)
            pe.wait_ge(s["selc"], 1)
            pe.wait_ge(s["w"], 32)
            for n in range(4):
                for kc in range(KC):
                    w = wk[:, kc, n * CH:(n + 1) * CH] if n < 3 else wv[:, kc, :]
                    last = nc.tensor.matmul(bank[3 + n][0:KEEP, :], selT[:, kc, :], w, start=(kc == 0), stop=(kc == KC - 1))
                last.then_inc(s["ks"], 1)
            pe.wait_ge(s["rope"], 1)
            for h in range(H):
                last = nc.tensor.transpose(bank[h // 8][0:DQK, (h % 8) * KEEP:(h % 8 + 1) * KEEP], krt[:, h, :], g.ident[0:KEEP, 0:KEEP])
            last.then_inc(s["kt"], 1)

        @block.scalar
        def _(act):
            act.wait_ge(s["ge"], 1)
            nc.scalar.activation(gm[:, 2:5], g.gates[:], ACT.Exp, bias=gm[:, 0:1], accum_out=gm[:, 1:2]).then_inc(s["gx"], 1)
            act.wait_ge(s["ks"], 4)
            nc.scalar.copy(g.vs[:], bank[6][0:KEEP, :].rearrange("p (h d) -> p h d", h=H)).then_inc(s["vsc"], 1)
            act.wait_ge(s["kt"], 1)
            act.wait_ge(s["c1"], 2)
            for n in range(2):
                nc.scalar.copy(khi[0:DQK, 8 * n:8 * n + 8, 0:KEEP], bank[n][0:DQK, :].rearrange("p (h k) -> p h k", h=8)).then_inc(s["khi"], 1)
            act.wait_ge(s["vsc"], 1)

        @block.vector
        def _(dve):
            v = Count(dve, s["v"])
            v.add(nc.vector.tensor_reduce(gm[:, 0:1], g.gates[:], axis=AX.X, op=ALU.max))
            v.wait()
            nc.vector.tensor_scalar(gm[:, 0:1], gm[:, 0:1], -1.0, None, ALU.mult).then_inc(s["ge"], 1)
            dve.wait_ge(s["row"], 16)
            dve.wait_ge(s["p"], 6)
            for t in range(NT):
                sc = g.imp[:, t:t + 1]
                v.wait()
                v.add(nc.vector.tensor_scalar(junk[:], srow[:], sc, None, ALU.is_gt, ALU.add, accum_out=ranks[:, 0, t:t + 1]))
                n = (t + 1) * P
                v.wait()
                v.add(nc.vector.scalar_tensor_tensor(junk[:, 0:n], srow[:, 0:n], sc, before[:, T - n:T], ALU.is_equal, ALU.mult,
                                                     accum_out=ranks[:, 1, t:t + 1]))
            v.wait()
            v.add(nc.vector.tensor_tensor(flag[:], ranks[:, 0, :], ranks[:, 1, :], ALU.add))
            v.wait()
            nc.vector.tensor_scalar(flag[:], flag[:], float(KEEP), None, ALU.is_lt).then_inc(s["flag"], 1)
            dve.wait_ge(s["flag"], 1)
            v.add(nc.vector.tensor_tensor_scan(run[:], flag[:], zero[:], 0.0, ALU.add, ALU.add))
            v.wait()
            nc.vector.tensor_tensor(run[:], run[:], flag[:], ALU.subtract).then_inc(s["run"], 1)
            dve.wait_ge(s["gx"], 1)
            v.add(nc.vector.reciprocal(gm[:, 5:6], gm[:, 1:2]))
            v.wait()
            v.add(nc.vector.tensor_scalar(g.gates[:], gm[:, 2:5], gm[:, 5:6], None, ALU.mult))
            dve.wait_ge(s["pos"], 1)
            v.add(nc.vector.tensor_copy(pos[:], bank[0][:, 0:NT]))
            v.add(nc.vector.tensor_tensor(frs[:], flag[:], g.rstd[:], ALU.mult))
            v.wait()
            for t in range(NT):
                ins = nc.vector.tensor_scalar(hot[:, t, :], slots[:], pos[:, t:t + 1], frs[:, t:t + 1], ALU.is_equal, ALU.mult)
            ins.then_inc(s["hot"], 1)
            dve.wait_ge(s["sel"], 1)
            v.add(nc.vector.tensor_copy(selT[:, 0, :], bank[1][:, 0:KEEP]))
            nc.vector.tensor_copy(selT[:, 1, :], bank[2][:, 0:KEEP]).then_inc(s["selc"], 1)
            dve.wait_ge(s["ks"], 3)
            for n in range(3):
                v.add(nc.vector.tensor_copy(ktm[:].rearrange("p h d -> p (h d)")[:, n * CH:(n + 1) * CH], bank[3 + n][0:KEEP, :]))
            v.wait()
            dve.wait_ge(s["t"], 32)
            x1, x2 = ktm[:, :, NOPE:NOPE + HALF], ktm[:, :, NOPE + HALF:DQK]
            cb = ck[:].unsqueeze(1).to_broadcast([KEEP, H, HALF])
            sbc = sk[:].unsqueeze(1).to_broadcast([KEEP, H, HALF])
            v.add(nc.vector.tensor_tensor(kt1[:], x1, cb, ALU.mult))
            v.add(nc.vector.tensor_tensor(kt2[:], x2, sbc, ALU.mult))
            v.add(nc.vector.tensor_tensor(kt3[:], x1, sbc, ALU.mult))
            v.add(nc.vector.tensor_tensor(kt4[:], x2, cb, ALU.mult))
            v.add(nc.vector.tensor_copy(krt[:, :, 0:NOPE], ktm[:, :, 0:NOPE]))
            v.wait()
            v.add(nc.vector.tensor_tensor(krt[:, :, NOPE:NOPE + HALF], kt1[:], kt2[:], ALU.subtract))
            nc.vector.tensor_tensor(krt[:, :, NOPE + HALF:DQK], kt3[:], kt4[:], ALU.add).then_inc(s["rope"], 1)
            for n in range(2):
                dve.wait_ge(s["khi"], n + 1)
                nc.vector.tensor_tensor(klo[:, 8 * n:8 * n + 8, 0:KEEP], bank[n][0:DQK, :].rearrange("p (h k) -> p h k", h=8),
                                        khi[0:DQK, 8 * n:8 * n + 8, 0:KEEP].bitcast(F32), ALU.subtract).then_inc(s["klo"], 1)
            v.wait()


def units():
    out = []
    for b in (WINDOW, LATENT):
        out += [(b, j, k) for j in range(NJ) for k in range(4 * j + 4)]
    return out + [(SELECT, j, 0) for j in range(NJ)]


UNITS = units()
NU = len(UNITS)
HU = NU // 2 - 2


def side_tasks():
    proj = lambda what: [(what, j, rot) for j in range(NJ) for rot in (0, 1)]
    mx = lambda b: [("max", b, q, c) for q in range(NT) for c in range(q // 4 + 1)]
    at = {}

    def spread(tasks, lo, hi):
        for n, t in enumerate(tasks):
            at.setdefault(lo + n * (hi - lo) // len(tasks), []).append(t)
    spread([("k1", j) for j in range(NJ)] + mx(LATENT) + [("neg", 0)], 0, 32)
    spread([("v", LATENT)], 12, 13)
    spread(proj("q"), 32, 40)
    spread(proj("kw") + [("max", SELECT, n, 0) for n in range(2)] + [("v", WINDOW)], 40, 50)
    spread(mx(WINDOW), 50, 78)
    spread([("neg", 1), ("v", SELECT)], 78, 79)
    return at


SIDE = side_tasks()
ALL_SIDE = [t for i in sorted(SIDE) for t in SIDE[i]]
OWN = [t for t in ALL_SIDE if t[0] == "k1" or t in (("v", LATENT), ("v", SELECT), ("neg", 0)) or t[:2] == ("max", LATENT)]
PJ = {t: n for n, t in enumerate(t for t in ALL_SIDE if t[0] not in ("max", "v"))}
MX = {t: n for n, t in enumerate(t for t in ALL_SIDE if t[0] == "max")}
PJ_OWN = sum(t in OWN for t in PJ)
MX_OWN = sum(t in OWN for t in MX)
ROPED = [(w, j) for w in ("q", "kw") for j in range(NJ)]
LO_DVE = [i for i in range(NU) if i % 4 == 3]
LO_POOL = [i for i in range(NU) if i not in LO_DVE]
PV_LAG = 4
OUT_LAG = PV_LAG + 1
SLOTS, LSLOTS = 6, 4
NPROB = 3


def attend(nc, g, a):
    with ExitStack() as ctx:
        tile = lambda n, s, d=F32: ctx.enter_context(nc.sbuf_tensor(n, s, d))
        q_hi = [tile(f"q_hi{i}", [QA, T], F32R) for i in range(2)]
        q_lo = [tile(f"q_lo{i}", [DQK, T], F32R) for i in range(2)]
        kw_hi, kw_lo = tile("kw_hi", [QA, T], F32R), tile("kw_lo", [DQK, T], F32R)
        ks_hi = [tile(f"ks_hi{i}", [QA, P], F32R) for i in range(2)]
        ks_lo = [tile(f"ks_lo{i}", [DQK, P], F32R) for i in range(2)]
        vals = {WINDOW: tile("v_win", [P, NT, P], F32R), LATENT: tile("v_lat", [P, NT, P], F32R), SELECT: tile("v_one", [KEEP, 1, P], F32R)}
        p_hi, p_lo = tile("p_hi", [P, SLOTS, CH], F32R), tile("p_lo", [P, LSLOTS, CH], F32R)
        ot = tile("o_sum", [P, CH])
        part = lambda lo, n: g.early[:, lo:lo + n * CH].rearrange("p (n c) -> p n c", c=CH)
        prob = part(0, NPROB)
        t1, t2, full = (part((NPROB + n) * CH, 2)[0:DQK] for n in (0, 2, 4))
        raw_o, sums = part((NPROB + 6) * CH, 2), part((NPROB + 8) * CH, 2)
        v_raw = part((NPROB + 10) * CH, 1)[:, 0, :].rearrange("p (t d) -> p t d", d=DV)
        mpart = tile("max_part", [P, NT, NJ])
        nm = tile("neg_max", [P, 2 * NT])
        nm_t = tile("neg_max_t", [2 * NT, P], F32R)
        raw_qk = tile("raw_qk", [P, DQK])
        raw_q, raw_k1 = raw_qk[0:QL, :], raw_qk[:, 0:NOPE]
        raw_kw = tile("raw_kw", [P, KC, DQK])
        wqk = [tile(f"wqk_{n}", [P, 2, DQK], F32R) for n in ("hi", "lo")]
        wq, wk1 = [w[0:QL] for w in wqk], [w[:, 0, :] for w in wqk]
        wkw = [tile(f"wkw_{n}", [P, KC, 2, DQK], F32R) for n in ("hi", "lo")]
        ps_s = [ctx.enter_context(nc.psum_tensor(f"ps_s{i}", [P, CH], F32)) for i in range(3)]
        ps_o = [ctx.enter_context(nc.psum_tensor(f"ps_o{i}", [P, CH], F32)) for i in range(2)]
        ps_m = [ctx.enter_context(nc.psum_tensor(f"ps_m{i}", [P, CH], F32)) for i in range(2)]
        ps_p = ctx.enter_context(nc.psum_tensor("ps_p", [P, CH], F32))
        sem = lambda n: ctx.enter_context(nc.semaphore("h_" + n))
        scores = Signal(sem("scores"), NU)
        p_full = Signal(sem("p_full"), NU)
        p_up = Signal(sem("p_up"), NU)
        lo_pool = Signal(sem("lo_pool"), len(LO_POOL))
        lo_dve = Signal(sem("lo_dve"), len(LO_DVE))
        pv = Signal(sem("pv"), NU)
        o_read = Signal(sem("o_read"), 12)
        s_read = Signal(sem("s_read"), 12)
        lower_read = Signal(sem("lower_read"), 12)
        inv = Signal(sem("inv"), 3)
        norm = Signal(sem("norm"), 3)
        done = Signal(sem("done"), 3)
        v_split = {b: Signal(sem(f"v_split{b}"), 1, t0=(-1 if b == WINDOW else 0)) for b in (WINDOW, LATENT, SELECT)}
        v_up = {b: Signal(sem(f"v_up{b}"), 1, t0=(-1 if b == WINDOW else 0)) for b in (WINDOW, LATENT, SELECT)}
        k1c, k1 = Signal(sem("k1_hi"), NJ), Signal(sem("k1"), NJ)
        pj = Signal(sem("pj"), len(PJ), -1, PJ_OWN, PJ_OWN)
        pj_read = Signal(sem("pj_read"), len(PJ), -1, PJ_OWN, PJ_OWN)
        mx = Signal(sem("mx"), len(MX), -1, MX_OWN, MX_OWN)
        mx_read = Signal(sem("mx_read"), len(MX), -1, MX_OWN, MX_OWN)
        roped = Signal(sem("roped"), 8, -1)
        r_full = Signal(sem("r_full"), 8, -1)
        r_up = Signal(sem("r_up"), 8, -1)
        r_lo = Signal(sem("r_lo"), 8, -1)
        nmax = Signal(sem("nmax"), 2, -1, 1)
        nmax_t = Signal(sem("nmax_t"), 2, -1, 1)
        built = Signal(sem("built"), 1, -1)
        s = {k: sem(k) for k in ("rows_w", "rows_l", "raw", "v_w", "v_l", "ks", "store", "wb", "wz", "mz", "kwz", "ones", "passed", "pe_passed", "dve_passed", "sp_passed")}
        block = ctx.enter_context(nc.Block())
        k_hi = {LATENT: [g.k1_hi] * 2, WINDOW: [kw_hi] * 2, SELECT: ks_hi}
        k_lo = {LATENT: [g.k1_lo] * 2, WINDOW: [kw_lo] * 2, SELECT: ks_lo}
        ORDER = (WINDOW, LATENT, SELECT)

        def heads(eng, head):
            head(0, 0, False, True)
            with eng.Fori(0, H // 2 - 1) as pair:
                head(2 * pair + 1, 1, True, True)
                head(2 * pair + 2, 0, True, True)
            head(H - 1, 1, True, False)

        def lagged(h, par, i, lag, prev):
            if i >= lag:
                return h, par, i - lag
            return (h - 1, 1 - par, i - lag + NU) if prev else None

        def side(i, nxt):
            return [t for t in SIDE.get(i, ()) if nxt or t in OWN]

        def width(i):
            b, j, k = UNITS[i]
            return (max(0, k - 4 * j) * P if b != SELECT else 0), (KEEP if b == SELECT else P)

        def lower_done(eng, h, i):
            i, back = (i, 0) if i >= 0 else (i + NU, 1)
            if i in LO_DVE:
                lo_dve.wait(eng, h, LO_DVE.index(i) - back * len(LO_DVE))
            else:
                lo_pool.wait(eng, h, LO_POOL.index(i) - back * len(LO_POOL))

        def load_raw(sp, h):
            sp.dma_start(raw_q[:, 0:NOPE], a["w_dq_nope"][:, bass.ds(h * NOPE, NOPE)]).then_inc(s["raw"], 16)
            sp.dma_start(raw_q[:, NOPE:DQK], a["w_dq_rope"][:, bass.ds(h * ROPE, ROPE)]).then_inc(s["raw"], 16)
            sp.dma_start(raw_k1[QL:P, :], a["w_dk_nope"][:, bass.ds(h * NOPE, NOPE)]).then_inc(s["raw"], 16)
            sp.dma_start(raw_kw[:], a["w_wink"].rearrange("(k p) n -> p k n", p=P)[:, :, bass.ds(h * DQK, DQK)]).then_inc(s["raw"], 16)

        def load_v(sp, h, b):
            sp.dma_start(v_raw.rearrange("p t d -> p (t d)"), g.v_dram[0 if b == LATENT else 1, bass.ds(h, 1)].rearrange("o p n -> (o p) n")
                         ).then_inc(s["v_l" if b == LATENT else "v_w"], 16)

        def load_ks(sp, h, par):
            sp.dma_start(ks_hi[par][:].bitcast(F32), g.ks_dram[bass.ds(h, 1), 0:QA, :].rearrange("o r k -> (o r) k")).then_inc(s["ks"], 16)
            sp.dma_start(ks_lo[par][:].bitcast(F32), g.ks_dram[bass.ds(h, 1), QA:QA + DQK, :].rearrange("o r k -> (o r) k")).then_inc(s["ks"], 16)

        def store_rows(sp, t, n, par):
            nmax_t.wait(sp, t, n)
            sp.sem_inc(s["sp_passed"], 1)
            for r, b in enumerate((LATENT,) if n == 0 else (WINDOW, SELECT)):
                sp.dma_start(q_hi[par][DQK + b:DQK + b + 1, :].bitcast(F32).rearrange("o (t q) -> o t q", q=P),
                             nm_t[r * NT:(r + 1) * NT, :].bitcast(F32)).then_inc(s["rows_l" if n == 0 else "rows_w"], 16)

        @block.sync
        def _(sp):
            sp.sem_inc(s["store"], 16)
            load_raw(sp, 0)
            load_v(sp, 0, WINDOW)
            load_ks(sp, 0, 0)
            v_split[WINDOW].wait(sp, -1, 0)
            load_v(sp, 0, LATENT)
            store_rows(sp, -1, 1, 0)

            def store(h):
                done.wait(sp, h, 2)
                sp.sem_inc(s["sp_passed"], 1)
                sp.dma_start(g.o_dram[bass.ds(h, 1)].rearrange("o r q -> (o r) q"), ot[:]).then_inc(s["store"], 16)

            def head(h, par, prev, nxt):
                if nxt:
                    built.wait(sp, h - 1, 0)
                    sp.sem_inc(s["sp_passed"], 1)
                    load_raw(sp, h + 1)
                if prev:
                    store(h - 1)
                if nxt:
                    pv.wait(sp, h, -1)
                    sp.sem_inc(s["sp_passed"], 1)
                    load_ks(sp, h + 1, 1 - par)
                    v_split[LATENT].wait(sp, h, 0)
                    sp.sem_inc(s["sp_passed"], 1)
                    load_v(sp, h + 1, WINDOW)
                store_rows(sp, h, 0, par)
                if nxt:
                    v_split[WINDOW].wait(sp, h, 0)
                    sp.sem_inc(s["sp_passed"], 1)
                    load_v(sp, h + 1, LATENT)
                    store_rows(sp, h, 1, 1 - par)
            heads(sp, head)
            store(H - 1)
            sp.wait_ge(s["store"], 16 + 16 * H)

        NWB = 14

        def build_weights(pool, t):
            w = Count(pool, s["wb"], NWB * (t + 1), after=s["passed"])
            pool.wait_ge(s["raw"], 64 * (t + 2))
            if not isinstance(t, int) or t >= 0:
                pj.wait(pool, t, PJ[("k1", NJ - 1)])
            pool.sem_inc(s["passed"], 1)
            w.add(nc.gpsimd.tensor_copy(wq[0][:, 0, :], raw_q[:]))
            w.add(nc.gpsimd.tensor_copy(wkw[0][:, :, 0, :], raw_kw[:]))
            w.wait()
            w.add(nc.gpsimd.tensor_copy(wk1[0][QL:P, 0:NOPE], raw_k1[QL:P, :]))
            w.wait()
            w.add(nc.gpsimd.tensor_tensor(wq[1][:, 0, :], raw_q[:], wq[0][:, 0, :].bitcast(F32), ALU.subtract))
            w.add(nc.gpsimd.tensor_tensor(wkw[1][:, :, 0, :], raw_kw[:], wkw[0][:, :, 0, :].bitcast(F32), ALU.subtract))
            w.wait()
            w.add(nc.gpsimd.tensor_tensor(wk1[1][QL:P, 0:NOPE], raw_k1[QL:P, :], wk1[0][QL:P, 0:NOPE].bitcast(F32), ALU.subtract))
            w.wait()
            x1, x2 = slice(NOPE, NOPE + HALF), slice(NOPE + HALF, DQK)
            for t_ in wq:
                w.add(nc.gpsimd.tensor_scalar(t_[:, 1, x1], t_[:, 0, x2].bitcast(F32), -1.0, None, ALU.mult))
                w.add(nc.gpsimd.tensor_copy(t_[:, 1, x2], t_[:, 0, x1].bitcast(F32)))
            for t_ in wkw:
                w.add(nc.gpsimd.tensor_scalar(t_[:, :, 1, x1], t_[:, :, 0, x2].bitcast(F32), -1.0, None, ALU.mult))
                w.add(nc.gpsimd.tensor_copy(t_[:, :, 1, x2], t_[:, :, 0, x1].bitcast(F32)))
            w.wait()
            assert w.n == NWB, w.n
            pool.sem_inc(built.sem, 1)

        def dst(what, par):
            return (q_hi[par], q_lo[par]) if what == "q" else (kw_hi, kw_lo)

        def rope_number(task):
            return ROPED.index(task[:2]) if task[0] in ("q", "kw") and task[2] == 1 else None

        def rope_sum(pool, task, t, par):
            n = rope_number(task)
            if n is not None:
                roped.wait(pool, t, n)
                r_lo.wait(pool, t, n - 2)
                r_full.after(nc.gpsimd.tensor_tensor(full[:, n % 2, :], t1[:, n % 2, :], t2[:, n % 2, :], ALU.add))

        def rope_rest(pool, task, t, par):
            n = rope_number(task)
            if n is not None:
                hi, lo = dst(task[0], par)
                c = slice(task[1] * CH, (task[1] + 1) * CH)
                r_up.wait(pool, t, n)
                r_lo.after(nc.gpsimd.tensor_tensor(lo[0:DQK, c], full[:, n % 2, :], hi[0:DQK, c].bitcast(F32), ALU.subtract))

        def lower(eng, h, i, own):
            c, rows = width(i)
            p_up.wait(eng, h, i)
            pv.wait(eng, h, i - LSLOTS)
            ns = nc.gpsimd if own is lo_pool else nc.vector
            own.after(ns.tensor_tensor(p_lo[0:rows, i % LSLOTS, c:CH], prob[0:rows, i % NPROB, c:CH],
                                       p_hi[0:rows, i % SLOTS, c:CH].bitcast(F32), ALU.subtract))

        def output_of(i):
            b, j, k = UNITS[i]
            return (4 * ORDER.index(b) + j, j, b) if b == SELECT or k == 4 * j + 3 else None

        @block.gpsimd
        def _(pool):
            for sg in (lo_pool, r_full, r_lo, built):
                sg.prime(pool)
            for t in wq + wkw:
                nc.gpsimd.memset(t[:].bitcast(F32), 0.0).then_inc(s["wz"], 1)
            nc.gpsimd.memset(mpart[:], -3.0e38).then_inc(s["mz"], 1)
            for b in ORDER:
                nc.gpsimd.memset(vals[b][:, :, 2 * DV:P].bitcast(F32), 1.0).then_inc(s["ones"], 1)
            pool.wait_ge(s["wz"], 4)
            pool.wait_ge(s["mz"], 1)
            pool.wait_ge(s["ones"], 3)
            for t in wk1:
                nc.gpsimd.memset(t[QL:P, :].bitcast(F32), 0.0).then_inc(s["wz"], 1)
            nc.gpsimd.tensor_copy(kw_hi[DQK:QA, :], g.onehot[DQK:QA, WINDOW:WINDOW + 1].to_broadcast([NB, T])).then_inc(s["kwz"], 1)
            pool.wait_ge(s["wz"], 6)
            pool.wait_ge(s["kwz"], 1)
            build_weights(pool, -1)
            tasks = [t for t in ALL_SIDE if rope_number(t) is not None]
            for n, t in enumerate(tasks):
                rope_sum(pool, t, -1, 0)
                if n:
                    rope_rest(pool, tasks[n - 1], -1, 0)
            rope_rest(pool, tasks[-1], -1, 0)

            def head(h, par, prev, nxt):
                for i in range(NU + 3 if nxt else NU):
                    if nxt:
                        for t in SIDE.get(i - 1, ()):
                            rope_sum(pool, t, h, 1 - par)
                    if i in LO_POOL:
                        lower(pool, h, i, lo_pool)
                    if nxt:
                        for t in SIDE.get(i - 3, ()):
                            rope_rest(pool, t, h, 1 - par)
                    if nxt and i == 12:
                        build_weights(pool, h)
            heads(pool, head)

        def round_up(act, task, t, par):
            n = rope_number(task)
            if n is not None:
                r_full.wait(act, t, n)
                r_up.after(nc.scalar.copy(dst(task[0], par)[0][0:DQK, task[1] * CH:(task[1] + 1) * CH], full[:, n % 2, :]))

        @block.scalar
        def _(act):
            for sg in (p_full, p_up, r_up, s_read, lower_read):
                sg.prime(act)
            for t in ALL_SIDE:
                round_up(act, t, -1, 0)

            def read_sums(h, par, i):
                out = output_of(i)
                if out:
                    n, j, b = out
                    slot = (par + n // NJ) % 2
                    pv.wait(act, h, i)
                    done.wait(act, h, n // NJ - 2)
                    lower_read.after(nc.scalar.copy(raw_o[j * DV:(j + 1) * DV, slot, :], ps_o[n % 2][DV:2 * DV, :]))
                    s_read.after(nc.scalar.copy(sums[j * DV:(j + 1) * DV, slot, :], ps_o[n % 2][2 * DV:3 * DV, :]))

            def head(h, par, prev, nxt):
                for i in range(NU):
                    c, rows = width(i)
                    scores.wait(act, h, i)
                    lower_done(act, h, i - NPROB)
                    p_full.after(nc.scalar.activation(prob[0:rows, i % NPROB, c:CH], ps_s[i % 3][0:rows, c:CH], ACT.Exp, scale=SCALE))
                    pv.wait(act, h, i - SLOTS)
                    p_up.after(nc.scalar.activation(p_hi[0:rows, i % SLOTS, c:CH], ps_s[i % 3][0:rows, c:CH], ACT.Exp, scale=SCALE))
                    if nxt:
                        for t in SIDE.get(i - 2, ()):
                            round_up(act, t, h, 1 - par)
                    back = lagged(h, par, i, OUT_LAG, prev)
                    if back:
                        read_sums(*back)
            heads(act, head)
            for i in range(NU - OUT_LAG, NU):
                read_sums(H - 1, 1, i)

        def three(out, hi, lo, xhi, xlo, mid=None, rows=None):
            nc.tensor.matmul(out, hi, xhi, start=True, stop=False)
            if mid:
                mid()
            nc.tensor.matmul(out, hi[0:rows] if rows else hi, xlo, start=False, stop=False)
            return nc.tensor.matmul(out, lo, xhi[0:rows] if rows else xhi, start=False, stop=True)

        FIRST_MX = {}
        for t in MX:
            FIRST_MX.setdefault(t[1], t)

        def pe_task(pe, task, t, par):
            if task[0] == "v":
                return
            if task[0] == "max":
                _, b, q, c = task
                n = MX[task]
                if task == FIRST_MX[b]:
                    if b == LATENT:
                        k1.wait(pe, t, 3)
                    else:
                        r_up.wait(pe, t, 7 if b == WINDOW else 3)
                    if b == SELECT:
                        pe.wait_ge(s["ks"], 32 * (t + 2))
                mx_read.wait(pe, t, n - 2)
                bank = ps_m[n % 2]
                if b == SELECT:
                    for r in range(8):
                        last = nc.tensor.matmul(bank[:, r * KEEP:(r + 1) * KEEP], q_hi[par][0:DQK, (8 * q + r) * P:(8 * q + r + 1) * P],
                                                ks_hi[par][0:DQK, 0:KEEP], start=True, stop=True)
                else:
                    w = min(CH, (q + 1) * P - c * CH)
                    diag = c == q // 4
                    last = nc.tensor.matmul(bank[:, 0:w], q_hi[par][0:DQK, q * P:(q + 1) * P], k_hi[b][par][0:DQK, c * CH:c * CH + w],
                                            start=True, stop=not diag)
                    if diag:
                        last = nc.tensor.matmul(bank[:, w - P:w], g.ident16[:], g.mask_qk[:], start=False, stop=True)
                mx.after(last)
                return
            n = PJ[task]
            if task == ("q", 0, 0):
                built.wait(pe, t, 0)
            pj_read.wait(pe, t, n - 1)
            if task[0] == "q":
                _, j, rot = task
                c = slice(j * CH, (j + 1) * CH)
                last = three(ps_p[0:DQK, :], wq[0][:, rot, :], wq[1][:, rot, :], g.lat_hi[0:QL, c], g.lat_lo[0:QL, c])
            elif task[0] == "k1":
                c = slice(task[1] * CH, (task[1] + 1) * CH)
                last = three(ps_p[0:DQK, :], wk1[0][QL:P, :], wk1[1][QL:P, :], g.lat_hi[QL:P, c], g.lat_lo[QL:P, c])
            elif task[0] == "kw":
                _, j, rot = task
                for kc in range(KC):
                    for w in range(2):
                        last = nc.tensor.matmul(ps_p[0:DQK, :], wkw[w][:, kc, rot, :], g.uT[:, kc, j * CH:(j + 1) * CH],
                                                start=(kc == 0 and w == 0), stop=(kc == KC - 1 and w == 1))
            else:
                nmax.wait(pe, t, task[1])
                pe.sem_inc(s["pe_passed"], 1)
                rows = NT * (1 + task[1])
                last = nc.tensor.transpose(ps_p[0:rows, 0:P], nm[:, 0:rows], g.ident[:])
            pj.after(last)

        def pe_scores(pe, h, par, i):
            b, j, k = UNITS[i]
            if i == 0:
                r_lo.wait(pe, h - 1, 7)
                pe.wait_ge(s["rows_w"], 32 * (h + 1))
            if i == HU:
                k1.wait(pe, h, 3)
                pe.wait_ge(s["rows_l"], 16 * (h + 1))
            col, _ = width(i)
            d = col // P
            diag = b != SELECT and k >= 4 * j
            p_up.wait(pe, h, i - 3)
            qs, ks = slice(j * CH + col, (j + 1) * CH), slice(k * P, (k + 1) * P)
            bank = ps_s[i % 3]
            mid = (lambda: nc.tensor.matmul(bank[:, col:col + P], g.ident16[:], g.mask_kq[:], start=False, stop=False)) if diag else None
            aug = DQK + b + 1
            scores.after(three(bank[:, col:CH], k_hi[b][par][0:aug, ks], k_lo[b][par][:, ks], q_hi[par][0:aug, qs], q_lo[par][:, qs], mid, DQK))

        def pe_values(pe, h, par, i):
            b, j, k = UNITS[i]
            n = 4 * ORDER.index(b) + j
            if j == 0 and k == 0:
                v_split[b].wait(pe, h - 1 if b == WINDOW else h, 0)
            lower_done(pe, h, i)
            if k == 0:
                o_read.wait(pe, h, n - 2)
                s_read.wait(pe, h, n - 2)
            c, rows = width(i)
            w = vals[b][:, k if b != SELECT else 0, :]
            nc.tensor.matmul(ps_o[n % 2][:, c:CH], w, p_hi[0:rows, i % SLOTS, c:CH], start=(k == 0), stop=False)
            pv.after(nc.tensor.matmul(ps_o[n % 2][:, c:CH], w, p_lo[0:rows, i % LSLOTS, c:CH], start=False,
                                      stop=output_of(i) is not None))

        @block.tensor
        def _(pe):
            for sg in (scores, pv, pj, mx):
                sg.prime(pe)
            pe.wait_ge(s["kwz"], 1)
            pe.wait_ge(s["wz"], 6)
            pe.wait_ge(s["ones"], 3)
            for t in ALL_SIDE:
                if t not in OWN:
                    pe_task(pe, t, -1, 0)

            def head(h, par, prev, nxt):
                for i in range(NU):
                    pe_scores(pe, h, par, i)
                    for t in side(i, nxt):
                        pe_task(pe, t, h, par if t in OWN else 1 - par)
                    back = lagged(h, par, i, PV_LAG, prev)
                    if back:
                        pe_values(pe, *back)
            heads(pe, head)
            for i in range(NU - PV_LAG, NU):
                pe_values(pe, H - 1, 1, i)

        def dve_task(dve, task, t, par):
            if task[0] == "v":
                b = task[1]
                up, done = v_up[b], v_split[b]
                if b == SELECT:
                    src = g.vs[:, bass.ds(t, 1), :]
                    pv.wait(dve, t, -1)
                    dve.sem_inc(s["dve_passed"], 1)
                else:
                    src = v_raw
                    pv.wait(dve, t, -5 if b == LATENT else HU - 1) if not (isinstance(t, int) and t < 0) else None
                    dve.wait_ge(s["v_l" if b == LATENT else "v_w"], 16 * (t + 1 if b == LATENT else t + 2))
                up.after(nc.vector.tensor_copy(vals[b][:, :, 0:DV], src))
                up.wait(dve, t, 0)
                done.after(nc.vector.tensor_tensor(vals[b][:, :, DV:2 * DV], src, vals[b][:, :, 0:DV].bitcast(F32), ALU.subtract))
                return
            if task[0] == "max":
                _, b, q, c = task
                n = MX[task]
                mx.wait(dve, t, n)
                bank = ps_m[n % 2]
                if b == SELECT:
                    ins = nc.vector.tensor_reduce(nm[:, NT + 8 * q:NT + 8 * q + 8],
                                                  bank[:].rearrange("p (q k) -> p q k", k=KEEP), axis=AX.X, op=ALU.max, negate=True)
                else:
                    w = min(CH, (q + 1) * P - c * CH)
                    ins = nc.vector.tensor_reduce(mpart[:, q, c:c + 1], bank[:, 0:w], axis=AX.X, op=ALU.max)
                mx_read.after(ins)
                return
            n = PJ[task]
            if task[0] in ("q", "kw"):
                what, j, rot = task
                r = ROPED.index((what, j))
                c = slice(j * CH, (j + 1) * CH)
                tab = (g.cos, g.sin) if what == "q" else (g.cos_a, g.sin_a)
                if rot == 0:
                    r_full.wait(dve, t, r - 2)
                pj.wait(dve, t, n)
                pj_read.after(nc.vector.tensor_tensor((t1, t2)[rot][:, r % 2, :], ps_p[0:DQK, :], tab[rot][:, c], ALU.mult))
                if rot:
                    pj_read.wait(dve, t, n)
                    dve.sem_inc(roped.sem, 1)
            elif task[0] == "k1":
                c = slice(task[1] * CH, (task[1] + 1) * CH)
                pj.wait(dve, t, n)
                k1c.after(nc.vector.tensor_copy(g.k1_hi[0:NOPE, c], ps_p[0:NOPE, :]))
                k1c.wait(dve, t, task[1])
                pj_read.after(nc.vector.tensor_tensor(g.k1_lo[0:NOPE, c], ps_p[0:NOPE, :], g.k1_hi[0:NOPE, c].bitcast(F32), ALU.subtract))
                pj_read.wait(dve, t, n)
                dve.sem_inc(k1.sem, 1)
            else:
                last_mx = max(m for task_, m in MX.items() if task_[1] == (LATENT if task[1] == 0 else WINDOW))
                mx_read.wait(dve, t, last_mx)
                nmax.after(nc.vector.tensor_reduce(nm[:, 0:NT], mpart[:], axis=AX.X, op=ALU.max, negate=True))
                pj.wait(dve, t, n)
                if task[1] == 0:
                    dve.wait_ge(s["rows_w"], 32 * (t + 1))
                elif not (isinstance(t, int) and t < 0):
                    dve.wait_ge(s["rows_l"], 16 * (t + 1))
                rows = NT * (1 + task[1])
                pj_read.after(nc.vector.tensor_copy(nm_t[0:rows, :], ps_p[0:rows, 0:P]))
                pj_read.wait(dve, t, n)
                dve.sem_inc(nmax_t.sem, 1)

        def dve_output(dve, h, par, i):
            out = output_of(i)
            if out is None:
                return
            n, j, b = out
            br = n // NJ
            slot = (par + br) % 2
            bank = ps_o[n % 2]
            pv.wait(dve, h, i)
            lower_read.wait(dve, h, n)
            rows = raw_o[j * DV:(j + 1) * DV, slot, :]
            o_read.after(nc.vector.tensor_tensor(rows, bank[0:DV, :], rows, ALU.add))
            if j < NJ - 1:
                return
            o_read.wait(dve, h, n)
            s_read.wait(dve, h, n)
            inv.after(nc.vector.reciprocal(sums[:, slot, :], sums[:, slot, :]))
            inv.wait(dve, h, br)
            if br == 0:
                dve.wait_ge(s["store"], 16 * (h + 1))
            norm.after(nc.vector.scalar_tensor_tensor(ot[:] if br == 0 else raw_o[:, slot, :], raw_o[:, slot, :], g.gates[:, GATE[b]:GATE[b] + 1],
                                                      sums[:, slot, :], ALU.mult, ALU.mult))
            norm.wait(dve, h, br)
            if br == 0:
                dve.sem_inc(done.sem, 1)
            else:
                done.wait(dve, h, br - 1)
                done.after(nc.vector.tensor_tensor(ot[:], ot[:], raw_o[:, slot, :], ALU.add))

        @block.vector
        def _(dve):
            for sg in (lo_dve, o_read, inv, norm, done, k1c, k1, pj_read, mx_read, roped, nmax, nmax_t, *v_split.values(), *v_up.values()):
                sg.prime(dve)
            dve.wait_ge(s["mz"], 1)
            dve.wait_ge(s["ones"], 3)
            for t in ALL_SIDE:
                if t not in OWN:
                    dve_task(dve, t, -1, 0)

            def head(h, par, prev, nxt):
                for i in range(NU):
                    for t in side(i, nxt):
                        dve_task(dve, t, h, par if t in OWN else 1 - par)
                    if i in LO_DVE:
                        lower(dve, h, i, lo_dve)
                    back = lagged(h, par, i, OUT_LAG, prev)
                    if back:
                        dve_output(dve, *back)
            heads(dve, head)
            for i in range(NU - OUT_LAG, NU):
                dve_output(dve, H - 1, 1, i)


def mix(nc, g, a):
    with ExitStack() as ctx:
        tile = lambda n, s, d=F32: ctx.enter_context(nc.sbuf_tensor(n, s, d))
        KB = H * DV // P
        o = tile("o_in", [P, 2, KB, CH])
        h0 = tile("h0_again", [P, NT, C])
        wp = tile("wp", [P, KB, C])
        wp_hi, wp_lo = tile("wp_hi", [P, KB, C], F32R), tile("wp_lo", [P, KB, C], F32R)
        rw = tile("rw", [P, KC, E])
        rw_hi, rw_lo = tile("rw_hi", [P, KC, E], F32R), tile("rw_lo", [P, KC, E], F32R)
        o_hi, o_lo = tile("o_hi", [P, 2, KB, CH], F32R), tile("o_lo", [P, 2, KB, CH], F32R)
        stats = tile("bn", [P, NT, 6])
        mv = tile("bn_mv", [P, NT, 2])
        rstd = tile("rstd2", [P, NT])
        x2 = tile("x2", [P, NT, C])
        logit = tile("logit", [P, NT, E])
        sc = {n: tile("sm_" + n, [P, NT, E]) for n in ("hot1", "hot2", "rest", "dist", "fac", "keep", "ex", "tie", "order")}
        top = {n: tile("st_" + n, [P, NT]) for n in ("m1", "m2", "t", "sum", "w1", "w2")}
        bank = [ctx.enter_context(nc.psum_tensor(f"m_ps{i}", [P, CH], F32)) for i in range(8)]
        s = {k: ctx.enter_context(nc.semaphore("m_" + k)) for k in
             ("o0", "o1", "w", "rw", "h0", "whi", "wlo", "ohi", "olo", "y", "h1", "v", "var", "rt", "x2", "xt", "xhi", "xlo", "lg", "ord", "ex", "exd")}
        block = ctx.enter_context(nc.Block())

        @block.sync
        def _(sp):
            sp.dma_start(wp[:], a["w_proj"].rearrange("(k p) n -> p k n", p=P)).then_inc(s["w"], 16)
            heads = g.o_dram.rearrange("(k f) (j r) q -> f j r k q", f=P // DV, j=NJ)
            for n in range(NJ):
                if n >= 2:
                    sp.wait_ge(s["olo"], n - 1)
                for f in range(P // DV):
                    sp.dma_start(o[f * DV:(f + 1) * DV, n % 2], heads[f, n]).then_inc(s["o%d" % (n % 2)], 16)
                if n == 0:
                    sp.dma_start(h0[:].rearrange("p t c -> p (t c)"), g.h0_dram).then_inc(s["h0"], 16)

        @block.gpsimd
        def _(pool):
            for k in range(KC):
                pool.dma_start(rw[:, k, :], a["router_w"][:, k * P:(k + 1) * P].rearrange("e p -> p e")).then_inc(s["rw"], 16)
            nc.gpsimd.iota(sc["order"][:], pattern=[[0, NT], [-1, E]], base=E, channel_multiplier=0,
                           allow_small_or_imprecise_dtypes=True).then_inc(s["ord"], 1)
            pool.wait_ge(s["ord"], 1)

        @block.tensor
        def _(pe):
            def out_product(t):
                n, m = divmod(t, CH // P)
                c = slice(m * P, (m + 1) * P)
                pe.wait_ge(s["olo"], n + 1)
                if t >= 2:
                    pe.wait_ge(s["h1"], t - 1)
                for k in range(KB):
                    for i, (l, w) in enumerate(((o_hi, wp_hi), (o_hi, wp_lo), (o_lo, wp_hi))):
                        last = nc.tensor.matmul(bank[2 + t % 2][:, 0:C], l[:, n % 2, k, c], w[:, k, :],
                                                start=(k == 0 and i == 0), stop=(k == KB - 1 and i == 2))
                last.then_inc(s["y"], 1)
            pe.wait_ge(s["whi"], 2)
            pe.wait_ge(s["wlo"], 2)
            for t in range(NT):
                out_product(t)
            for n in range(8):
                kc, j = divmod(n, NJ)
                pe.wait_ge(s["x2"], 4 * j + 4)
                if n >= 4:
                    pe.wait_ge(s["xlo"], n - 3)
                for q in range(4):
                    last = nc.tensor.transpose(bank[4 + n % 4][:, q * P:(q + 1) * P], x2[:, 4 * j + q, kc * P:(kc + 1) * P], g.ident[:])
                last.then_inc(s["xt"], 1)
            pe.wait_ge(s["xlo"], 8)
            for t in range(NT):
                for kc in range(KC):
                    for n, (l, w) in enumerate(((g.x_hi, rw_hi), (g.x_hi, rw_lo), (g.x_lo, rw_hi))):
                        last = nc.tensor.matmul(bank[0][:, t * E:(t + 1) * E], l[:, kc, t * P:(t + 1) * P], w[:, kc, :],
                                                start=(kc == 0 and n == 0), stop=(kc == KC - 1 and n == 2))
            last.then_inc(s["lg"], 1)

        @block.scalar
        def _(act):
            act.wait_ge(s["w"], 16)
            act.wait_ge(s["rw"], 32)
            nc.scalar.copy(wp_hi[:], wp[:]).then_inc(s["whi"], 1)
            nc.scalar.copy(rw_hi[:], rw[:]).then_inc(s["whi"], 1)
            for n in range(NJ):
                act.wait_ge(s["o%d" % (n % 2)], 64 * (n // 2 + 1))
                if n >= 2:
                    act.wait_ge(s["y"], 4 * (n - 1))
                nc.scalar.copy(o_hi[:, n % 2], o[:, n % 2]).then_inc(s["ohi"], 1)
            act.wait_ge(s["var"], 1)
            nc.scalar.activation(rstd[:], rstd[:], ACT.Sqrt).then_inc(s["rt"], 1)
            for n in range(8):
                kc, j = divmod(n, NJ)
                act.wait_ge(s["xt"], n + 1)
                nc.scalar.copy(g.x_hi[:, kc, j * CH:(j + 1) * CH], bank[4 + n % 4][:]).then_inc(s["xhi"], 1)
            for n in range(2):
                act.wait_ge(s["ex"], n + 1)
                nc.scalar.activation(sc["ex"][:], sc["dist"][:], ACT.Exp, scale=-1.0).then_inc(s["exd"], 1)

        @block.vector
        def _(dve):
            v = Count(dve, s["v"])
            dve.wait_ge(s["whi"], 2)
            nc.vector.tensor_tensor(wp_lo[:], wp[:], wp_hi[:].bitcast(F32), ALU.subtract).then_inc(s["wlo"], 1)
            nc.vector.tensor_tensor(rw_lo[:], rw[:], rw_hi[:].bitcast(F32), ALU.subtract).then_inc(s["wlo"], 1)
            dve.wait_ge(s["h0"], 16)

            def residual(t):
                dve.wait_ge(s["y"], t + 1)
                nc.vector.tensor_tensor(g.h1[:, t, :], bank[2 + t % 2][:, 0:C], h0[:, t, :], ALU.add).then_inc(s["h1"], 1)
            for n in range(NJ):
                dve.wait_ge(s["ohi"], n + 1)
                if n >= 2:
                    dve.wait_ge(s["y"], 4 * (n - 1))
                nc.vector.tensor_tensor(o_lo[:, n % 2], o[:, n % 2], o_hi[:, n % 2].bitcast(F32), ALU.subtract).then_inc(s["olo"], 1)
                if n:
                    for t in range(4 * n - 4, 4 * n):
                        residual(t)
            for t in range(NT - 4, NT):
                residual(t)
            for t in range(NT):
                dve.wait_ge(s["h1"], t + 1)
                v.add(nc.vector.bn_stats(stats[:, t, :], g.h1[:, t, :]))
            v.wait()
            for t in range(NT):
                v.add(nc.vector.bn_aggr(mv[:, t, :], stats[:, t, :]))
            v.wait()
            nc.vector.tensor_scalar(rstd[:], mv[:, :, 1], 1e-5, None, ALU.add).then_inc(s["var"], 1)
            dve.wait_ge(s["rt"], 1)
            v.add(nc.vector.reciprocal(rstd[:], rstd[:]))
            v.wait()
            for t in range(NT):
                nc.vector.tensor_scalar(x2[:, t, :], g.h1[:, t, :], mv[:, t, 0:1], rstd[:, t:t + 1], ALU.subtract, ALU.mult).then_inc(s["x2"], 1)
            for n in range(8):
                kc, j = divmod(n, NJ)
                c = slice(j * CH, (j + 1) * CH)
                dve.wait_ge(s["xhi"], n + 1)
                nc.vector.tensor_tensor(g.x_lo[:, kc, c], bank[4 + n % 4][:], g.x_hi[:, kc, c].bitcast(F32), ALU.subtract).then_inc(s["xlo"], 1)
            dve.wait_ge(s["lg"], 1)
            dve.wait_ge(s["ord"], 1)
            v.add(nc.vector.tensor_copy(logit[:].rearrange("p t e -> p (t e)"), bank[0][:, 0:NT * E]))
            v.wait()

            def step(ins):
                v.add(ins)
                v.wait()

            wide = lambda t: t[:].unsqueeze(2).to_broadcast([P, NT, E])

            def gate(scores, m, hot, weight, n, banned):
                step(nc.vector.tensor_reduce(m[:], scores[:], axis=AX.X, op=ALU.max))
                step(nc.vector.tensor_tensor(sc["tie"][:], scores[:], wide(m), ALU.is_equal))
                step(nc.vector.tensor_tensor(sc["tie"][:], sc["tie"][:], sc["order"][:], ALU.mult))
                step(nc.vector.tensor_reduce(top["t"][:], sc["tie"][:], axis=AX.X, op=ALU.max))
                step(nc.vector.tensor_tensor(hot[:], sc["tie"][:], wide(top["t"]), ALU.is_equal))
                step(nc.vector.tensor_scalar(sc["fac"][:], logit[:], -1.0, None, ALU.mult))
                step(nc.vector.tensor_tensor(sc["fac"][:], sc["fac"][:], logit[:], ALU.max))
                step(nc.vector.tensor_tensor(sc["fac"][:], sc["fac"][:], wide(m), ALU.max))
                v.add(nc.vector.tensor_tensor(sc["dist"][:], wide(m), logit[:], ALU.subtract))
                v.wait()
                step(nc.vector.tensor_scalar(sc["fac"][:], sc["fac"][:], 2.0 * JITTER, None, ALU.mult))
                step(nc.vector.tensor_tensor(sc["keep"][:], sc["dist"][:], sc["fac"][:], ALU.is_le))
                if banned is not None:
                    step(nc.vector.tensor_tensor(sc["tie"][:], sc["keep"][:], banned[:], ALU.mult))
                    step(nc.vector.tensor_tensor(sc["keep"][:], sc["keep"][:], sc["tie"][:], ALU.subtract))
                    step(nc.vector.tensor_scalar(sc["dist"][:], sc["dist"][:], 0.0, None, ALU.max))
                dve.sem_inc(s["ex"], 1)
                dve.wait_ge(s["exd"], n + 1)
                step(nc.vector.tensor_tensor(sc["keep"][:], sc["keep"][:], sc["ex"][:], ALU.mult))
                step(nc.vector.tensor_reduce(top["sum"][:], sc["keep"][:], axis=AX.X, op=ALU.add))
                step(nc.vector.reciprocal(weight[:], top["sum"][:]))

            gate(logit, top["m1"], sc["hot1"], top["w1"], 0, None)
            step(nc.vector.tensor_scalar(sc["rest"][:], sc["hot1"][:], -3.0e38, None, ALU.mult))
            step(nc.vector.tensor_tensor(sc["rest"][:], sc["rest"][:], logit[:], ALU.add))
            gate(sc["rest"], top["m2"], sc["hot2"], top["w2"], 1, sc["hot1"])
            step(nc.vector.tensor_tensor(sc["hot1"][:], sc["hot1"][:], wide(top["w1"]), ALU.mult))
            step(nc.vector.tensor_tensor(sc["hot2"][:], sc["hot2"][:], wide(top["w2"]), ALU.mult))
            step(nc.vector.tensor_tensor(g.dense[:], sc["hot1"][:], sc["hot2"][:], ALU.add))


def experts(nc, g, a, out):
    with ExitStack() as ctx:
        tile = lambda n, s, d=F32: ctx.enter_context(nc.sbuf_tensor(n, s, d))
        NG = NJ * FB
        raw = {"g": tile("raw_g", [P, FB, C]), "u": tile("raw_u", [P, FB, C]), "d": tile("raw_d", [P, KC, F])}
        wt = [[tile(f"wt{i}_{n}", [P, 6, CH], F32R) for n in ("hi", "lo")] for i in range(2)]
        sg = tile("silu", [P, 2, CH])
        hm = tile("hm", [P, 2, CH])
        h_hi, h_lo = tile("h_hi", [P, 2, FB, CH], F32R), tile("h_lo", [P, 2, FB, CH], F32R)
        ps_g = [ctx.enter_context(nc.psum_tensor(f"e_g{i}", [P, CH], F32)) for i in range(2)]
        ps_u = [ctx.enter_context(nc.psum_tensor(f"e_u{i}", [P, CH], F32)) for i in range(2)]
        ps_y = [ctx.enter_context(nc.psum_tensor(f"e_y{i}", [P, CH], F32)) for i in range(2)]
        ps_t = [ctx.enter_context(nc.psum_tensor(f"e_t{i}", [P, CH], F32)) for i in range(2)]
        s = {k: ctx.enter_context(nc.semaphore("e_" + k)) for k in
             ("raw", "tr", "whi", "wlo", "g", "u", "silu", "hm", "hi", "lo", "y", "acc", "out")}
        block = ctx.enter_context(nc.Block())
        LOOP = E - 2

        def load(sp, e):
            pick = lambda w: w[bass.ds(e, 1)].rearrange("o r c -> (o r) c")
            sp.dma_start(raw["g"][:], pick(a["w_gate_e"]).rearrange("(b p) c -> p b c", p=P)).then_inc(s["raw"], 16)
            sp.dma_start(raw["u"][:], pick(a["w_up"]).rearrange("(b p) c -> p b c", p=P)).then_inc(s["raw"], 16)
            sp.dma_start(raw["d"][:], pick(a["w_down"]).rearrange("(b p) c -> p b c", p=P)).then_inc(s["raw"], 16)

        @block.sync
        def _(sp):
            load(sp, 0)
            sp.wait_ge(s["tr"], 6)
            load(sp, 1)
            with sp.Fori(0, LOOP) as e:
                sp.wait_ge(s["tr"], 6 * e + 12)
                load(sp, e + 2)
            for n in range(NT):
                sp.wait_ge(s["acc"], 2 + NT * (E - 1) + n + 1)
                sp.dma_start(out[0, n * P:(n + 1) * P, :], g.h1[:, n, :]).then_inc(s["out"], 16)
            sp.wait_ge(s["out"], 16 * NT)

        def transposes(pe, e, par):
            pe.wait_ge(s["raw"], 48 * (e + 1))
            for b in range(6):
                pe.wait_ge(s["wlo"], 6 * e + b + 1)
                for q in range(4):
                    if b < 4:
                        src = raw["gu"[b // 2]][:, q, (b % 2) * P:(b % 2 + 1) * P]
                    else:
                        f = 2 * (b - 4) + q // 2
                        src = raw["d"][:, q % 2, f * P:(f + 1) * P]
                    last = nc.tensor.transpose(ps_t[b % 2][:, q * P:(q + 1) * P], src, g.ident[:])
                last.then_inc(s["tr"], 1)

        def gate_up(pe, e, par, n):
            hi, lo = wt[par]
            c = slice(n * CH, (n + 1) * CH)
            if n == 0:
                pe.wait_ge(s["wlo"], 2 + 6 * (e + 1))
            for f in range(FB):
                i = n * FB + f
                cols = slice(f * P, (f + 1) * P)
                for ps, m, sem, free in ((ps_g, 0, "g", "silu"), (ps_u, 2, "u", "hm")):
                    pe.wait_ge(s[free], NG * e + i + 1)
                    for kc in range(KC):
                        for k, (w, x) in enumerate(((hi, g.x_hi), (hi, g.x_lo), (lo, g.x_hi))):
                            last = nc.tensor.matmul(ps[i % 2][:], w[:, m + kc, cols], x[:, kc, c],
                                                    start=(kc == 0 and k == 0), stop=(kc == KC - 1 and k == 2))
                    last.then_inc(s[sem], 1)

        def down(pe, e, par, n):
            hi, lo = wt[par]
            pe.wait_ge(s["lo"], 2 + NG * e + FB * (n + 1))
            for q in range(4):
                i = 4 * n + q
                pe.wait_ge(s["acc"], NT * e + i + 1)
                for f in range(FB):
                    wcols = slice((f % 2) * C, (f % 2 + 1) * C)
                    for k, (h, w) in enumerate(((h_hi, hi), (h_hi, lo), (h_lo, hi))):
                        last = nc.tensor.matmul(ps_y[i % 2][:, 0:C], h[:, n % 2, f, q * P:(q + 1) * P], w[:, 4 + f // 2, wcols],
                                                start=(f == 0 and k == 0), stop=(f == FB - 1 and k == 2))
                last.then_inc(s["y"], 1)

        @block.tensor
        def _(pe):
            def expert(e, par, prep):
                for n in range(NJ):
                    gate_up(pe, e, par, n)
                    if n:
                        down(pe, e, par, n - 1)
                if prep:
                    transposes(pe, e + 1, 1 - par)
                down(pe, e, par, NJ - 1)
            transposes(pe, 0, 0)
            with pe.Fori(0, LOOP // 2) as pair:
                expert(2 * pair, 0, True)
                expert(2 * pair + 1, 1, True)
            expert(E - 2, 0, True)
            expert(E - 1, 1, False)

        @block.scalar
        def _(act):
            act.sem_inc(s["silu"], 2)

            def upper_weights(e, par):
                for b in range(6):
                    act.wait_ge(s["tr"], 6 * e + b + 1)
                    nc.scalar.copy(wt[par][0][:, b, :], ps_t[b % 2][:]).then_inc(s["whi"], 1)

            def upper(e, i):
                n, f = divmod(i, FB)
                act.wait_ge(s["hm"], 2 + NG * e + i + 1)
                act.wait_ge(s["y"], NT * e + 4 * n + 4)
                nc.scalar.copy(h_hi[:, n % 2, f, :], hm[:, i % 2, :]).then_inc(s["hi"], 1)

            def expert(e, par, prep):
                for i in range(NG):
                    act.wait_ge(s["g"], NG * e + i + 1)
                    act.wait_ge(s["hm"], NG * e + i + 1)
                    nc.scalar.activation(sg[:, i % 2, :], ps_g[i % 2][:], ACT.Silu).then_inc(s["silu"], 1)
                    if i:
                        upper(e, i - 1)
                upper(e, NG - 1)
                if prep:
                    upper_weights(e + 1, 1 - par)
            upper_weights(0, 0)
            with act.Fori(0, LOOP // 2) as pair:
                expert(2 * pair, 0, True)
                expert(2 * pair + 1, 1, True)
            expert(E - 2, 0, True)
            expert(E - 1, 1, False)

        @block.gpsimd
        def _(pool):
            pool.sem_inc(s["lo"], 2)

            def expert(e):
                for i in range(NG):
                    n, f = divmod(i, FB)
                    pool.wait_ge(s["hi"], NG * e + i + 1)
                    nc.gpsimd.tensor_tensor(h_lo[:, n % 2, f, :], hm[:, i % 2, :], h_hi[:, n % 2, f, :].bitcast(F32), ALU.subtract).then_inc(s["lo"], 1)
            with pool.Fori(0, E) as e:
                expert(e)

        @block.vector
        def _(dve):
            dve.sem_inc(s["wlo"], 2)
            dve.sem_inc(s["hm"], 2)
            dve.sem_inc(s["acc"], 2)
            dve.sem_inc(s["y"], 8)

            def lower_weights(e, par):
                for b in range(6):
                    dve.wait_ge(s["whi"], 6 * e + b + 1)
                    nc.vector.tensor_tensor(wt[par][1][:, b, :], ps_t[b % 2][:], wt[par][0][:, b, :].bitcast(F32), ALU.subtract).then_inc(s["wlo"], 1)

            def accumulate(e, n):
                for q in range(4):
                    i = 4 * n + q
                    dve.wait_ge(s["y"], 8 + NT * e + i + 1)
                    nc.vector.scalar_tensor_tensor(g.h1[:, i, :], ps_y[i % 2][:, 0:C], g.dense[:, i, bass.ds(e, 1)], g.h1[:, i, :],
                                                   ALU.mult, ALU.add).then_inc(s["acc"], 1)

            def expert(e, par, prep):
                for n in range(NJ):
                    for f in range(FB):
                        i = n * FB + f
                        dve.wait_ge(s["silu"], 2 + NG * e + i + 1)
                        dve.wait_ge(s["u"], NG * e + i + 1)
                        dve.wait_ge(s["lo"], NG * e + i + 1)
                        nc.vector.tensor_tensor(hm[:, i % 2, :], sg[:, i % 2, :], ps_u[i % 2][:], ALU.mult).then_inc(s["hm"], 1)
                    if n:
                        accumulate(e, n - 1)
                if prep:
                    lower_weights(e + 1, 1 - par)
                accumulate(e, NJ - 1)
            lower_weights(0, 0)
            with dve.Fori(0, LOOP // 2) as pair:
                expert(2 * pair, 0, True)
                expert(2 * pair + 1, 1, True)
            expert(E - 2, 0, True)
            expert(E - 1, 1, False)


class Tiles:
    pass


def layer(nc, a, out):
    g = Tiles()
    g.h0_dram = nc.dram_tensor("h0_scratch", [P, NT * C], F32).ap()
    g.row_dram = nc.dram_tensor("row_scratch", [2, T], F32).ap()
    g.v_dram = nc.dram_tensor("v_scratch", [2, H, P, NT * DV], F32).ap()
    g.ks_dram = nc.dram_tensor("ks_scratch", [H, QA + DQK, P], F32).ap()
    g.o_dram = nc.dram_tensor("o_scratch", [H, P, CH], F32).ap()
    with ExitStack() as ctx:
        tile = lambda n, s, d=F32: ctx.enter_context(nc.sbuf_tensor(n, s, d))
        g.ident, g.ones = tile("ident", [P, P]), tile("ones", [P, P])
        g.ident16, g.mask_qk, g.mask_kq = tile("ident16", [P, P], BF16), tile("mask_qk", [P, P], BF16), tile("mask_kq", [P, P], BF16)
        g.inv, g.rstd, g.imp, g.gates = tile("inv", [P, 1]), tile("rstd", [P, NT]), tile("imp", [P, NT]), tile("gates", [P, 3])
        g.onehot = tile("onehot", [QA, NB])
        g.vs = tile("v_sel", [KEEP, H, DV])
        early = tile("early", [P, NT * (C + NS)])
        g.early = early
        g.U = early[:, 0:NT * C].rearrange("p (t c) -> p t c", c=C)
        g.sm = early[:, NT * C:NT * (C + NS)].rearrange("p (t n) -> p t n", n=NS)
        embed(nc, g, a["x"], a["tok_weight"])
        with ExitStack() as mid:
            tile = lambda n, s, d=F32: mid.enter_context(nc.sbuf_tensor(n, s, d))
            g.uT = tile("uT", [P, KC, T], F32R)
            g.lat_hi, g.lat_lo = tile("lat_hi", [P, T], F32R), tile("lat_lo", [P, T], F32R)
            g.cos, g.sin, g.cos_a, g.sin_a = (tile(n, [DQK, T]) for n in ("cos", "sin", "cos_a", "sin_a"))
            g.k1_hi, g.k1_lo = tile("k1_hi", [QA, T], F32R), tile("k1_lo", [DQK, T], F32R)
            project(nc, g, a)
            select(nc, g, a)
            attend(nc, g, a)
        g.h1 = ctx.enter_context(nc.sbuf_tensor("h1", [P, NT, C], F32))
        g.x_hi = ctx.enter_context(nc.sbuf_tensor("x2T_hi", [P, KC, T], F32R))
        g.x_lo = ctx.enter_context(nc.sbuf_tensor("x2T_lo", [P, KC, T], F32R))
        g.dense = ctx.enter_context(nc.sbuf_tensor("dense_w", [P, NT, E], F32))
        mix(nc, g, a)
        experts(nc, g, a, out)


_NAMES = {
    "x": "x", "L0_tok_weight": "tok_weight", "L0_attn_w_cq": "w_cq", "L0_attn_g_qnorm": "g_qnorm", "L0_attn_w_dq_nope": "w_dq_nope",
    "L0_attn_w_dq_rope": "w_dq_rope", "L0_attn_w_ckv": "w_ckv", "L0_attn_g_kvnorm": "g_kvnorm", "L0_attn_w_dk_nope": "w_dk_nope",
    "L0_attn_w_dv": "w_dv", "L0_attn_w_krope": "w_krope", "L0_attn_w_imp": "w_imp", "L0_attn_w_selk": "w_selk", "L0_attn_w_selv": "w_selv",
    "L0_attn_w_wink": "w_wink", "L0_attn_w_winv": "w_winv", "L0_attn_w_gate": "w_gate", "L0_attn_w_proj": "w_proj",
    "L0_ffn_router_w": "router_w", "L0_ffn_w_gate": "w_gate_e", "L0_ffn_w_up": "w_up", "L0_ffn_w_down": "w_down",
}
_OUTS = [((1, T, C), "float32")]


def rope_tables():
    import numpy as np
    f = (np.float32(1.0) / np.power(np.float32(10000.0), np.arange(0, ROPE, 2, dtype=np.float32) / np.float32(ROPE))).astype(np.float32)
    angle = np.outer(np.arange(T, dtype=np.float32), f).astype(np.float32)
    c, s = np.cos(angle), np.sin(angle)
    return {"cos": np.ascontiguousarray(c.T), "sin": np.ascontiguousarray(s.T), "cos_tok": c[:KEEP].copy(), "sin_tok": s[:KEEP].copy()}


def kernel(**inputs):
    import numpy as _np
    import concourse.bacc as _bacc
    from concourse import mybir as _mybir
    from concourse.bass_utils import run_bass_kernel_spmd as _run

    nc = _bacc.Bacc("TRN2", target_bir_lowering=False, num_devices=1)
    arrays, args = {}, {}
    given = {_NAMES[n]: inputs[n] for n in _NAMES}
    for name, value in {**given, **rope_tables()}.items():
        v = _np.ascontiguousarray(value)
        arrays[f"in_{name}_dram"] = v
        args[name] = nc.dram_tensor(f"in_{name}_dram", v.shape, _mybir.dt.from_np(v.dtype), kind="ExternalInput").ap()
    outs = [nc.dram_tensor(f"out_{i}_dram", shape, _mybir.dt.from_np(_np.dtype(dtype)), kind="ExternalOutput").ap()
            for i, (shape, dtype) in enumerate(_OUTS)]
    with nc.allow_non_contiguous_dma(reason="small index, router and row loads"):
        layer(nc, args, outs[0])
    r = _run(nc, [arrays], core_ids=[0])
    return r.results[0]["out_0_dram"]
```

```python
from contextlib import ExitStack

import concourse.bass as bass
from concourse import mybir

F32 = mybir.dt.float32
F32R = mybir.dt.float32r
BF16 = mybir.dt.bfloat16
I32 = mybir.dt.int32
ALU = mybir.AluOpType
ACT = mybir.ActivationFunctionType
AX = mybir.AxisListType

P = 128
T = 2048
C = 256
NT = T // P
KC = C // P
H = 16
NOPE, ROPE, HALF = 32, 64, 32
DQK = NOPE + ROPE
DV = 32
QL, KVL = 96, 32
KEEP = 64
VOCAB = 32000
SCALE = float(DQK) ** -0.5
MASKED = -1.0e30
CH = 512
NJ = T // CH
WINDOW, SELECT, LATENT = 0, 1, 2
NB = 3
GATE = {LATENT: 0, SELECT: 1, WINDOW: 2}
QA = DQK + NB
E, F = 8, 512
FB = F // P
JITTER = 0.01

CQ0, CKV0, KR0, IMP0, GATE0, NS = 0, QL, QL + KVL, QL + KVL + ROPE, QL + KVL + ROPE + 1, QL + KVL + ROPE + 4


class Count:

    def __init__(self, eng, sem, base=0, after=None):
        self.eng, self.sem, self.base, self.n, self.after = eng, sem, base, 0, after

    def add(self, ins):
        self.n += 1
        return ins.then_inc(self.sem, 1)

    def wait(self):
        self.eng.wait_ge(self.sem, self.base + self.n)
        if self.after is not None:
            self.eng.sem_inc(self.after, 1)


class Signal:

    def __init__(self, sem, per, t0=0, k0=0, prime=None):
        self.sem, self.per, self.t0, self.k0 = sem, per, t0, k0
        self.prime_by = per if prime is None else prime

    def prime(self, eng):
        eng.sem_inc(self.sem, self.prime_by)

    def wait(self, eng, t, k):
        eng.wait_ge(self.sem, self.per * t + (self.prime_by - self.per * self.t0 + k - self.k0 + 1))

    def after(self, ins):
        return ins.then_inc(self.sem, 1)


def embed(nc, g, x, weight):
    ROWS = VOCAB // P
    NCHUNK, BUF = 16, 4
    W = ROWS * C // NCHUNK
    SPLIT = 2200
    wv = weight.rearrange("(p r) c -> p (r c)", p=P)
    with ExitStack() as ctx:
        tile = lambda n, s, d=F32: ctx.enter_context(nc.sbuf_tensor(n, s, d))
        wbuf = tile("wbuf", [P, BUF, W])
        junk = tile("abs_junk", [P, SPLIT], BF16)
        part = tile("abs_part", [P, 2 * NCHUNK])
        tot = tile("abs_tot", [P, 1])
        scale = tile("scale", [P, 4])
        idx = tile("tok_idx", [P, NT], I32)
        rows = tile("tok_rows", [P, NT, C])
        below = tile("below", [P, NT, C])
        h0 = tile("h0_tile", [P, NT, C])
        tsum = tile("tsum", [P, NT])
        usq = tile("usq", [P, C])
        var = tile("var_u", [P, NT])
        inv2 = tile("inv2", [P, 1])
        std = tile("std_u", [P, NT])
        pt = ctx.enter_context(nc.psum_tensor("ps_total", [P, CH], F32))
        s = {k: ctx.enter_context(nc.semaphore("a_" + k)) for k in
             ("idx", "gather", "act", "dve", "pe", "scale", "tern", "sq", "h0", "h0st", "std", "v", "const", "rst")}
        ld = [ctx.enter_context(nc.semaphore(f"a_w{i}")) for i in range(BUF)]
        block = ctx.enter_context(nc.Block())

        @block.sync
        def _(sp):
            for n in range(NCHUNK):
                if n >= BUF:
                    sp.wait_ge(s["act"], n - BUF + 1)
                    sp.wait_ge(s["dve"], n - BUF + 1)
                sp.dma_start(wbuf[:, n % BUF, :], wv[:, n * W:(n + 1) * W]).then_inc(ld[n % BUF], 16)
            sp.wait_ge(s["h0"], 1)
            sp.dma_start(g.h0_dram, h0[:].rearrange("p t c -> p (t c)")).then_inc(s["h0st"], 16)
            sp.wait_ge(s["h0st"], 16)

        @block.gpsimd
        def _(pool):
            pool.dma_start(idx[:], x.rearrange("o (t p) -> p (o t)", p=P)).then_inc(s["idx"], 16)
            cst = Count(pool, s["const"])
            cst.add(nc.gpsimd.memset(g.ones[:], 1.0))
            cst.add(nc.gpsimd.memset(g.ident[:], 0.0))
            cst.wait()
            cst.add(nc.gpsimd.affine_select(out=g.ident[:], in_=g.ident[:], compare_op=ALU.not_equal, fill=1.0,
                                            base=0, pattern=[[-1, P]], channel_multiplier=1))
            cst.wait()
            cst.add(nc.gpsimd.tensor_copy(g.ident16[:], g.ident[:]))
            cst.add(nc.gpsimd.memset(g.mask_qk[:], 0.0))
            cst.add(nc.gpsimd.memset(g.mask_kq[:], 0.0))
            cst.wait()
            cst.add(nc.gpsimd.affine_select(out=g.mask_qk[:], in_=g.mask_qk[:], compare_op=ALU.is_ge, fill=MASKED,
                                            base=0, pattern=[[-1, P]], channel_multiplier=1))
            cst.add(nc.gpsimd.affine_select(out=g.mask_kq[:], in_=g.mask_kq[:], compare_op=ALU.is_ge, fill=MASKED,
                                            base=0, pattern=[[1, P]], channel_multiplier=-1))
            pool.wait_ge(s["idx"], 16)
            for t in range(NT):
                nc.gpsimd.indirect_dma_start(out=rows[:, t, :], out_offset=None, in_=weight,
                                             in_offset=bass.IndirectOffsetOnAxis(ap=idx[:, t:t + 1], axis=0)
                                             ).then_inc(s["gather"], 16)
            cst.wait()

        @block.scalar
        def _(act):
            for n in range(NCHUNK):
                act.wait_ge(ld[n % BUF], 16 * (n // BUF + 1))
                if n:
                    act.wait_ge(s["act"], n)
                nc.scalar.activation(junk[:], wbuf[:, n % BUF, 0:SPLIT], ACT.Abs,
                                     accum_out=part[:, n:n + 1]).then_inc(s["act"], 1)
            act.wait_ge(s["tern"], 1)
            nc.scalar.activation(h0[:].rearrange("p t c -> p (t c)"), rows[:].rearrange("p t c -> p (t c)"),
                                 ACT.Copy, scale=g.inv[:, 0:1]).then_inc(s["h0"], 1)
            act.wait_ge(s["tern"], 2)
            for t in range(NT):
                if t:
                    act.wait_ge(s["sq"], t)
                nc.scalar.activation(usq[:], g.U[:, t, :], ACT.Square, accum_out=var[:, t:t + 1]).then_inc(s["sq"], 1)
            act.wait_ge(s["std"], 1)
            nc.scalar.activation(std[:], var[:], ACT.Sqrt).then_inc(s["rst"], 1)

        @block.tensor
        def _(pe):
            pe.wait_ge(s["const"], 1)
            pe.wait_ge(s["scale"], 1)
            nc.tensor.matmul(pt[:, 0:1], g.ones[:], tot[:], start=True, stop=True).then_inc(s["pe"], 1)

        @block.vector
        def _(dve):
            for n in range(NCHUNK):
                dve.wait_ge(ld[n % BUF], 16 * (n // BUF + 1))
                nc.vector.tensor_reduce(part[:, NCHUNK + n:NCHUNK + n + 1], wbuf[:, n % BUF, SPLIT:W], axis=AX.X,
                                        op=ALU.add, apply_absolute_value=True).then_inc(s["dve"], 1)
            v = Count(dve, s["v"])
            dve.wait_ge(s["act"], NCHUNK)
            dve.wait_ge(s["dve"], NCHUNK)
            nc.vector.tensor_reduce(tot[:], part[:], axis=AX.X, op=ALU.add).then_inc(s["scale"], 1)
            dve.wait_ge(s["pe"], 1)
            v.add(nc.vector.tensor_scalar(scale[:, 0:1], pt[:, 0:1], 1.0 / (VOCAB * C), 1e-5, ALU.mult, ALU.max))
            v.wait()
            v.add(nc.vector.reciprocal(scale[:, 1:2], scale[:, 0:1]))
            v.wait()
            v.add(nc.vector.reciprocal(g.inv[:], scale[:, 1:2]))
            dve.wait_ge(s["gather"], 16 * NT)
            v.add(nc.vector.tensor_scalar(below[:], rows[:], scale[:, 1:2], -0.5, ALU.mult, ALU.is_lt))
            v.wait()
            v.add(nc.vector.tensor_scalar(rows[:], rows[:], scale[:, 1:2], 0.5, ALU.mult, ALU.is_gt))
            v.wait()
            nc.vector.tensor_tensor(rows[:], rows[:], below[:], ALU.subtract).then_inc(s["tern"], 1)
            dve.wait_ge(s["tern"], 1)
            v.add(nc.vector.tensor_reduce(tsum[:], rows[:], axis=AX.X, op=ALU.add))
            v.wait()
            v.add(nc.vector.tensor_scalar(tsum[:], tsum[:], -1.0 / C, None, ALU.mult))
            v.wait()
            nc.vector.tensor_tensor(g.U[:], rows[:], tsum[:].unsqueeze(2).to_broadcast([P, NT, C]),
                                    ALU.add).then_inc(s["tern"], 1)
            v.add(nc.vector.tensor_tensor(inv2[:], g.inv[:], g.inv[:], ALU.mult))
            dve.wait_ge(s["sq"], NT)
            v.wait()
            v.add(nc.vector.tensor_scalar(var[:], var[:], inv2[:, 0:1], 1.0 / C, ALU.mult, ALU.mult))
            v.wait()
            nc.vector.tensor_scalar(var[:], var[:], 1e-5, None, ALU.add).then_inc(s["std"], 1)
            dve.wait_ge(s["rst"], 1)
            v.add(nc.vector.reciprocal(std[:], std[:]))
            v.wait()
            v.add(nc.vector.tensor_scalar(g.rstd[:], std[:], g.inv[:, 0:1], None, ALU.mult))
            v.wait()


def project(nc, g, a):
    with ExitStack() as ctx:
        tile = lambda n, s, d=F32: ctx.enter_context(nc.sbuf_tensor(n, s, d))
        wsm = tile("wsm", [P, KC, NS])
        wsm_hi, wsm_lo = tile("wsm_hi", [P, KC, NS], F32R), tile("wsm_lo", [P, KC, NS], F32R)
        wv = tile("wv", [P, KC, CH])
        wv_hi, wv_lo = tile("wv_hi", [P, KC, CH], F32R), tile("wv_lo", [P, KC, CH], F32R)
        wd = tile("wd", [P, CH])
        wd_hi, wd_lo = tile("wd_hi", [P, CH], F32R), tile("wd_lo", [P, CH], F32R)
        gains = tile("gains", [P, QL + KVL])
        lat = tile("latents", [P, NT, P])
        ss = tile("lat_ss", [P, 2, NT])
        krot = tile("krot", [P, NT, DQK])
        srow = tile("score_row", [P, T])
        junk = tile("rank_junk", [P, T], BF16)
        before = tile("before", [P, T], BF16)
        vt = tile("vt", [P, H, NT, DV])
        t1 = tile("kr_t1", [DQK, CH])
        t2 = tile("kr_t2", [DQK, CH])
        full = tile("kr_full", [DQK, CH])
        bank = [ctx.enter_context(nc.psum_tensor(f"b_ps{i}", [P, CH], F32)) for i in range(8)]
        s = {k: ctx.enter_context(nc.semaphore("b_" + k)) for k in
             ("w", "wd", "tab", "gain", "whi", "wlo", "tr", "ut", "sm", "smev", "smev1", "v", "std", "rt", "lat", "lt", "lhi", "llo",
              "kt", "kt1", "full", "khi", "klo", "vps", "vev", "v1ps", "v1ev", "vst", "arst", "arld", "ca", "gt", "rot", "sst", "p", "row", "bef")}
        block = ctx.enter_context(nc.Block())

        @block.sync
        def _(sp):
            for lo, w in ((CQ0, a["w_cq"]), (CKV0, a["w_ckv"]), (KR0, a["w_krope"]), (IMP0, a["w_imp"]), (GATE0, a["w_gate"])):
                sp.dma_start(wsm[:, :, lo:lo + w.shape[1]], w.rearrange("(k p) n -> p k n", p=P)).then_inc(s["w"], 16)
            sp.dma_start(wv[:], a["w_winv"].rearrange("(k p) n -> p k n", p=P)).then_inc(s["wd"], 16)
            sp.dma_start(wd[QL:P, :], a["w_dv"]).then_inc(s["wd"], 16)
            sp.dma_start(g.row_dram[0:1, :].rearrange("o (t p) -> p (o t)", p=P), g.rstd[:]).then_inc(s["arst"], 16)
            sp.wait_ge(s["arst"], 16)
            sp.dma_start(g.cos_a[:], g.row_dram[0:1, :].to_broadcast([DQK, T])).then_inc(s["arld"], 16)
            sp.wait_ge(s["smev1"], 1)
            sp.dma_start(g.row_dram[1:2, :].rearrange("o (t p) -> p (o t)", p=P), g.imp[:]).then_inc(s["sst"], 16)
            sp.wait_ge(s["sst"], 16)
            sp.dma_start(srow[:], g.row_dram[1:2, :].to_broadcast([P, T])).then_inc(s["row"], 16)
            for b, (ev, n) in enumerate((("vev", 16), ("v1ev", 16))):
                sp.wait_ge(s[ev], n)
                sp.dma_start(g.v_dram[(1, 0)[b]].rearrange("h p n -> p h n"),
                             vt[:].rearrange("p h t n -> p h (t n)")).then_inc(s["vst"], 16)
                sp.wait_ge(s["vst"], 16 * (b + 1))

        @block.gpsimd
        def _(pool):
            for r in (NOPE, NOPE + HALF):
                pool.dma_start(g.cos[r:r + HALF, :], a["cos"]).then_inc(s["tab"], 16)
                pool.dma_start(g.sin[r:r + HALF, :], a["sin"]).then_inc(s["tab"], 16)
            pool.dma_start(gains[:, 0:QL], a["g_qnorm"].rearrange("(o n) -> o n", o=1).to_broadcast([P, QL])).then_inc(s["gain"], 16)
            pool.dma_start(gains[:, QL:P], a["g_kvnorm"].rearrange("(o n) -> o n", o=1).to_broadcast([P, KVL])).then_inc(s["gain"], 16)
            p = Count(pool, s["p"])
            p.add(nc.gpsimd.memset(g.cos[0:NOPE, :], 1.0))
            p.add(nc.gpsimd.memset(g.sin[0:NOPE, :], 0.0))
            p.add(nc.gpsimd.memset(krot[:, :, 0:NOPE], 0.0))
            pool.wait_ge(s["tab"], 64)
            pool.wait_ge(s["arld"], 16)
            p.wait()
            nc.gpsimd.tensor_tensor(g.sin_a[:], g.sin[:], g.cos_a[:], ALU.mult).then_inc(s["ca"], 1)
            pool.wait_ge(s["ca"], 1)
            nc.gpsimd.tensor_tensor(g.cos_a[:], g.cos[:], g.cos_a[:], ALU.mult).then_inc(s["ca"], 1)
            nc.gpsimd.memset(before[:], 1.0).then_inc(s["bef"], 1)
            pool.wait_ge(s["bef"], 1)
            nc.gpsimd.affine_select(out=before[:], in_=before[:], compare_op=ALU.is_gt, fill=0.0,
                                    base=T - P, pattern=[[-1, T]], channel_multiplier=1).then_inc(s["bef"], 1)
            pool.wait_ge(s["bef"], 2)
            pool.wait_ge(s["ca"], 2)

        def kr_transposes(pe):
            for j in range(NJ):
                for n, src in ((0, g.sm[:, :, CKV0:CKV0 + DQK]), (1, krot[:])):
                    m = 2 * j + n
                    if m >= 2:
                        pe.wait_ge(s["kt1"], m - 1)
                    for q in range(4):
                        last = nc.tensor.transpose(bank[4 + m % 2][0:DQK, q * P:(q + 1) * P], src[:, 4 * j + q, :], g.ident[:])
                    last.then_inc(s["kt"], 1)

        @block.tensor
        def _(pe):
            for n in range(8):
                kc, j = divmod(n, NJ)
                if n >= 4:
                    pe.wait_ge(s["ut"], n - 3)
                for q in range(4):
                    last = nc.tensor.transpose(bank[n % 4][:, q * P:(q + 1) * P],
                                               g.U[:, 4 * j + q, kc * P:(kc + 1) * P], g.ident[:])
                last.then_inc(s["tr"], 1)
            pe.wait_ge(s["ut"], 8)
            pe.wait_ge(s["whi"], 1)
            pe.wait_ge(s["wlo"], 1)
            for t in range(NT):
                if t >= 2:
                    pe.wait_ge(s["smev"], t - 1)
                for kc in range(KC):
                    for w in (wsm_hi, wsm_lo):
                        last = nc.tensor.matmul(bank[4 + t % 2][:, 0:NS], g.uT[:, kc, t * P:(t + 1) * P], w[:, kc, :],
                                                start=(kc == 0 and w is wsm_hi), stop=(kc == KC - 1 and w is wsm_lo))
                last.then_inc(s["sm"], 1)
            pe.wait_ge(s["whi"], 2)
            pe.wait_ge(s["wlo"], 2)
            for t in range(NT):
                if t >= 4:
                    pe.wait_ge(s["vev"], t - 3)
                for kc in range(KC):
                    for w in (wv_hi, wv_lo):
                        last = nc.tensor.matmul(bank[t % 4][:], g.uT[:, kc, t * P:(t + 1) * P], w[:, kc, :],
                                                start=(kc == 0 and w is wv_hi), stop=(kc == KC - 1 and w is wv_lo))
                last.then_inc(s["vps"], 1)
            pe.wait_ge(s["smev"], NT)
            for t in range(NT):
                last = nc.tensor.matmul(bank[7][:, 0:3], g.ones[:], g.sm[:, t, GATE0:GATE0 + 3], start=(t == 0), stop=(t == NT - 1))
            last.then_inc(s["gt"], 1)
            pe.wait_ge(s["rot"], 2)
            pe.wait_ge(s["p"], 3)
            kr_transposes(pe)
            pe.wait_ge(s["lat"], 1)
            for j in range(NJ):
                if j == 0:
                    pe.wait_ge(s["vev"], NT)
                if j >= 2:
                    pe.wait_ge(s["llo"], j - 1)
                for q in range(4):
                    last = nc.tensor.transpose(bank[j % 2][:, q * P:(q + 1) * P], lat[:, 4 * j + q, :], g.ident[:])
                last.then_inc(s["lt"], 1)
            pe.wait_ge(s["llo"], NJ)
            pe.wait_ge(s["whi"], 3)
            pe.wait_ge(s["wlo"], 3)
            for t in range(NT):
                if t >= 4:
                    pe.wait_ge(s["v1ev"], t - 3)
                for n, (l, w) in enumerate(((g.lat_hi, wd_hi), (g.lat_hi, wd_lo), (g.lat_lo, wd_hi))):
                    last = nc.tensor.matmul(bank[t % 4][:], l[QL:P, t * P:(t + 1) * P], w[QL:P, :], start=(n == 0), stop=(n == 2))
                last.then_inc(s["v1ps"], 1)

        @block.scalar
        def _(act):
            act.wait_ge(s["w"], 80)
            nc.scalar.copy(wsm_hi[:], wsm[:]).then_inc(s["whi"], 1)
            for n in range(0, 8, 2):
                kc, j = divmod(n, NJ)
                act.wait_ge(s["tr"], n + 1)
                if n:
                    act.wait_ge(s["ut"], n)
                nc.scalar.copy(g.uT[:, kc, j * CH:(j + 1) * CH], bank[n % 4][:]).then_inc(s["ut"], 1)
            for t in range(NT):
                act.wait_ge(s["sm"], t + 1)
                nc.scalar.activation(g.sm[:, t, :], bank[4 + t % 2][:, 0:NS], ACT.Copy, scale=g.rstd[:, t:t + 1]).then_inc(s["smev"], 1)
            act.wait_ge(s["wd"], 32)
            nc.scalar.copy(wv_hi[:], wv[:]).then_inc(s["whi"], 1)
            nc.scalar.copy(wd_hi[QL:P, :], wd[QL:P, :]).then_inc(s["whi"], 1)
            for t in range(NT):
                act.wait_ge(s["vps"], t + 1)
                nc.scalar.activation(vt[:, :, t, :], bank[t % 4][:].rearrange("p (h d) -> p h d", h=H), ACT.Copy,
                                     scale=g.rstd[:, t:t + 1]).then_inc(s["vev"], 1)
            act.wait_ge(s["std"], 1)
            nc.scalar.activation(ss[:], ss[:], ACT.Sqrt).then_inc(s["rt"], 1)
            for j in range(NJ):
                act.wait_ge(s["full"], j + 1)
                nc.scalar.copy(g.k1_hi[0:DQK, j * CH:(j + 1) * CH], full[:]).then_inc(s["khi"], 1)
            for j in range(NJ):
                act.wait_ge(s["lt"], j + 1)
                nc.scalar.copy(g.lat_hi[:, j * CH:(j + 1) * CH], bank[j % 2][:]).then_inc(s["lhi"], 1)
            act.wait_ge(s["vst"], 16)
            for t in range(NT):
                act.wait_ge(s["v1ps"], t + 1)
                nc.scalar.copy(vt[:, :, t, :], bank[t % 4][:].rearrange("p (h d) -> p h d", h=H)).then_inc(s["v1ev"], 1)

        @block.vector
        def _(dve):
            v = Count(dve, s["v"])
            for n in range(1, 8, 2):
                kc, j = divmod(n, NJ)
                dve.wait_ge(s["tr"], n + 1)
                dve.wait_ge(s["ut"], n)
                nc.vector.tensor_copy(g.uT[:, kc, j * CH:(j + 1) * CH], bank[n % 4][:]).then_inc(s["ut"], 1)
            dve.wait_ge(s["whi"], 1)
            nc.vector.tensor_tensor(wsm_lo[:], wsm[:], wsm_hi[:].bitcast(F32), ALU.subtract).then_inc(s["wlo"], 1)
            dve.wait_ge(s["whi"], 3)
            nc.vector.tensor_tensor(wv_lo[:], wv[:], wv_hi[:].bitcast(F32), ALU.subtract).then_inc(s["wlo"], 1)
            nc.vector.tensor_tensor(wd_lo[QL:P, :], wd[QL:P, :], wd_hi[QL:P, :].bitcast(F32), ALU.subtract).then_inc(s["wlo"], 1)
            dve.wait_ge(s["smev"], NT)
            nc.vector.tensor_copy(g.imp[:], g.sm[:, :, IMP0]).then_inc(s["smev1"], 1)
            v.add(nc.vector.tensor_scalar(g.sm[:, :, KR0:KR0 + ROPE], g.sm[:, :, KR0:KR0 + ROPE], 1.0 / H, None, ALU.mult))
            v.wait()
            nc.vector.tensor_scalar(krot[:, :, NOPE:NOPE + HALF], g.sm[:, :, KR0 + HALF:KR0 + ROPE], -1.0, None, ALU.mult).then_inc(s["rot"], 1)
            nc.vector.tensor_copy(krot[:, :, NOPE + HALF:DQK], g.sm[:, :, KR0:KR0 + HALF]).then_inc(s["rot"], 1)
            v.add(nc.vector.tensor_tensor(lat[:], g.sm[:, :, 0:P], g.sm[:, :, 0:P], ALU.mult))
            v.wait()
            v.add(nc.vector.tensor_reduce(ss[:, 0, :], lat[:, :, 0:QL], axis=AX.X, op=ALU.add))
            v.add(nc.vector.tensor_reduce(ss[:, 1, :], lat[:, :, QL:P], axis=AX.X, op=ALU.add))
            v.wait()
            v.add(nc.vector.tensor_scalar(ss[:, 0, :], ss[:, 0, :], 1.0 / QL, 1e-6, ALU.mult, ALU.add))
            nc.vector.tensor_scalar(ss[:, 1, :], ss[:, 1, :], 1.0 / KVL, 1e-6, ALU.mult, ALU.add).then_inc(s["std"], 1)
            dve.wait_ge(s["rt"], 1)
            v.add(nc.vector.reciprocal(ss[:], ss[:]))
            v.wait()
            v.add(nc.vector.tensor_tensor(lat[:, :, 0:QL], g.sm[:, :, 0:QL], ss[:, 0, :].unsqueeze(2).to_broadcast([P, NT, QL]), ALU.mult))
            v.add(nc.vector.tensor_tensor(lat[:, :, QL:P], g.sm[:, :, QL:P], ss[:, 1, :].unsqueeze(2).to_broadcast([P, NT, KVL]), ALU.mult))
            dve.wait_ge(s["gain"], 32)
            v.wait()
            nc.vector.tensor_tensor(lat[:], lat[:], gains[:].unsqueeze(1).to_broadcast([P, NT, P]), ALU.mult).then_inc(s["lat"], 1)
            dve.wait_ge(s["gt"], 1)
            v.add(nc.vector.tensor_scalar(g.gates[:], bank[7][:, 0:3], 1.0 / T, None, ALU.mult))
            dve.wait_ge(s["tab"], 64)
            dve.wait_ge(s["p"], 3)
            for j in range(NJ):
                c = slice(j * CH, (j + 1) * CH)
                dve.wait_ge(s["kt"], 2 * j + 1)
                nc.vector.tensor_tensor(t1[:], bank[4][0:DQK, :], g.cos[:, c], ALU.mult).then_inc(s["kt1"], 1)
                dve.wait_ge(s["kt"], 2 * j + 2)
                nc.vector.tensor_tensor(t2[:], bank[5][0:DQK, :], g.sin[:, c], ALU.mult).then_inc(s["kt1"], 1)
                dve.wait_ge(s["kt1"], 2 * j + 2)
                if j:
                    dve.wait_ge(s["klo"], j)
                nc.vector.tensor_tensor(full[:], t1[:], t2[:], ALU.add).then_inc(s["full"], 1)
                dve.wait_ge(s["khi"], j + 1)
                dve.wait_ge(s["full"], j + 1)
                nc.vector.tensor_tensor(g.k1_lo[:, c], full[:], g.k1_hi[0:DQK, c].bitcast(F32), ALU.subtract).then_inc(s["klo"], 1)
            for j in range(NJ):
                dve.wait_ge(s["lhi"], j + 1)
                nc.vector.tensor_tensor(g.lat_lo[:, j * CH:(j + 1) * CH], bank[j % 2][:], g.lat_hi[:, j * CH:(j + 1) * CH].bitcast(F32),
                                        ALU.subtract).then_inc(s["llo"], 1)
            dve.wait_ge(s["row"], 16)
            dve.wait_ge(s["bef"], 2)
            for t in range(NT):
                sc = g.imp[:, t:t + 1]
                v.wait()
                v.add(nc.vector.tensor_scalar(junk[:], srow[:], sc, None, ALU.is_gt, ALU.add, accum_out=g.ranks[:, 0, t:t + 1]))
                n = (t + 1) * P
                v.wait()
                v.add(nc.vector.scalar_tensor_tensor(junk[:, 0:n], srow[:, 0:n], sc, before[:, T - n:T], ALU.is_equal, ALU.mult,
                                                     accum_out=g.ranks[:, 1, t:t + 1]))
            v.wait()
            v.wait()


def select(nc, g, a):
    with ExitStack() as ctx:
        tile = lambda n, s, d=F32: ctx.enter_context(nc.sbuf_tensor(n, s, d))
        strict = tile("strict", [P, P])
        flag = tile("flag", [P, NT])
        run = tile("flag_run", [P, NT])
        zero = tile("zero16", [P, NT])
        pos = tile("pos", [P, NT])
        slots = tile("slots", [P, KEEP])
        hot = tile("hot", [P, NT, KEEP])
        frs = tile("flag_rstd", [P, NT])
        selT = tile("selT", [P, KC, KEEP])
        wk = tile("wselk", [P, KC, H * DQK])
        wv = tile("wselv", [P, KC, H * DV])
        ktm = tile("ks_tok", [KEEP, H, DQK])
        krt = tile("ks_rot", [KEEP, H, DQK])
        kt1, kt2 = tile("ks_t1", [KEEP, H, HALF]), tile("ks_t2", [KEEP, H, HALF])
        kt3, kt4 = tile("ks_t3", [KEEP, H, HALF]), tile("ks_t4", [KEEP, H, HALF])
        ck, sk = tile("ck", [KEEP, HALF]), tile("sk", [KEEP, HALF])
        khi = tile("ks_hi_all", [QA, H, P], F32R)
        klo = tile("ks_lo_all", [DQK, H, P], F32R)
        gm = tile("gate_tmp", [P, 8])
        bank = [ctx.enter_context(nc.psum_tensor(f"s_ps{i}", [P, CH], F32)) for i in range(8)]
        s = {k: ctx.enter_context(nc.semaphore("s_" + k)) for k in
             ("w", "t", "p", "v", "flag", "run", "pos", "hot", "sel", "selc", "ks", "rope", "kt", "khi", "klo", "vsc", "st", "ge", "gx", "c1")}
        block = ctx.enter_context(nc.Block())

        @block.sync
        def _(sp):
            sp.dma_start(wk[:], a["w_selk"].rearrange("(k p) n -> p k n", p=P)).then_inc(s["w"], 16)
            sp.dma_start(wv[:], a["w_selv"].rearrange("(k p) n -> p k n", p=P)).then_inc(s["w"], 16)
            sp.dma_start(ck[:], a["cos_tok"]).then_inc(s["t"], 16)
            sp.dma_start(sk[:], a["sin_tok"]).then_inc(s["t"], 16)
            sp.wait_ge(s["khi"], 2)
            sp.wait_ge(s["c1"], 6)
            sp.dma_start(g.ks_dram[:, 0:QA, :].rearrange("h r k -> r h k"), khi[:].bitcast(F32)).then_inc(s["st"], 16)
            sp.wait_ge(s["klo"], 2)
            sp.dma_start(g.ks_dram[:, QA:QA + DQK, :].rearrange("h r k -> r h k"), klo[:].bitcast(F32)).then_inc(s["st"], 16)
            sp.wait_ge(s["st"], 32)

        @block.gpsimd
        def _(pool):
            p = Count(pool, s["p"])
            p.add(nc.gpsimd.memset(strict[:], 1.0))
            p.add(nc.gpsimd.memset(zero[:], 0.0))
            p.add(nc.gpsimd.iota(slots[:], pattern=[[1, KEEP]], base=0, channel_multiplier=0, allow_small_or_imprecise_dtypes=True))
            p.wait()
            p.add(nc.gpsimd.affine_select(out=strict[:], in_=strict[:], compare_op=ALU.is_gt, fill=0.0,
                                          base=0, pattern=[[1, P]], channel_multiplier=-1))
            c1 = Count(pool, s["c1"])
            c1.add(nc.gpsimd.memset(khi[:].bitcast(F32), 0.0))
            c1.add(nc.gpsimd.memset(klo[:].bitcast(F32), 0.0))
            c1.wait()
            c1.add(nc.gpsimd.memset(g.onehot[DQK:QA, :], 0.0))
            c1.wait()
            c1.add(nc.gpsimd.affine_select(out=g.onehot[DQK:QA, :], in_=g.onehot[DQK:QA, :], compare_op=ALU.not_equal, fill=1.0,
                                           base=0, pattern=[[-1, NB]], channel_multiplier=1))
            c1.wait()
            c1.add(nc.gpsimd.tensor_copy(g.k1_hi[DQK:QA, :], g.onehot[DQK:QA, LATENT:LATENT + 1].to_broadcast([NB, T])))
            c1.add(nc.gpsimd.tensor_copy(khi[DQK:QA, :, :].rearrange("r h k -> r (h k)"),
                                         g.onehot[DQK:QA, SELECT:SELECT + 1].to_broadcast([NB, H * P])))
            c1.wait()
            p.wait()

        @block.tensor
        def _(pe):
            pe.wait_ge(s["p"], 4)
            pe.wait_ge(s["flag"], 1)
            nc.tensor.matmul(bank[0][:, 0:NT], strict[:], flag[:], start=True, stop=False)
            pe.wait_ge(s["run"], 1)
            nc.tensor.matmul(bank[0][:, 0:NT], g.ones[:], run[:], start=False, stop=True).then_inc(s["pos"], 1)
            pe.wait_ge(s["hot"], 1)
            for kc in range(KC):
                for t in range(NT):
                    last = nc.tensor.matmul(bank[1 + kc][:, 0:KEEP], g.U[:, t, kc * P:(kc + 1) * P], hot[:, t, :], start=(t == 0), stop=(t == NT - 1))
            last.then_inc(s["sel"], 1)
            pe.wait_ge(s["selc"], 1)
            pe.wait_ge(s["w"], 32)
            for n in range(4):
                for kc in range(KC):
                    w = wk[:, kc, n * CH:(n + 1) * CH] if n < 3 else wv[:, kc, :]
                    last = nc.tensor.matmul(bank[3 + n][0:KEEP, :], selT[:, kc, :], w, start=(kc == 0), stop=(kc == KC - 1))
                last.then_inc(s["ks"], 1)
            pe.wait_ge(s["rope"], 1)
            for h in range(H):
                last = nc.tensor.transpose(bank[h // 8][0:DQK, (h % 8) * KEEP:(h % 8 + 1) * KEEP], krt[:, h, :], g.ident[0:KEEP, 0:KEEP])
            last.then_inc(s["kt"], 1)

        @block.scalar
        def _(act):
            act.wait_ge(s["ge"], 1)
            nc.scalar.activation(gm[:, 2:5], g.gates[:], ACT.Exp, bias=gm[:, 0:1], accum_out=gm[:, 1:2]).then_inc(s["gx"], 1)
            act.wait_ge(s["ks"], 4)
            nc.scalar.copy(g.vs[:], bank[6][0:KEEP, :].rearrange("p (h d) -> p h d", h=H)).then_inc(s["vsc"], 1)
            act.wait_ge(s["kt"], 1)
            act.wait_ge(s["c1"], 2)
            for n in range(2):
                nc.scalar.copy(khi[0:DQK, 8 * n:8 * n + 8, 0:KEEP], bank[n][0:DQK, :].rearrange("p (h k) -> p h k", h=8)).then_inc(s["khi"], 1)
            act.wait_ge(s["vsc"], 1)

        @block.vector
        def _(dve):
            v = Count(dve, s["v"])
            v.add(nc.vector.tensor_reduce(gm[:, 0:1], g.gates[:], axis=AX.X, op=ALU.max))
            v.wait()
            nc.vector.tensor_scalar(gm[:, 0:1], gm[:, 0:1], -1.0, None, ALU.mult).then_inc(s["ge"], 1)
            v.add(nc.vector.tensor_tensor(flag[:], g.ranks[:, 0, :], g.ranks[:, 1, :], ALU.add))
            v.wait()
            nc.vector.tensor_scalar(flag[:], flag[:], float(KEEP), None, ALU.is_lt).then_inc(s["flag"], 1)
            dve.wait_ge(s["flag"], 1)
            dve.wait_ge(s["p"], 4)
            v.add(nc.vector.tensor_tensor_scan(run[:], flag[:], zero[:], 0.0, ALU.add, ALU.add))
            v.wait()
            nc.vector.tensor_tensor(run[:], run[:], flag[:], ALU.subtract).then_inc(s["run"], 1)
            dve.wait_ge(s["gx"], 1)
            v.add(nc.vector.reciprocal(gm[:, 5:6], gm[:, 1:2]))
            v.wait()
            v.add(nc.vector.tensor_scalar(g.gates[:], gm[:, 2:5], gm[:, 5:6], None, ALU.mult))
            dve.wait_ge(s["pos"], 1)
            v.add(nc.vector.tensor_copy(pos[:], bank[0][:, 0:NT]))
            v.add(nc.vector.tensor_tensor(frs[:], flag[:], g.rstd[:], ALU.mult))
            v.wait()
            for t in range(NT):
                ins = nc.vector.tensor_scalar(hot[:, t, :], slots[:], pos[:, t:t + 1], frs[:, t:t + 1], ALU.is_equal, ALU.mult)
            ins.then_inc(s["hot"], 1)
            dve.wait_ge(s["sel"], 1)
            v.add(nc.vector.tensor_copy(selT[:, 0, :], bank[1][:, 0:KEEP]))
            nc.vector.tensor_copy(selT[:, 1, :], bank[2][:, 0:KEEP]).then_inc(s["selc"], 1)
            dve.wait_ge(s["ks"], 3)
            for n in range(3):
                v.add(nc.vector.tensor_copy(ktm[:].rearrange("p h d -> p (h d)")[:, n * CH:(n + 1) * CH], bank[3 + n][0:KEEP, :]))
            v.wait()
            dve.wait_ge(s["t"], 32)
            x1, x2 = ktm[:, :, NOPE:NOPE + HALF], ktm[:, :, NOPE + HALF:DQK]
            cb = ck[:].unsqueeze(1).to_broadcast([KEEP, H, HALF])
            sbc = sk[:].unsqueeze(1).to_broadcast([KEEP, H, HALF])
            v.add(nc.vector.tensor_tensor(kt1[:], x1, cb, ALU.mult))
            v.add(nc.vector.tensor_tensor(kt2[:], x2, sbc, ALU.mult))
            v.add(nc.vector.tensor_tensor(kt3[:], x1, sbc, ALU.mult))
            v.add(nc.vector.tensor_tensor(kt4[:], x2, cb, ALU.mult))
            v.add(nc.vector.tensor_copy(krt[:, :, 0:NOPE], ktm[:, :, 0:NOPE]))
            v.wait()
            v.add(nc.vector.tensor_tensor(krt[:, :, NOPE:NOPE + HALF], kt1[:], kt2[:], ALU.subtract))
            nc.vector.tensor_tensor(krt[:, :, NOPE + HALF:DQK], kt3[:], kt4[:], ALU.add).then_inc(s["rope"], 1)
            for n in range(2):
                dve.wait_ge(s["khi"], n + 1)
                nc.vector.tensor_tensor(klo[:, 8 * n:8 * n + 8, 0:KEEP], bank[n][0:DQK, :].rearrange("p (h k) -> p h k", h=8),
                                        khi[0:DQK, 8 * n:8 * n + 8, 0:KEEP].bitcast(F32), ALU.subtract).then_inc(s["klo"], 1)
            v.wait()


def units():
    out = []
    for b in (WINDOW, LATENT):
        out += [(b, j, k) for j in range(NJ) for k in range(4 * j + 4)]
    return out + [(SELECT, j, 0) for j in range(NJ)]


UNITS = units()
NU = len(UNITS)
HU = NU // 2 - 2


def side_tasks():
    proj = lambda what, j: [(what, j, rot) for rot in (0, 1)]
    mx = lambda b, j=None: [("max", b, q, c) for q in (range(NT) if j is None else range(4 * j, 4 * j + 4)) for c in range(q // 4 + 1)]
    at = {}

    def spread(tasks, lo, hi):
        for n, t in enumerate(tasks):
            at.setdefault(lo + n * (hi - lo) // len(tasks), []).append(t)

    def weave(few, many):
        out = list(many)
        for n, t in enumerate(few):
            out.insert((n + 1) * len(many) // (len(few) + 1) + n, t)
        return out
    for j, i in enumerate((0, 2, 4, 7)):
        at[i] = [("k1", j)]
    spread(mx(LATENT, 0), 2, 6)
    spread(mx(LATENT, 1), 6, 12)
    late = mx(LATENT, 2) + mx(LATENT, 3)
    spread(late[:9] + weave([t for j in range(NJ) for t in proj("q", j)], late[9:]), 12, HU - 6)
    spread([("v", LATENT)], 12, 13)
    spread([("neg", 0)], HU - 5, HU - 4)
    win = proj("kw", 0)[:1] + [("max", SELECT, 0, 0)] + proj("kw", 0)[1:] + [("max", SELECT, 1, 0)] + proj("kw", 1)
    win += mx(WINDOW, 0) + weave(proj("kw", 2), mx(WINDOW, 1)) + weave(proj("kw", 3), mx(WINDOW, 2)) + mx(WINDOW, 3)
    spread(win, HU - 1, 76)
    spread([("v", WINDOW)], 50, 51)
    spread([("neg", 1), ("v", SELECT)], 78, 79)
    return at


SIDE = side_tasks()
ALL_SIDE = [t for i in sorted(SIDE) for t in SIDE[i]]
OWN = [t for t in ALL_SIDE if t[0] == "k1" or t in (("v", LATENT), ("v", SELECT), ("neg", 0)) or t[:2] == ("max", LATENT)]
PJ = [t for t in ALL_SIDE if t[0] not in ("max", "v")]
MX = {t: n for n, t in enumerate(t for t in ALL_SIDE if t[0] == "max")}
PJ_OWN = [t for t in PJ if t in OWN]
PJ_NEXT = [t for t in PJ if t not in OWN]
MX_OWN = sum(t in OWN for t in MX)
ROPED = [(w, j) for w in ("q", "kw") for j in range(NJ)]
LO_DVE = [i for i in range(14, NU, 4) if not HU <= i < HU + 12]
LO_POOL = [i for i in range(NU) if i not in LO_DVE]
PV_LAG = 4
OUT_LAG = PV_LAG
SLOTS, LSLOTS = 6, 4
NPROB = 3


def attend(nc, g, a):
    with ExitStack() as ctx:
        tile = lambda n, s, d=F32: ctx.enter_context(nc.sbuf_tensor(n, s, d))
        q_hi = [tile(f"q_hi{i}", [QA, T], F32R) for i in range(2)]
        q_lo = [tile(f"q_lo{i}", [DQK, T], F32R) for i in range(2)]
        kw_hi, kw_lo = tile("kw_hi", [QA, T], F32R), tile("kw_lo", [DQK, T], F32R)
        ks_hi = [tile(f"ks_hi{i}", [QA, P], F32R) for i in range(2)]
        ks_lo = [tile(f"ks_lo{i}", [DQK, P], F32R) for i in range(2)]
        vals = {WINDOW: tile("v_win", [P, NT, P], F32R), LATENT: tile("v_lat", [P, NT, P], F32R), SELECT: tile("v_one", [KEEP, 1, P], F32R)}
        p_hi, p_lo = tile("p_hi", [P, SLOTS, CH], F32R), tile("p_lo", [P, LSLOTS, CH], F32R)
        ot = tile("o_sum", [P, CH])
        part = lambda lo, n: g.early[:, lo:lo + n * CH].rearrange("p (n c) -> p n c", c=CH)
        prob = part(0, NPROB)
        t1, t2, full = (part((NPROB + n) * CH, 2)[0:DQK] for n in (0, 2, 4))
        raw_o, sums = part((NPROB + 6) * CH, 2), part((NPROB + 8) * CH, 2)
        v_raw = part((NPROB + 10) * CH, 1)[:, 0, :].rearrange("p (t d) -> p t d", d=DV)
        mpart = tile("max_part", [P, NT, NJ])
        nm = tile("neg_max", [P, 2 * NT])
        nm_t = tile("neg_max_t", [2 * NT, P], F32R)
        raw_qk = tile("raw_qk", [P, DQK])
        raw_q, raw_k1 = raw_qk[0:QL, :], raw_qk[:, 0:NOPE]
        raw_kw = tile("raw_kw", [P, KC, DQK])
        wqk = [tile(f"wqk_{n}", [P, 2, DQK], F32R) for n in ("hi", "lo")]
        wq, wk1 = [w[0:QL] for w in wqk], [w[:, 0, :] for w in wqk]
        wkw = [tile(f"wkw_{n}", [P, KC, 2, DQK], F32R) for n in ("hi", "lo")]
        ps_s = [ctx.enter_context(nc.psum_tensor(f"ps_s{i}", [P, CH], F32)) for i in range(3)]
        ps_o = [ctx.enter_context(nc.psum_tensor(f"ps_o{i}", [P, CH], F32)) for i in range(2)]
        ps_m = [ctx.enter_context(nc.psum_tensor(f"ps_m{i}", [P, CH], F32)) for i in range(2)]
        ps_p = ctx.enter_context(nc.psum_tensor("ps_p", [P, CH], F32))
        sem = lambda n: ctx.enter_context(nc.semaphore("h_" + n))
        scores = Signal(sem("scores"), NU)
        p_full = Signal(sem("p_full"), NU)
        p_up = Signal(sem("p_up"), NU)
        lo_pool = Signal(sem("lo_pool"), len(LO_POOL))
        lo_dve = Signal(sem("lo_dve"), len(LO_DVE))
        pv = Signal(sem("pv"), NU)
        o_read = Signal(sem("o_read"), 12)
        s_read = Signal(sem("s_read"), 12)
        lower_read = Signal(sem("lower_read"), 12)
        inv = Signal(sem("inv"), 3 * NJ)
        norm = Signal(sem("norm"), 3)
        done = Signal(sem("done"), 3)
        v_split = {b: Signal(sem(f"v_split{b}"), 1, t0=(-1 if b == WINDOW else 0)) for b in (WINDOW, LATENT, SELECT)}
        v_up = {b: Signal(sem(f"v_up{b}"), 1, t0=(-1 if b == WINDOW else 0)) for b in (WINDOW, LATENT, SELECT)}
        k1c, k1 = Signal(sem("k1_hi"), NJ), Signal(sem("k1"), NJ)
        pj = {True: Signal(sem("pj_own"), len(PJ_OWN)), False: Signal(sem("pj_next"), len(PJ_NEXT), -1)}
        pj_read = {True: Signal(sem("pj_own_read"), len(PJ_OWN)), False: Signal(sem("pj_next_read"), len(PJ_NEXT), -1)}
        mx = Signal(sem("mx"), len(MX), -1, MX_OWN, MX_OWN)
        mx_read = Signal(sem("mx_read"), len(MX), -1, MX_OWN, MX_OWN)
        roped = Signal(sem("roped"), 8, -1)
        r_full = Signal(sem("r_full"), 8, -1)
        r_up = Signal(sem("r_up"), 8, -1)
        r_lo = Signal(sem("r_lo"), 8, -1)
        nmax = Signal(sem("nmax"), 2, -1, 1)
        nmax_t = Signal(sem("nmax_t"), 2, -1, 1)
        built = Signal(sem("built"), 1, -1)
        s = {k: sem(k) for k in ("rows_w", "rows_l", "raw", "v_w", "v_l", "ks", "store", "wb", "set", "ones", "passed", "pe_passed", "dve_passed", "sp_passed")}
        block = ctx.enter_context(nc.Block())
        k_hi = {LATENT: [g.k1_hi] * 2, WINDOW: [kw_hi] * 2, SELECT: ks_hi}
        k_lo = {LATENT: [g.k1_lo] * 2, WINDOW: [kw_lo] * 2, SELECT: ks_lo}
        ORDER = (WINDOW, LATENT, SELECT)

        def heads(eng, head):
            head(0, 0, False, True)
            with eng.Fori(0, H // 2 - 1) as pair:
                head(2 * pair + 1, 1, True, True)
                head(2 * pair + 2, 0, True, True)
            head(H - 1, 1, True, False)

        def lagged(h, par, i, lag, prev):
            if i >= lag:
                return h, par, i - lag
            return (h - 1, 1 - par, i - lag + NU) if prev else None

        def pj_wait(eng, which, t, task):
            own = task in OWN
            which[own].wait(eng, t, (PJ_OWN if own else PJ_NEXT).index(task))

        def is_first(t):
            return isinstance(t, int) and t < 0

        def mx_bank(t, task):
            banks = ps_m + ps_s[0:2] if is_first(t) else ps_m
            return banks[MX[task] % len(banks)]

        def pj_bank(t, task):
            return (ps_p, ps_o[0])[PJ_NEXT.index(task) % 2] if is_first(t) else ps_p

        def side(i, nxt):
            return [t for t in SIDE.get(i, ()) if nxt or t in OWN]

        def width(i):
            b, j, k = UNITS[i]
            return (max(0, k - 4 * j) * P if b != SELECT else 0), (KEEP if b == SELECT else P)

        def lower_done(eng, h, i):
            i, back = (i, 0) if i >= 0 else (i + NU, 1)
            if i in LO_DVE:
                lo_dve.wait(eng, h, LO_DVE.index(i) - back * len(LO_DVE))
            else:
                lo_pool.wait(eng, h, LO_POOL.index(i) - back * len(LO_POOL))

        def load_raw(sp, h):
            sp.dma_start(raw_q[:, 0:NOPE], a["w_dq_nope"][:, bass.ds(h * NOPE, NOPE)]).then_inc(s["raw"], 16)
            sp.dma_start(raw_q[:, NOPE:DQK], a["w_dq_rope"][:, bass.ds(h * ROPE, ROPE)]).then_inc(s["raw"], 16)
            sp.dma_start(raw_k1[QL:P, :], a["w_dk_nope"][:, bass.ds(h * NOPE, NOPE)]).then_inc(s["raw"], 16)
            sp.dma_start(raw_kw[:], a["w_wink"].rearrange("(k p) n -> p k n", p=P)[:, :, bass.ds(h * DQK, DQK)]).then_inc(s["raw"], 16)

        def load_v(sp, h, b):
            sp.dma_start(v_raw.rearrange("p t d -> p (t d)"), g.v_dram[0 if b == LATENT else 1, bass.ds(h, 1)].rearrange("o p n -> (o p) n")
                         ).then_inc(s["v_l" if b == LATENT else "v_w"], 16)

        def load_ks(sp, h, par):
            sp.dma_start(ks_hi[par][:].bitcast(F32), g.ks_dram[bass.ds(h, 1), 0:QA, :].rearrange("o r k -> (o r) k")).then_inc(s["ks"], 16)
            sp.dma_start(ks_lo[par][:].bitcast(F32), g.ks_dram[bass.ds(h, 1), QA:QA + DQK, :].rearrange("o r k -> (o r) k")).then_inc(s["ks"], 16)

        def store_rows(sp, t, n, par):
            nmax_t.wait(sp, t, n)
            sp.sem_inc(s["sp_passed"], 1)
            for r, b in enumerate((LATENT,) if n == 0 else (WINDOW, SELECT)):
                sp.dma_start(q_hi[par][DQK + b:DQK + b + 1, :].bitcast(F32).rearrange("o (t q) -> o t q", q=P),
                             nm_t[r * NT:(r + 1) * NT, :].bitcast(F32)).then_inc(s["rows_l" if n == 0 else "rows_w"], 16)

        @block.sync
        def _(sp):
            sp.sem_inc(s["store"], 16)
            load_raw(sp, 0)
            load_v(sp, 0, WINDOW)
            load_ks(sp, 0, 0)
            v_split[WINDOW].wait(sp, -1, 0)
            load_v(sp, 0, LATENT)
            store_rows(sp, -1, 1, 0)

            def store(h):
                done.wait(sp, h, 2)
                sp.sem_inc(s["sp_passed"], 1)
                sp.dma_start(g.o_dram[bass.ds(h, 1)].rearrange("o r q -> (o r) q"), ot[:]).then_inc(s["store"], 16)

            def head(h, par, prev, nxt):
                if nxt:
                    built.wait(sp, h - 1, 0)
                    sp.sem_inc(s["sp_passed"], 1)
                    load_raw(sp, h + 1)
                if prev:
                    store(h - 1)
                if nxt:
                    pv.wait(sp, h, -1)
                    sp.sem_inc(s["sp_passed"], 1)
                    load_ks(sp, h + 1, 1 - par)
                    v_split[LATENT].wait(sp, h, 0)
                    sp.sem_inc(s["sp_passed"], 1)
                    load_v(sp, h + 1, WINDOW)
                store_rows(sp, h, 0, par)
                if nxt:
                    v_split[WINDOW].wait(sp, h, 0)
                    sp.sem_inc(s["sp_passed"], 1)
                    load_v(sp, h + 1, LATENT)
                    store_rows(sp, h, 1, 1 - par)
            heads(sp, head)
            store(H - 1)
            sp.wait_ge(s["store"], 16 + 16 * H)

        WB = (0, 3, 6, 10, 14)

        def build_weights(pool, t, part):
            w = Count(pool, s["wb"], WB[-1] * (t + 1) + WB[part], after=s["passed"])
            x1, x2 = slice(NOPE, NOPE + HALF), slice(NOPE + HALF, DQK)
            if part == 0:
                pool.wait_ge(s["raw"], 64 * (t + 2))
                if not isinstance(t, int) or t >= 0:
                    pj_wait(pool, pj, t, ("k1", NJ - 1))
                pool.sem_inc(s["passed"], 1)
                w.add(nc.gpsimd.tensor_copy(wq[0][:, 0, :], raw_q[:]))
                w.add(nc.gpsimd.tensor_copy(wkw[0][:, :, 0, :], raw_kw[:]))
                w.wait()
                w.add(nc.gpsimd.tensor_copy(wk1[0][QL:P, 0:NOPE], raw_k1[QL:P, :]))
                w.wait()
            elif part == 1:
                w.add(nc.gpsimd.tensor_tensor(wq[1][:, 0, :], raw_q[:], wq[0][:, 0, :].bitcast(F32), ALU.subtract))
                w.add(nc.gpsimd.tensor_tensor(wkw[1][:, :, 0, :], raw_kw[:], wkw[0][:, :, 0, :].bitcast(F32), ALU.subtract))
                w.wait()
                w.add(nc.gpsimd.tensor_tensor(wk1[1][QL:P, 0:NOPE], raw_k1[QL:P, :], wk1[0][QL:P, 0:NOPE].bitcast(F32), ALU.subtract))
                w.wait()
            elif part == 2:
                for half in wq:
                    w.add(nc.gpsimd.tensor_scalar(half[:, 1, x1], half[:, 0, x2].bitcast(F32), -1.0, None, ALU.mult))
                    w.add(nc.gpsimd.tensor_copy(half[:, 1, x2], half[:, 0, x1].bitcast(F32)))
                w.wait()
            else:
                for half in wkw:
                    w.add(nc.gpsimd.tensor_scalar(half[:, :, 1, x1], half[:, :, 0, x2].bitcast(F32), -1.0, None, ALU.mult))
                    w.add(nc.gpsimd.tensor_copy(half[:, :, 1, x2], half[:, :, 0, x1].bitcast(F32)))
                w.wait()
                pool.sem_inc(built.sem, 1)
            assert WB[part] + w.n == WB[part + 1], w.n

        def dst(what, par):
            return (q_hi[par], q_lo[par]) if what == "q" else (kw_hi, kw_lo)

        def rope_number(task):
            return ROPED.index(task[:2]) if task[0] in ("q", "kw") and task[2] == 1 else None

        def rope_sum(pool, task, t, par):
            n = rope_number(task)
            if n is not None:
                roped.wait(pool, t, n)
                r_lo.wait(pool, t, n - 2)
                r_full.after(nc.gpsimd.tensor_tensor(full[:, n % 2, :], t1[:, n % 2, :], t2[:, n % 2, :], ALU.add))

        def rope_rest(pool, task, t, par):
            n = rope_number(task)
            if n is not None:
                hi, lo = dst(task[0], par)
                c = slice(task[1] * CH, (task[1] + 1) * CH)
                r_up.wait(pool, t, n)
                r_lo.after(nc.gpsimd.tensor_tensor(lo[0:DQK, c], full[:, n % 2, :], hi[0:DQK, c].bitcast(F32), ALU.subtract))

        def lower(eng, h, i, own):
            c, rows = width(i)
            p_up.wait(eng, h, i)
            pv.wait(eng, h, i - LSLOTS)
            ns = nc.gpsimd if own is lo_pool else nc.vector
            own.after(ns.tensor_tensor(p_lo[0:rows, i % LSLOTS, c:CH], prob[0:rows, i % NPROB, c:CH],
                                       p_hi[0:rows, i % SLOTS, c:CH].bitcast(F32), ALU.subtract))

        def output_of(i):
            b, j, k = UNITS[i]
            return (4 * ORDER.index(b) + j, j, b) if b == SELECT or k == 4 * j + 3 else None

        @block.gpsimd
        def _(pool):
            for sg in (lo_pool, r_full, r_lo, built):
                sg.prime(pool)
            for t in wqk + wkw:
                nc.gpsimd.memset(t[:].bitcast(F32), 0.0).then_inc(s["set"], 1)
            nc.gpsimd.memset(mpart[:], -3.0e38).then_inc(s["set"], 1)
            pool.wait_ge(s["set"], 5)
            for part in range(4):
                build_weights(pool, -1, part)
            tasks = [t for t in ALL_SIDE if rope_number(t) is not None]
            for n, t in enumerate(tasks):
                rope_sum(pool, t, -1, 0)
                if n:
                    rope_rest(pool, tasks[n - 1], -1, 0)
                if 1 <= n <= NB:
                    nc.gpsimd.memset(vals[ORDER[n - 1]][:, :, 2 * DV:P].bitcast(F32), 1.0).then_inc(s["set"], 1)
            rope_rest(pool, tasks[-1], -1, 0)

            def head(h, par, prev, nxt):
                for i in range(NU + 3 if nxt else NU):
                    if nxt:
                        for t in SIDE.get(i - 1, ()):
                            rope_sum(pool, t, h, 1 - par)
                    if i in LO_POOL:
                        lower(pool, h, i, lo_pool)
                    if nxt:
                        for t in SIDE.get(i - 3, ()):
                            rope_rest(pool, t, h, 1 - par)
                    if nxt and 11 <= i < 15:
                        build_weights(pool, h, i - 11)
            heads(pool, head)

        def round_up(act, task, t, par):
            n = rope_number(task)
            if n is not None:
                r_full.wait(act, t, n)
                r_up.after(nc.scalar.copy(dst(task[0], par)[0][0:DQK, task[1] * CH:(task[1] + 1) * CH], full[:, n % 2, :]))

        @block.scalar
        def _(act):
            for sg in (p_full, p_up, r_up, s_read, lower_read):
                sg.prime(act)
            nc.scalar.copy(kw_hi[DQK:QA, :], g.onehot[DQK:QA, WINDOW:WINDOW + 1].to_broadcast([NB, T])).then_inc(s["ones"], 1)
            for t in ALL_SIDE:
                round_up(act, t, -1, 0)

            def read_sums(h, par, i):
                out = output_of(i)
                if out:
                    n, j, b = out
                    slot = (par + n // NJ) % 2
                    pv.wait(act, h, i)
                    done.wait(act, h, n // NJ - 2)
                    lower_read.after(nc.scalar.copy(raw_o[j * DV:(j + 1) * DV, slot, :], ps_o[n % 2][DV:2 * DV, :]))
                    s_read.after(nc.scalar.copy(sums[j * DV:(j + 1) * DV, slot, :], ps_o[n % 2][2 * DV:3 * DV, :]))

            def head(h, par, prev, nxt):
                for i in range(NU):
                    c, rows = width(i)
                    scores.wait(act, h, i)
                    lower_done(act, h, i - NPROB)
                    p_full.after(nc.scalar.activation(prob[0:rows, i % NPROB, c:CH], ps_s[i % 3][0:rows, c:CH], ACT.Exp, scale=SCALE))
                    pv.wait(act, h, i - SLOTS)
                    p_up.after(nc.scalar.activation(p_hi[0:rows, i % SLOTS, c:CH], ps_s[i % 3][0:rows, c:CH], ACT.Exp, scale=SCALE))
                    if nxt:
                        for t in SIDE.get(i - 2, ()):
                            round_up(act, t, h, 1 - par)
                    back = lagged(h, par, i, OUT_LAG, prev)
                    if back:
                        read_sums(*back)
            heads(act, head)
            for i in range(NU - OUT_LAG, NU):
                read_sums(H - 1, 1, i)

        def three(out, hi, lo, xhi, xlo, mid=None, rows=None):
            nc.tensor.matmul(out, hi, xhi, start=True, stop=False)
            if mid:
                mid()
            nc.tensor.matmul(out, hi[0:rows] if rows else hi, xlo, start=False, stop=False)
            return nc.tensor.matmul(out, lo, xhi[0:rows] if rows else xhi, start=False, stop=True)

        FIRST_MX = {}
        for t in MX:
            FIRST_MX.setdefault(t[1], t)

        def pe_task(pe, task, t, par, uses):
            if task[0] == "v":
                return
            if task[0] == "max":
                _, b, q, c = task
                n = MX[task]
                if task == FIRST_MX[b]:
                    if b == SELECT:
                        r_up.wait(pe, t, NJ - 1)
                        pe.wait_ge(s["ks"], 32 * (t + 2))
                if b == LATENT and q % 4 == 0 and c == 0:
                    k1.wait(pe, t, q // 4)
                if b == WINDOW and q % 4 == 0 and c == 0:
                    r_up.wait(pe, t, NJ + q // 4)
                mx_read.wait(pe, t, n - (4 if is_first(t) else 2))
                bank = mx_bank(t, task)
                if b == SELECT:
                    for r in range(8):
                        last = nc.tensor.matmul(bank[:, r * KEEP:(r + 1) * KEEP], q_hi[par][0:DQK, (8 * q + r) * P:(8 * q + r + 1) * P],
                                                ks_hi[par][0:DQK, 0:KEEP], start=True, stop=True)
                else:
                    w = min(CH, (q + 1) * P - c * CH)
                    diag = c == q // 4
                    last = nc.tensor.matmul(bank[:, 0:w], q_hi[par][0:DQK, q * P:(q + 1) * P], k_hi[b][par][0:DQK, c * CH:c * CH + w],
                                            start=True, stop=not diag)
                    if diag:
                        last = nc.tensor.matmul(bank[:, w - P:w], g.ident16[:], g.mask_qk[:], start=False, stop=True)
                mx.after(last)
                return
            if task == ("q", 0, 0):
                built.wait(pe, t, 0)
            n = uses.index(task)
            bank = pj_bank(t, task)
            if is_first(t):
                if n >= 2:
                    pj_wait(pe, pj_read, t, uses[n - 2])
            elif n:
                pj_wait(pe, pj_read, t, uses[n - 1])
            else:
                pj_wait(pe, pj_read, t - 1, PJ[-1])
            if task[0] == "q":
                _, j, rot = task
                c = slice(j * CH, (j + 1) * CH)
                last = three(bank[0:DQK, :], wq[0][:, rot, :], wq[1][:, rot, :], g.lat_hi[0:QL, c], g.lat_lo[0:QL, c])
            elif task[0] == "k1":
                c = slice(task[1] * CH, (task[1] + 1) * CH)
                last = three(bank[0:DQK, :], wk1[0][QL:P, :], wk1[1][QL:P, :], g.lat_hi[QL:P, c], g.lat_lo[QL:P, c])
            elif task[0] == "kw":
                _, j, rot = task
                for kc in range(KC):
                    for w in range(2):
                        last = nc.tensor.matmul(bank[0:DQK, :], wkw[w][:, kc, rot, :], g.uT[:, kc, j * CH:(j + 1) * CH],
                                                start=(kc == 0 and w == 0), stop=(kc == KC - 1 and w == 1))
            else:
                nmax.wait(pe, t, task[1])
                pe.sem_inc(s["pe_passed"], 1)
                rows = NT * (1 + task[1])
                last = nc.tensor.transpose(bank[0:rows, 0:P], nm[:, 0:rows], g.ident[:])
            pj[task in OWN].after(last)

        def pe_scores(pe, h, par, i):
            b, j, k = UNITS[i]
            if i == 0:
                r_lo.wait(pe, h - 1, 7)
                pe.wait_ge(s["rows_w"], 32 * (h + 1))
            if i == HU:
                k1.wait(pe, h, 3)
                pe.wait_ge(s["rows_l"], 16 * (h + 1))
            col, _ = width(i)
            d = col // P
            diag = b != SELECT and k >= 4 * j
            p_up.wait(pe, h, i - 3)
            qs, ks = slice(j * CH + col, (j + 1) * CH), slice(k * P, (k + 1) * P)
            bank = ps_s[i % 3]
            mid = (lambda: nc.tensor.matmul(bank[:, col:col + P], g.ident16[:], g.mask_kq[:], start=False, stop=False)) if diag else None
            aug = DQK + b + 1
            scores.after(three(bank[:, col:CH], k_hi[b][par][0:aug, ks], k_lo[b][par][:, ks], q_hi[par][0:aug, qs], q_lo[par][:, qs], mid, DQK))

        def pe_values(pe, h, par, i):
            b, j, k = UNITS[i]
            n = 4 * ORDER.index(b) + j
            if j == 0 and k == 0:
                v_split[b].wait(pe, h - 1 if b == WINDOW else h, 0)
            lower_done(pe, h, i)
            if k == 0:
                o_read.wait(pe, h, n - 2)
                s_read.wait(pe, h, n - 2)
            c, rows = width(i)
            w = vals[b][:, k if b != SELECT else 0, :]
            nc.tensor.matmul(ps_o[n % 2][:, c:CH], w, p_hi[0:rows, i % SLOTS, c:CH], start=(k == 0), stop=False)
            pv.after(nc.tensor.matmul(ps_o[n % 2][:, c:CH], w, p_lo[0:rows, i % LSLOTS, c:CH], start=False,
                                      stop=output_of(i) is not None))

        @block.tensor
        def _(pe):
            for sg in (scores, pv, *pj.values(), mx):
                sg.prime(pe)
            for t in ALL_SIDE:
                if t not in OWN:
                    pe_task(pe, t, -1, 0, PJ_NEXT)
            pe.wait_ge(s["set"], 8)
            pe.wait_ge(s["ones"], 1)

            def head(h, par, prev, nxt):
                for i in range(NU):
                    pe_scores(pe, h, par, i)
                    tasks = [t for t in side(i, nxt) if t[0] != "v"]
                    for n, t in enumerate(tasks or [None]):
                        if t:
                            pe_task(pe, t, h, par if t in OWN else 1 - par, PJ if nxt else PJ_OWN)
                        back = lagged(h, par, i, PV_LAG, prev)
                        if n == 0 and back:
                            pe_values(pe, *back)
            heads(pe, head)
            for i in range(NU - PV_LAG, NU):
                pe_values(pe, H - 1, 1, i)

        def dve_task(dve, task, t, par):
            if task[0] == "v":
                b = task[1]
                up, done = v_up[b], v_split[b]
                if b == SELECT:
                    src = g.vs[:, bass.ds(t, 1), :]
                    pv.wait(dve, t, -1)
                    dve.sem_inc(s["dve_passed"], 1)
                else:
                    src = v_raw
                    pv.wait(dve, t, -5 if b == LATENT else HU - 1) if not (isinstance(t, int) and t < 0) else None
                    dve.wait_ge(s["v_l" if b == LATENT else "v_w"], 16 * (t + 1 if b == LATENT else t + 2))
                up.after(nc.vector.tensor_copy(vals[b][:, :, 0:DV], src))
                up.wait(dve, t, 0)
                done.after(nc.vector.tensor_tensor(vals[b][:, :, DV:2 * DV], src, vals[b][:, :, 0:DV].bitcast(F32), ALU.subtract))
                return
            if task[0] == "max":
                _, b, q, c = task
                n = MX[task]
                mx.wait(dve, t, n)
                bank = mx_bank(t, task)
                if b == SELECT:
                    ins = nc.vector.tensor_reduce(nm[:, NT + 8 * q:NT + 8 * q + 8],
                                                  bank[:].rearrange("p (q k) -> p q k", k=KEEP), axis=AX.X, op=ALU.max, negate=True)
                else:
                    w = min(CH, (q + 1) * P - c * CH)
                    ins = nc.vector.tensor_reduce(mpart[:, q, c:c + 1], bank[:, 0:w], axis=AX.X, op=ALU.max)
                mx_read.after(ins)
                return
            if task[0] in ("q", "kw"):
                what, j, rot = task
                r = ROPED.index((what, j))
                c = slice(j * CH, (j + 1) * CH)
                tab = (g.cos, g.sin) if what == "q" else (g.cos_a, g.sin_a)
                if rot == 0:
                    r_full.wait(dve, t, r - 2)
                pj_wait(dve, pj, t, task)
                pj_read[task in OWN].after(nc.vector.tensor_tensor((t1, t2)[rot][:, r % 2, :], pj_bank(t, task)[0:DQK, :], tab[rot][:, c], ALU.mult))
                if rot:
                    pj_wait(dve, pj_read, t, task)
                    dve.sem_inc(roped.sem, 1)
            elif task[0] == "k1":
                c = slice(task[1] * CH, (task[1] + 1) * CH)
                pj_wait(dve, pj, t, task)
                k1c.after(nc.vector.tensor_copy(g.k1_hi[0:NOPE, c], pj_bank(t, task)[0:NOPE, :]))
                k1c.wait(dve, t, task[1])
                pj_read[task in OWN].after(nc.vector.tensor_tensor(g.k1_lo[0:NOPE, c], pj_bank(t, task)[0:NOPE, :], g.k1_hi[0:NOPE, c].bitcast(F32), ALU.subtract))
                pj_wait(dve, pj_read, t, task)
                dve.sem_inc(k1.sem, 1)
            else:
                last_mx = max(m for task_, m in MX.items() if task_[1] == (LATENT if task[1] == 0 else WINDOW))
                mx_read.wait(dve, t, last_mx)
                nmax.after(nc.vector.tensor_reduce(nm[:, 0:NT], mpart[:], axis=AX.X, op=ALU.max, negate=True))
                pj_wait(dve, pj, t, task)
                if task[1] == 0:
                    dve.wait_ge(s["rows_w"], 32 * (t + 1))
                elif not (isinstance(t, int) and t < 0):
                    dve.wait_ge(s["rows_l"], 16 * (t + 1))
                rows = NT * (1 + task[1])
                pj_read[task in OWN].after(nc.vector.tensor_copy(nm_t[0:rows, :], pj_bank(t, task)[0:rows, 0:P]))
                pj_wait(dve, pj_read, t, task)
                dve.sem_inc(nmax_t.sem, 1)

        def dve_output(dve, h, par, i):
            out = output_of(i)
            if out is None:
                return
            n, j, b = out
            br = n // NJ
            slot = (par + br) % 2
            bank = ps_o[n % 2]
            pv.wait(dve, h, i)
            lower_read.wait(dve, h, n)
            rows = raw_o[j * DV:(j + 1) * DV, slot, :]
            o_read.after(nc.vector.tensor_tensor(rows, bank[0:DV, :], rows, ALU.add))

        def dve_branch(dve, h, par, i, piece):
            out = output_of(i)
            if out is None or out[1] < NJ - 1:
                return
            n, j, b = out
            br = n // NJ
            slot = (par + br) % 2
            if piece < NJ:
                if piece == 0:
                    s_read.wait(dve, h, n)
                c = slice(piece * P, (piece + 1) * P)
                inv.after(nc.vector.reciprocal(sums[:, slot, c], sums[:, slot, c]))
                return
            inv.wait(dve, h, NJ * br + NJ - 1)
            o_read.wait(dve, h, n)
            if br == 0:
                dve.wait_ge(s["store"], 16 * (h + 1))
            norm.after(nc.vector.scalar_tensor_tensor(ot[:] if br == 0 else raw_o[:, slot, :], raw_o[:, slot, :], g.gates[:, GATE[b]:GATE[b] + 1],
                                                      sums[:, slot, :], ALU.mult, ALU.mult))
            norm.wait(dve, h, br)
            if br == 0:
                dve.sem_inc(done.sem, 1)

        def dve_sum(dve, h, par, i):
            out = output_of(i)
            if out and out[1] == NJ - 1 and out[0] >= NJ:
                br = out[0] // NJ
                slot = (par + br) % 2
                norm.wait(dve, h, br)
                done.wait(dve, h, br - 1)
                done.after(nc.vector.tensor_tensor(ot[:], ot[:], raw_o[:, slot, :], ALU.add))

        def dve_outputs(dve, back):
            if back(OUT_LAG):
                dve_output(dve, *back(OUT_LAG))
            for piece in range(NJ + 1):
                if back(OUT_LAG + 1 + piece):
                    dve_branch(dve, *back(OUT_LAG + 1 + piece), piece)
            if back(OUT_LAG + NJ + 2):
                dve_sum(dve, *back(OUT_LAG + NJ + 2))

        @block.vector
        def _(dve):
            for sg in (lo_dve, o_read, inv, norm, done, k1c, k1, *pj_read.values(), mx_read, roped, nmax, nmax_t, *v_split.values(), *v_up.values()):
                sg.prime(dve)
            dve.wait_ge(s["set"], 5)
            for t in ALL_SIDE:
                if t not in OWN:
                    dve_task(dve, t, -1, 0)

            def head(h, par, prev, nxt):
                for i in range(NU):
                    for t in side(i, nxt):
                        dve_task(dve, t, h, par if t in OWN else 1 - par)
                    if i - 1 in LO_DVE:
                        lower(dve, h, i - 1, lo_dve)
                    dve_outputs(dve, lambda lag: lagged(h, par, i, lag, prev))
                if NU - 1 in LO_DVE:
                    lower(dve, h, NU - 1, lo_dve)
            heads(dve, head)
            for i in range(NU, NU + OUT_LAG + NJ + 2):
                dve_outputs(dve, lambda lag: (H - 1, 1, i - lag) if i - lag < NU else None)


def mix(nc, g, a):
    with ExitStack() as ctx:
        tile = lambda n, s, d=F32: ctx.enter_context(nc.sbuf_tensor(n, s, d))
        KB = H * DV // P
        o = tile("o_in", [P, 2, KB, CH])
        h0 = tile("h0_again", [P, NT, C])
        wp = tile("wp", [P, KB, C])
        wp_hi, wp_lo = tile("wp_hi", [P, KB, C], F32R), tile("wp_lo", [P, KB, C], F32R)
        rw = tile("rw", [P, KC, E])
        rw_hi, rw_lo = tile("rw_hi", [P, KC, E], F32R), tile("rw_lo", [P, KC, E], F32R)
        o_hi, o_lo = tile("o_hi", [P, 2, KB, CH], F32R), tile("o_lo", [P, 2, KB, CH], F32R)
        stats = tile("bn", [P, NT, 6])
        mv = tile("bn_mv", [P, NT, 2])
        rstd = tile("rstd2", [P, NT])
        x2 = tile("x2", [P, NT, C])
        logit = tile("logit", [P, NT, E])
        sc = {n: tile("sm_" + n, [P, NT, E]) for n in ("hot1", "hot2", "rest", "dist", "fac", "keep", "ex", "tie", "order")}
        top = {n: tile("st_" + n, [P, NT]) for n in ("m1", "m2", "t", "sum", "w1", "w2")}
        bank = [ctx.enter_context(nc.psum_tensor(f"m_ps{i}", [P, CH], F32)) for i in range(8)]
        s = {k: ctx.enter_context(nc.semaphore("m_" + k)) for k in
             ("o0", "o1", "w", "rw", "h0", "whi", "wlo", "ohi", "olo", "y", "h1", "v", "var", "rt", "x2", "xt", "xhi", "xlo", "lg", "ord", "ex", "exd")}
        block = ctx.enter_context(nc.Block())

        @block.sync
        def _(sp):
            sp.dma_start(wp[:], a["w_proj"].rearrange("(k p) n -> p k n", p=P)).then_inc(s["w"], 16)
            heads = g.o_dram.rearrange("(k f) (j r) q -> f j r k q", f=P // DV, j=NJ)
            for n in range(NJ):
                if n >= 2:
                    sp.wait_ge(s["olo"], n - 1)
                for f in range(P // DV):
                    sp.dma_start(o[f * DV:(f + 1) * DV, n % 2], heads[f, n]).then_inc(s["o%d" % (n % 2)], 16)
                if n == 0:
                    sp.dma_start(h0[:].rearrange("p t c -> p (t c)"), g.h0_dram).then_inc(s["h0"], 16)
            load_expert(g, a, sp, 0)

        @block.gpsimd
        def _(pool):
            for k in range(KC):
                pool.dma_start(rw[:, k, :], a["router_w"][:, k * P:(k + 1) * P].rearrange("e p -> p e")).then_inc(s["rw"], 16)
            nc.gpsimd.iota(sc["order"][:], pattern=[[0, NT], [-1, E]], base=E, channel_multiplier=0,
                           allow_small_or_imprecise_dtypes=True).then_inc(s["ord"], 1)
            pool.wait_ge(s["ord"], 1)

        @block.tensor
        def _(pe):
            def out_product(t):
                n, m = divmod(t, CH // P)
                c = slice(m * P, (m + 1) * P)
                pe.wait_ge(s["olo"], n + 1)
                if t >= 2:
                    pe.wait_ge(s["h1"], t - 1)
                for k in range(KB):
                    for i, (l, w) in enumerate(((o_hi, wp_hi), (o_hi, wp_lo), (o_lo, wp_hi))):
                        last = nc.tensor.matmul(bank[2 + t % 2][:, 0:C], l[:, n % 2, k, c], w[:, k, :],
                                                start=(k == 0 and i == 0), stop=(k == KB - 1 and i == 2))
                last.then_inc(s["y"], 1)
            pe.wait_ge(s["whi"], 2)
            pe.wait_ge(s["wlo"], 2)
            def x_transposes(j):
                pe.wait_ge(s["x2"], 4 * j + 4)
                for kc in range(KC):
                    n = KC * j + kc
                    if n >= 4:
                        pe.wait_ge(s["xlo"], n - 3)
                    for q in range(4):
                        last = nc.tensor.transpose(bank[4 + n % 4][:, q * P:(q + 1) * P], x2[:, 4 * j + q, kc * P:(kc + 1) * P], g.ident[:])
                    last.then_inc(s["xt"], 1)

            def logits(j):
                pe.wait_ge(s["xlo"], KC * (j + 1))
                for t in range(4 * j, 4 * j + 4):
                    for kc in range(KC):
                        for n, (l, w) in enumerate(((g.x_hi, rw_hi), (g.x_hi, rw_lo), (g.x_lo, rw_hi))):
                            last = nc.tensor.matmul(bank[0][:, t * E:(t + 1) * E], l[:, kc, t * P:(t + 1) * P], w[:, kc, :],
                                                    start=(kc == 0 and n == 0), stop=(kc == KC - 1 and n == 2))
                last.then_inc(s["lg"], 1)

            for n in range(NJ):
                for t in range(4 * n, 4 * n + 4):
                    out_product(t)
                if n >= 2:
                    x_transposes(n - 2)
            for j in (2, 3):
                logits(j - 2)
                x_transposes(j)
            for j in (2, 3):
                logits(j)

        @block.scalar
        def _(act):
            act.wait_ge(s["w"], 16)
            act.wait_ge(s["rw"], 32)
            nc.scalar.copy(wp_hi[:], wp[:]).then_inc(s["whi"], 1)
            nc.scalar.copy(rw_hi[:], rw[:]).then_inc(s["whi"], 1)
            def upper_outputs(n):
                act.wait_ge(s["o%d" % (n % 2)], 64 * (n // 2 + 1))
                if n >= 2:
                    act.wait_ge(s["y"], 4 * (n - 1))
                nc.scalar.copy(o_hi[:, n % 2], o[:, n % 2]).then_inc(s["ohi"], 1)

            def deviation(j):
                act.wait_ge(s["var"], j + 1)
                nc.scalar.activation(rstd[:, 4 * j:4 * j + 4], rstd[:, 4 * j:4 * j + 4], ACT.Sqrt).then_inc(s["rt"], 1)

            def upper_x(j):
                for kc in range(KC):
                    n = KC * j + kc
                    act.wait_ge(s["xt"], n + 1)
                    nc.scalar.copy(g.x_hi[:, kc, j * CH:(j + 1) * CH], bank[4 + n % 4][:]).then_inc(s["xhi"], 1)
            for n in range(3):
                upper_outputs(n)
            deviation(0)
            upper_outputs(3)
            deviation(1)
            upper_x(0)
            deviation(2)
            upper_x(1)
            deviation(3)
            upper_x(2)
            upper_x(3)
            for n in range(2):
                act.wait_ge(s["ex"], n + 1)
                nc.scalar.activation(sc["ex"][:], sc["dist"][:], ACT.Exp, scale=-1.0).then_inc(s["exd"], 1)

        @block.vector
        def _(dve):
            v = Count(dve, s["v"])
            dve.wait_ge(s["whi"], 2)
            nc.vector.tensor_tensor(wp_lo[:], wp[:], wp_hi[:].bitcast(F32), ALU.subtract).then_inc(s["wlo"], 1)
            nc.vector.tensor_tensor(rw_lo[:], rw[:], rw_hi[:].bitcast(F32), ALU.subtract).then_inc(s["wlo"], 1)
            dve.wait_ge(s["h0"], 16)

            def residual(t):
                dve.wait_ge(s["y"], t + 1)
                nc.vector.tensor_tensor(g.h1[:, t, :], bank[2 + t % 2][:, 0:C], h0[:, t, :], ALU.add).then_inc(s["h1"], 1)
            def lower_outputs(n):
                dve.wait_ge(s["ohi"], n + 1)
                if n >= 2:
                    dve.wait_ge(s["y"], 4 * (n - 1))
                nc.vector.tensor_tensor(o_lo[:, n % 2], o[:, n % 2], o_hi[:, n % 2].bitcast(F32), ALU.subtract).then_inc(s["olo"], 1)

            def variances(j):
                c = slice(4 * j, 4 * j + 4)
                for t in range(4 * j, 4 * j + 4):
                    residual(t)
                for t in range(4 * j, 4 * j + 4):
                    dve.wait_ge(s["h1"], t + 1)
                    v.add(nc.vector.bn_stats(stats[:, t, :], g.h1[:, t, :]))
                v.wait()
                for t in range(4 * j, 4 * j + 4):
                    v.add(nc.vector.bn_aggr(mv[:, t, :], stats[:, t, :]))
                v.wait()
                nc.vector.tensor_scalar(rstd[:, c], mv[:, c, 1], 1e-5, None, ALU.add).then_inc(s["var"], 1)

            def layernorm(j):
                c = slice(4 * j, 4 * j + 4)
                dve.wait_ge(s["rt"], j + 1)
                v.add(nc.vector.reciprocal(rstd[:, c], rstd[:, c]))
                v.wait()
                for t in range(4 * j, 4 * j + 4):
                    nc.vector.tensor_scalar(x2[:, t, :], g.h1[:, t, :], mv[:, t, 0:1], rstd[:, t:t + 1], ALU.subtract, ALU.mult).then_inc(s["x2"], 1)

            def lower_x(j):
                c = slice(j * CH, (j + 1) * CH)
                for kc in range(KC):
                    n = KC * j + kc
                    dve.wait_ge(s["xhi"], n + 1)
                    nc.vector.tensor_tensor(g.x_lo[:, kc, c], bank[4 + n % 4][:], g.x_hi[:, kc, c].bitcast(F32), ALU.subtract).then_inc(s["xlo"], 1)
            lower_outputs(0)
            lower_outputs(1)
            variances(0)
            lower_outputs(2)
            layernorm(0)
            variances(1)
            lower_outputs(3)
            layernorm(1)
            variances(2)
            lower_x(0)
            layernorm(2)
            variances(3)
            lower_x(1)
            layernorm(3)
            lower_x(2)
            lower_x(3)
            dve.wait_ge(s["lg"], NJ)
            dve.wait_ge(s["ord"], 1)
            v.add(nc.vector.tensor_copy(logit[:].rearrange("p t e -> p (t e)"), bank[0][:, 0:NT * E]))
            v.wait()

            def step(ins):
                v.add(ins)
                v.wait()

            wide = lambda t: t[:].unsqueeze(2).to_broadcast([P, NT, E])

            def gate(scores, m, hot, weight, n, banned):
                step(nc.vector.tensor_reduce(m[:], scores[:], axis=AX.X, op=ALU.max))
                step(nc.vector.tensor_tensor(sc["tie"][:], scores[:], wide(m), ALU.is_equal))
                step(nc.vector.tensor_tensor(sc["tie"][:], sc["tie"][:], sc["order"][:], ALU.mult))
                step(nc.vector.tensor_reduce(top["t"][:], sc["tie"][:], axis=AX.X, op=ALU.max))
                step(nc.vector.tensor_tensor(hot[:], sc["tie"][:], wide(top["t"]), ALU.is_equal))
                step(nc.vector.tensor_scalar(sc["fac"][:], logit[:], -1.0, None, ALU.mult))
                step(nc.vector.tensor_tensor(sc["fac"][:], sc["fac"][:], logit[:], ALU.max))
                step(nc.vector.tensor_tensor(sc["fac"][:], sc["fac"][:], wide(m), ALU.max))
                v.add(nc.vector.tensor_tensor(sc["dist"][:], wide(m), logit[:], ALU.subtract))
                v.wait()
                step(nc.vector.tensor_scalar(sc["fac"][:], sc["fac"][:], 2.0 * JITTER, None, ALU.mult))
                step(nc.vector.tensor_tensor(sc["keep"][:], sc["dist"][:], sc["fac"][:], ALU.is_le))
                if banned is not None:
                    step(nc.vector.tensor_tensor(sc["tie"][:], sc["keep"][:], banned[:], ALU.mult))
                    step(nc.vector.tensor_tensor(sc["keep"][:], sc["keep"][:], sc["tie"][:], ALU.subtract))
                    step(nc.vector.tensor_scalar(sc["dist"][:], sc["dist"][:], 0.0, None, ALU.max))
                dve.sem_inc(s["ex"], 1)
                dve.wait_ge(s["exd"], n + 1)
                step(nc.vector.tensor_tensor(sc["keep"][:], sc["keep"][:], sc["ex"][:], ALU.mult))
                step(nc.vector.tensor_reduce(top["sum"][:], sc["keep"][:], axis=AX.X, op=ALU.add))
                step(nc.vector.reciprocal(weight[:], top["sum"][:]))

            gate(logit, top["m1"], sc["hot1"], top["w1"], 0, None)
            step(nc.vector.tensor_scalar(sc["rest"][:], sc["hot1"][:], -3.0e38, None, ALU.mult))
            step(nc.vector.tensor_tensor(sc["rest"][:], sc["rest"][:], logit[:], ALU.add))
            gate(sc["rest"], top["m2"], sc["hot2"], top["w2"], 1, sc["hot1"])
            step(nc.vector.tensor_tensor(sc["hot1"][:], sc["hot1"][:], wide(top["w1"]), ALU.mult))
            step(nc.vector.tensor_tensor(sc["hot2"][:], sc["hot2"][:], wide(top["w2"]), ALU.mult))
            step(nc.vector.tensor_tensor(g.dense[:], sc["hot1"][:], sc["hot2"][:], ALU.add))


def load_expert(g, a, sp, e):
    for k, w, n in (("g", a["w_gate_e"], FB), ("u", a["w_up"], FB), ("d", a["w_down"], KC)):
        sp.dma_start(g.raw[k][:], w[bass.ds(e, 1)].rearrange("o r c -> (o r) c").rearrange("(b p) c -> p b c", p=P)).then_inc(g.raw_in, 16)


def experts(nc, g, a, out):
    with ExitStack() as ctx:
        tile = lambda n, s, d=F32: ctx.enter_context(nc.sbuf_tensor(n, s, d))
        NG = NJ * FB
        raw = g.raw
        wt = [[tile(f"wt{i}_{n}", [P, 6, CH], F32R) for n in ("hi", "lo")] for i in range(2)]
        sg = tile("silu", [P, 2, CH])
        hm = tile("hm", [P, 2, CH])
        h_hi, h_lo = tile("h_hi", [P, 2, FB, CH], F32R), tile("h_lo", [P, 2, FB, CH], F32R)
        ps_g = [ctx.enter_context(nc.psum_tensor(f"e_g{i}", [P, CH], F32)) for i in range(2)]
        ps_u = [ctx.enter_context(nc.psum_tensor(f"e_u{i}", [P, CH], F32)) for i in range(2)]
        ps_y = [ctx.enter_context(nc.psum_tensor(f"e_y{i}", [P, CH], F32)) for i in range(2)]
        ps_t = [ctx.enter_context(nc.psum_tensor(f"e_t{i}", [P, CH], F32)) for i in range(2)]
        s = {k: ctx.enter_context(nc.semaphore("e_" + k)) for k in
             ("tr", "whi", "wlo", "g", "u", "silu", "hm", "hi", "lo", "y", "acc", "out")}
        block = ctx.enter_context(nc.Block())
        LOOP = E - 2

        @block.sync
        def _(sp):
            sp.wait_ge(s["tr"], 6)
            load_expert(g, a, sp, 1)
            with sp.Fori(0, LOOP) as e:
                sp.wait_ge(s["tr"], 6 * e + 12)
                load_expert(g, a, sp, e + 2)
            for n in range(NT):
                sp.wait_ge(s["acc"], 2 + NT * (E - 1) + n + 1)
                sp.dma_start(out[0, n * P:(n + 1) * P, :], g.h1[:, n, :]).then_inc(s["out"], 16)
            sp.wait_ge(s["out"], 16 * NT)

        def transposes(pe, e, par):
            pe.wait_ge(g.raw_in, 48 * (e + 1))
            for b in range(6):
                pe.wait_ge(s["wlo"], 6 * e + b + 1)
                for q in range(4):
                    if b < 4:
                        src = raw["gu"[b // 2]][:, q, (b % 2) * P:(b % 2 + 1) * P]
                    else:
                        f = 2 * (b - 4) + q // 2
                        src = raw["d"][:, q % 2, f * P:(f + 1) * P]
                    last = nc.tensor.transpose(ps_t[b % 2][:, q * P:(q + 1) * P], src, g.ident[:])
                last.then_inc(s["tr"], 1)

        def gate_up(pe, e, par, n):
            hi, lo = wt[par]
            c = slice(n * CH, (n + 1) * CH)
            if n == 0:
                pe.wait_ge(s["wlo"], 2 + 6 * (e + 1))
            for f in range(FB):
                i = n * FB + f
                cols = slice(f * P, (f + 1) * P)
                for ps, m, sem, free in ((ps_g, 0, "g", "silu"), (ps_u, 2, "u", "hm")):
                    pe.wait_ge(s[free], NG * e + i + 1)
                    for kc in range(KC):
                        for k, (w, x) in enumerate(((hi, g.x_hi), (hi, g.x_lo), (lo, g.x_hi))):
                            last = nc.tensor.matmul(ps[i % 2][:], w[:, m + kc, cols], x[:, kc, c],
                                                    start=(kc == 0 and k == 0), stop=(kc == KC - 1 and k == 2))
                    last.then_inc(s[sem], 1)

        def down(pe, e, par, n):
            hi, lo = wt[par]
            pe.wait_ge(s["lo"], 2 + NG * e + FB * (n + 1))
            for q in range(4):
                i = 4 * n + q
                pe.wait_ge(s["acc"], NT * e + i + 1)
                for f in range(FB):
                    wcols = slice((f % 2) * C, (f % 2 + 1) * C)
                    for k, (h, w) in enumerate(((h_hi, hi), (h_hi, lo), (h_lo, hi))):
                        last = nc.tensor.matmul(ps_y[i % 2][:, 0:C], h[:, n % 2, f, q * P:(q + 1) * P], w[:, 4 + f // 2, wcols],
                                                start=(f == 0 and k == 0), stop=(f == FB - 1 and k == 2))
                last.then_inc(s["y"], 1)

        @block.tensor
        def _(pe):
            def expert(e, par, prep):
                for n in range(NJ):
                    gate_up(pe, e, par, n)
                    if n:
                        down(pe, e, par, n - 1)
                if prep:
                    transposes(pe, e + 1, 1 - par)
                down(pe, e, par, NJ - 1)
            transposes(pe, 0, 0)
            with pe.Fori(0, LOOP // 2) as pair:
                expert(2 * pair, 0, True)
                expert(2 * pair + 1, 1, True)
            expert(E - 2, 0, True)
            expert(E - 1, 1, False)

        @block.scalar
        def _(act):
            act.sem_inc(s["silu"], 2)

            def upper_weights(e, par):
                for b in range(6):
                    act.wait_ge(s["tr"], 6 * e + b + 1)
                    nc.scalar.copy(wt[par][0][:, b, :], ps_t[b % 2][:]).then_inc(s["whi"], 1)

            def upper(e, i):
                n, f = divmod(i, FB)
                act.wait_ge(s["hm"], 2 + NG * e + i + 1)
                act.wait_ge(s["y"], NT * e + 4 * n + 4)
                nc.scalar.copy(h_hi[:, n % 2, f, :], hm[:, i % 2, :]).then_inc(s["hi"], 1)

            def expert(e, par, prep):
                for i in range(NG):
                    act.wait_ge(s["g"], NG * e + i + 1)
                    act.wait_ge(s["hm"], NG * e + i + 1)
                    nc.scalar.activation(sg[:, i % 2, :], ps_g[i % 2][:], ACT.Silu).then_inc(s["silu"], 1)
                    if i:
                        upper(e, i - 1)
                upper(e, NG - 1)
                if prep:
                    upper_weights(e + 1, 1 - par)
            upper_weights(0, 0)
            with act.Fori(0, LOOP // 2) as pair:
                expert(2 * pair, 0, True)
                expert(2 * pair + 1, 1, True)
            expert(E - 2, 0, True)
            expert(E - 1, 1, False)

        @block.gpsimd
        def _(pool):
            pool.sem_inc(s["lo"], 2)

            def expert(e):
                for i in range(NG):
                    n, f = divmod(i, FB)
                    pool.wait_ge(s["hi"], NG * e + i + 1)
                    nc.gpsimd.tensor_tensor(h_lo[:, n % 2, f, :], hm[:, i % 2, :], h_hi[:, n % 2, f, :].bitcast(F32), ALU.subtract).then_inc(s["lo"], 1)
            with pool.Fori(0, E) as e:
                expert(e)

        @block.vector
        def _(dve):
            dve.sem_inc(s["wlo"], 2)
            dve.sem_inc(s["hm"], 2)
            dve.sem_inc(s["acc"], 2)
            dve.sem_inc(s["y"], 8)

            def lower_weights(e, par):
                for b in range(6):
                    dve.wait_ge(s["whi"], 6 * e + b + 1)
                    nc.vector.tensor_tensor(wt[par][1][:, b, :], ps_t[b % 2][:], wt[par][0][:, b, :].bitcast(F32), ALU.subtract).then_inc(s["wlo"], 1)

            def accumulate(e, n):
                for q in range(4):
                    i = 4 * n + q
                    dve.wait_ge(s["y"], 8 + NT * e + i + 1)
                    nc.vector.scalar_tensor_tensor(g.h1[:, i, :], ps_y[i % 2][:, 0:C], g.dense[:, i, bass.ds(e, 1)], g.h1[:, i, :],
                                                   ALU.mult, ALU.add).then_inc(s["acc"], 1)

            def expert(e, par, prep):
                for n in range(NJ):
                    for f in range(FB):
                        i = n * FB + f
                        dve.wait_ge(s["silu"], 2 + NG * e + i + 1)
                        dve.wait_ge(s["u"], NG * e + i + 1)
                        dve.wait_ge(s["lo"], NG * e + i + 1)
                        nc.vector.tensor_tensor(hm[:, i % 2, :], sg[:, i % 2, :], ps_u[i % 2][:], ALU.mult).then_inc(s["hm"], 1)
                    if n:
                        accumulate(e, n - 1)
                if prep:
                    lower_weights(e + 1, 1 - par)
                accumulate(e, NJ - 1)
            lower_weights(0, 0)
            with dve.Fori(0, LOOP // 2) as pair:
                expert(2 * pair, 0, True)
                expert(2 * pair + 1, 1, True)
            expert(E - 2, 0, True)
            expert(E - 1, 1, False)


class Tiles:
    pass


def layer(nc, a, out):
    g = Tiles()
    g.h0_dram = nc.dram_tensor("h0_scratch", [P, NT * C], F32).ap()
    g.row_dram = nc.dram_tensor("row_scratch", [2, T], F32).ap()
    g.v_dram = nc.dram_tensor("v_scratch", [2, H, P, NT * DV], F32).ap()
    g.ks_dram = nc.dram_tensor("ks_scratch", [H, QA + DQK, P], F32).ap()
    g.o_dram = nc.dram_tensor("o_scratch", [H, P, CH], F32).ap()
    with ExitStack() as ctx:
        tile = lambda n, s, d=F32: ctx.enter_context(nc.sbuf_tensor(n, s, d))
        g.ident, g.ones = tile("ident", [P, P]), tile("ones", [P, P])
        g.ident16, g.mask_qk, g.mask_kq = tile("ident16", [P, P], BF16), tile("mask_qk", [P, P], BF16), tile("mask_kq", [P, P], BF16)
        g.inv, g.rstd, g.imp, g.gates = tile("inv", [P, 1]), tile("rstd", [P, NT]), tile("imp", [P, NT]), tile("gates", [P, 3])
        g.ranks = tile("ranks", [P, 2, NT])
        g.onehot = tile("onehot", [QA, NB])
        g.vs = tile("v_sel", [KEEP, H, DV])
        early = tile("early", [P, NT * (C + NS)])
        g.early = early
        g.U = early[:, 0:NT * C].rearrange("p (t c) -> p t c", c=C)
        g.sm = early[:, NT * C:NT * (C + NS)].rearrange("p (t n) -> p t n", n=NS)
        embed(nc, g, a["x"], a["tok_weight"])
        with ExitStack() as mid:
            tile = lambda n, s, d=F32: mid.enter_context(nc.sbuf_tensor(n, s, d))
            g.uT = tile("uT", [P, KC, T], F32R)
            g.lat_hi, g.lat_lo = tile("lat_hi", [P, T], F32R), tile("lat_lo", [P, T], F32R)
            g.cos, g.sin, g.cos_a, g.sin_a = (tile(n, [DQK, T]) for n in ("cos", "sin", "cos_a", "sin_a"))
            g.k1_hi, g.k1_lo = tile("k1_hi", [QA, T], F32R), tile("k1_lo", [DQK, T], F32R)
            project(nc, g, a)
            select(nc, g, a)
            attend(nc, g, a)
        g.h1 = ctx.enter_context(nc.sbuf_tensor("h1", [P, NT, C], F32))
        g.x_hi = ctx.enter_context(nc.sbuf_tensor("x2T_hi", [P, KC, T], F32R))
        g.x_lo = ctx.enter_context(nc.sbuf_tensor("x2T_lo", [P, KC, T], F32R))
        g.dense = ctx.enter_context(nc.sbuf_tensor("dense_w", [P, NT, E], F32))
        g.raw = {"g": ctx.enter_context(nc.sbuf_tensor("raw_g", [P, FB, C], F32)), "u": ctx.enter_context(nc.sbuf_tensor("raw_u", [P, FB, C], F32)),
                 "d": ctx.enter_context(nc.sbuf_tensor("raw_d", [P, KC, F], F32))}
        g.raw_in = ctx.enter_context(nc.semaphore("e_raw"))
        mix(nc, g, a)
        experts(nc, g, a, out)


_NAMES = {
    "x": "x", "L0_tok_weight": "tok_weight", "L0_attn_w_cq": "w_cq", "L0_attn_g_qnorm": "g_qnorm", "L0_attn_w_dq_nope": "w_dq_nope",
    "L0_attn_w_dq_rope": "w_dq_rope", "L0_attn_w_ckv": "w_ckv", "L0_attn_g_kvnorm": "g_kvnorm", "L0_attn_w_dk_nope": "w_dk_nope",
    "L0_attn_w_dv": "w_dv", "L0_attn_w_krope": "w_krope", "L0_attn_w_imp": "w_imp", "L0_attn_w_selk": "w_selk", "L0_attn_w_selv": "w_selv",
    "L0_attn_w_wink": "w_wink", "L0_attn_w_winv": "w_winv", "L0_attn_w_gate": "w_gate", "L0_attn_w_proj": "w_proj",
    "L0_ffn_router_w": "router_w", "L0_ffn_w_gate": "w_gate_e", "L0_ffn_w_up": "w_up", "L0_ffn_w_down": "w_down",
}
_OUTS = [((1, T, C), "float32")]


def rope_tables():
    import numpy as np
    f = (np.float32(1.0) / np.power(np.float32(10000.0), np.arange(0, ROPE, 2, dtype=np.float32) / np.float32(ROPE))).astype(np.float32)
    angle = np.outer(np.arange(T, dtype=np.float32), f).astype(np.float32)
    c, s = np.cos(angle), np.sin(angle)
    return {"cos": np.ascontiguousarray(c.T), "sin": np.ascontiguousarray(s.T), "cos_tok": c[:KEEP].copy(), "sin_tok": s[:KEEP].copy()}


def kernel(**inputs):
    import numpy as _np
    import concourse.bacc as _bacc
    from concourse import mybir as _mybir
    from concourse.bass_utils import run_bass_kernel_spmd as _run

    nc = _bacc.Bacc("TRN2", target_bir_lowering=False, num_devices=1)
    arrays, args = {}, {}
    given = {_NAMES[n]: inputs[n] for n in _NAMES}
    for name, value in {**given, **rope_tables()}.items():
        v = _np.ascontiguousarray(value)
        arrays[f"in_{name}_dram"] = v
        args[name] = nc.dram_tensor(f"in_{name}_dram", v.shape, _mybir.dt.from_np(v.dtype), kind="ExternalInput").ap()
    outs = [nc.dram_tensor(f"out_{i}_dram", shape, _mybir.dt.from_np(_np.dtype(dtype)), kind="ExternalOutput").ap()
            for i, (shape, dtype) in enumerate(_OUTS)]
    with nc.allow_non_contiguous_dma(reason="small index, router and row loads"):
        layer(nc, args, outs[0])
    r = _run(nc, [arrays], core_ids=[0])
    return r.results[0]["out_0_dram"]
```
